# Optimizing a Trainium2 kernel written in Bass

```python
import numpy as np
import jax
import jax.numpy as jnp

def _softmax(x, axis=-1):
    return jax.nn.softmax(x, axis=axis)

def _gelu(x):
    return jax.nn.gelu(x, approximate=True)

def _silu(x):
    return jax.nn.silu(x)

def _sigmoid(x):
    return jax.nn.sigmoid(x)

def _layernorm(x, axis=-1, eps=1e-05):
    m = jnp.mean(x, axis=axis, keepdims=True)
    v = jnp.var(x, axis=axis, keepdims=True)
    return (x - m) / jnp.sqrt(v + eps)

def _scatter_add(tgt, idx, src, axis=0):
    return tgt.at[idx].add(src)

def _segment_sum(src, seg, n):
    return jax.ops.segment_sum(src, seg, n)
kernel_name = 'mk_gnn_ffn_d2_gnn_r16_655976'

def setup_inputs(seed: int=0):
    np.random.seed(seed)
    _w = jnp.asarray

    def _rec_inputs():
        import jax
        import jax.numpy as jnp
        _gk = jax.random.key(seed)
        x = -0.0003713 + 1 * jax.random.normal(jax.random.fold_in(_gk, 1), (3125, 256), jnp.float32)
        _s = jax.random.randint(jax.random.fold_in(_gk, 2), (25000,), 0, 3125, jnp.int32)
        _d = jax.random.randint(jax.random.fold_in(_gk, 3), (25000,), 0, 3125, jnp.int32)
        _loop = jnp.arange(3125, dtype=jnp.int32)
        src = jnp.concatenate([_s, _d, _loop])
        dst = jnp.concatenate([_d, _s, _loop])
        _o = jnp.argsort(dst, stable=True)
        src = src[_o]
        dst = dst[_o]
        edge_type_4 = jax.random.randint(jax.random.fold_in(_gk, 13), (53125,), 0, 4, jnp.int32)
        return (x, src, dst, edge_type_4)
    x, src, dst, edge_type_4 = _rec_inputs()

    def _L0_gnn_setup():
        import jax, jax.numpy as jnp
        import numpy as np
        N = 3125
        E = 50000
        IN_F = 256
        OUT_F = 64
        NHEAD = 4
        ALPHA = 0.2

        def _gat_forward(x, W, a_l, a_r, edge):
            n = x.shape[0]
            row, col = (edge[0], edge[1])
            h = (x @ W).reshape(n, NHEAD, OUT_F)
            hl = jnp.sum(a_l * h, axis=-1)
            hr = jnp.sum(a_r * h, axis=-1)
            e = jax.nn.leaky_relu(hl[row] + hr[col], negative_slope=ALPHA)
            e_max = jax.ops.segment_max(e, row, num_segments=n)
            e_max = jnp.where(jnp.isfinite(e_max), e_max, 0.0)
            ee = jnp.exp(e - e_max[row])
            denom = jax.ops.segment_sum(ee, row, num_segments=n)
            att = ee / denom[row]
            msg = att[:, :, None] * h[col]
            out_h = jax.ops.segment_sum(msg, row, num_segments=n)
            return out_h.reshape(n, NHEAD * OUT_F)
        key = jax.random.key(seed)
        k1, k2, k3, k4, k5 = jax.random.split(key, 5)
        x = jax.random.normal(k1, (N, IN_F), dtype=jnp.float32)
        edge = jax.random.randint(k2, (2, E), 0, N, dtype=jnp.int32)
        stdv_W = float(np.sqrt(6.0 / (IN_F + OUT_F * NHEAD)))
        W = jax.random.uniform(k3, (IN_F, OUT_F * NHEAD), jnp.float32, -stdv_W, stdv_W)
        stdv_a = float(np.sqrt(6.0 / (NHEAD + OUT_F)))
        a_l = jax.random.uniform(k4, (1, NHEAD, OUT_F), jnp.float32, -stdv_a, stdv_a)
        a_r = jax.random.uniform(k5, (1, NHEAD, OUT_F), jnp.float32, -stdv_a, stdv_a)
        return {'x': x, 'edge': edge, 'W': W, 'a_l': a_l, 'a_r': a_r}
    _L0_gnn_all = _L0_gnn_setup()
    _L0_gnn_in = {k: v for k, v in _L0_gnn_all.items() if k in ('W', 'a_l', 'a_r')}
    del _L0_gnn_all

    def _L0_ffn_setup():
        import jax, jax.numpy as jnp
        import numpy as np
        B, S, D = (8, 256, 256)
        H = 4 * D
        CAPACITY = 0.5
        key = jax.random.key(seed)
        ks = jax.random.split(key, 6)
        x = jax.random.normal(ks[0], (B, S, D), dtype=jnp.float32)
        attention_mask = jnp.zeros((B, 1, 1, S), dtype=jnp.float32)
        wr = jax.random.normal(ks[1], (D, 1), dtype=jnp.float32) * 0.02
        br = jnp.zeros((1,), dtype=jnp.float32)
        w1 = jax.random.normal(ks[2], (D, H), dtype=jnp.float32) * 0.02
        b1 = jnp.zeros((H,), dtype=jnp.float32)
        w2 = jax.random.normal(ks[3], (H, D), dtype=jnp.float32) * 0.02
        b2 = jnp.zeros((D,), dtype=jnp.float32)
        return {'x': x, 'attention_mask': attention_mask, 'wr': wr, 'br': br, 'w1': w1, 'b1': b1, 'w2': w2, 'b2': b2}
    _L0_ffn_all = _L0_ffn_setup()
    _L0_ffn_in = {k: v for k, v in _L0_ffn_all.items() if k in ('attention_mask', 'wr', 'br', 'w1', 'b1', 'w2', 'b2')}
    del _L0_ffn_all

    def _L1_gnn_setup():
        import jax, jax.numpy as jnp
        import numpy as np
        N_NODES = 3125
        N_EDGES = 25000
        D_IN = 256
        D_OUT = 256
        N_REL = 4
        key = jax.random.key(seed)
        ks = jax.random.split(key, 7)
        x = jax.random.normal(ks[0], (N_NODES, D_IN), dtype=jnp.float32)
        src = jax.random.randint(ks[1], (N_EDGES,), 0, N_NODES, dtype=jnp.int32)
        dst = jax.random.randint(ks[2], (N_EDGES,), 0, N_NODES, dtype=jnp.int32)
        edge_type = jax.random.randint(ks[3], (N_EDGES,), 0, N_REL, dtype=jnp.int32)
        scale_in = 1.0 / np.sqrt(D_IN)
        self_W = jax.random.uniform(ks[4], (D_IN, D_OUT), dtype=jnp.float32, minval=-scale_in, maxval=scale_in)
        self_b = jax.random.uniform(ks[5], (D_OUT,), dtype=jnp.float32, minval=-scale_in, maxval=scale_in)
        rel_W = jax.random.uniform(ks[6], (N_REL, D_IN, D_OUT), dtype=jnp.float32, minval=-scale_in, maxval=scale_in)
        return {'x': x, 'src': src, 'dst': dst, 'edge_type': edge_type, 'self_W': self_W, 'self_b': self_b, 'rel_W': rel_W}
    _L1_gnn_all = _L1_gnn_setup()
    _L1_gnn_in = {k: v for k, v in _L1_gnn_all.items() if k in ('self_W', 'self_b', 'rel_W')}
    del _L1_gnn_all

    def _L1_ffn_setup():
        import jax, jax.numpy as jnp
        import numpy as np
        NUM_EXPERTS = 8
        TOP_K = 2
        B, S, D = (8, 512, 256)

        def _moe(tokens, router_w, w1, b1, w2, b2):
            N = tokens.shape[0]
            E = router_w.shape[0]
            logits = tokens.astype(jnp.float32) @ router_w.astype(jnp.float32).T
            probs = jax.nn.softmax(logits, axis=-1)
            rw, re = jax.lax.top_k(probs, TOP_K)
            if TOP_K > 1:
                rw = rw / jnp.maximum(rw.sum(-1, keepdims=True), 1e-12)
            rw = rw.astype(tokens.dtype)
            combine = jnp.zeros((N, E), tokens.dtype).at[jnp.arange(N)[:, None], re].set(rw)
            out = tokens
            for e in range(E):
                h = jax.nn.gelu(tokens @ w1[e] + b1[e], approximate=False)
                y = h @ w2[e] + b2[e]
                out = out + combine[:, e:e + 1] * y
            return out
        key = jax.random.key(seed)
        ks = jax.random.split(key, 4)
        scale = 1.0 / np.sqrt(D).astype(np.float32)
        return {'input_embeddings': jax.random.normal(ks[0], (B, S, D), jnp.float32), 'router_w': jax.random.normal(ks[1], (NUM_EXPERTS, D), jnp.float32) * scale, 'w1': jax.random.normal(ks[2], (NUM_EXPERTS, D, D), jnp.float32) * scale, 'b1': jnp.zeros((NUM_EXPERTS, D), jnp.float32), 'w2': jax.random.normal(ks[3], (NUM_EXPERTS, D, D), jnp.float32) * scale, 'b2': jnp.zeros((NUM_EXPERTS, D), jnp.float32)}
    _L1_ffn_all = _L1_ffn_setup()
    _L1_ffn_in = {k: v for k, v in _L1_ffn_all.items() if k in ('router_w', 'w1', 'b1', 'w2', 'b2')}
    del _L1_ffn_all
    return {'x': x, 'src': src, 'dst': dst, 'edge_type_4': edge_type_4, 'L0_gnn_W': _L0_gnn_in['W'], 'L0_gnn_a_l': _L0_gnn_in['a_l'], 'L0_gnn_a_r': _L0_gnn_in['a_r'], 'L0_ffn_attention_mask': _L0_ffn_in['attention_mask'], 'L0_ffn_wr': _L0_ffn_in['wr'], 'L0_ffn_br': _L0_ffn_in['br'], 'L0_ffn_w1': _L0_ffn_in['w1'], 'L0_ffn_b1': _L0_ffn_in['b1'], 'L0_ffn_w2': _L0_ffn_in['w2'], 'L0_ffn_b2': _L0_ffn_in['b2'], 'L1_gnn_self_W': _L1_gnn_in['self_W'], 'L1_gnn_self_b': _L1_gnn_in['self_b'], 'L1_gnn_rel_W': _L1_gnn_in['rel_W'], 'L1_ffn_router_w': _L1_ffn_in['router_w'], 'L1_ffn_w1': _L1_ffn_in['w1'], 'L1_ffn_b1': _L1_ffn_in['b1'], 'L1_ffn_w2': _L1_ffn_in['w2'], 'L1_ffn_b2': _L1_ffn_in['b2']}

def reference(x, src, dst, edge_type_4, L0_gnn_W, L0_gnn_a_l, L0_gnn_a_r, L0_ffn_attention_mask, L0_ffn_wr, L0_ffn_br, L0_ffn_w1, L0_ffn_b1, L0_ffn_w2, L0_ffn_b2, L1_gnn_self_W, L1_gnn_self_b, L1_gnn_rel_W, L1_ffn_router_w, L1_ffn_w1, L1_ffn_b1, L1_ffn_w2, L1_ffn_b2):
    import jax
    import jax.numpy as jnp

    def _L0_gnn_ref(x, edge, W, a_l, a_r):
        import jax, jax.numpy as jnp
        import numpy as np
        N = 3125
        E = 50000
        IN_F = 256
        OUT_F = 64
        NHEAD = 4
        ALPHA = 0.2

        def _gat_forward(x, W, a_l, a_r, edge):
            n = x.shape[0]
            row, col = (edge[0], edge[1])
            h = (x @ W).reshape(n, NHEAD, OUT_F)
            hl = jnp.sum(a_l * h, axis=-1)
            hr = jnp.sum(a_r * h, axis=-1)
            e = jax.nn.leaky_relu(hl[row] + hr[col], negative_slope=ALPHA)
            e_max = jax.ops.segment_max(e, row, num_segments=n)
            e_max = jnp.where(jnp.isfinite(e_max), e_max, 0.0)
            ee = jnp.exp(e - e_max[row])
            denom = jax.ops.segment_sum(ee, row, num_segments=n)
            att = ee / denom[row]
            msg = att[:, :, None] * h[col]
            out_h = jax.ops.segment_sum(msg, row, num_segments=n)
            return out_h.reshape(n, NHEAD * OUT_F)
        return _gat_forward(x, W, a_l, a_r, edge)

    def _L0_ffn_ref(x, attention_mask, wr, br, w1, b1, w2, b2):
        import jax, jax.numpy as jnp
        import numpy as np
        B, S, D = (8, 256, 256)
        H = 4 * D
        CAPACITY = 0.5
        b, s, d = x.shape
        weights = (jnp.einsum('bsd,do->bso', x, wr) + br)[..., 0]
        k = max(1, int(CAPACITY * s))
        kk = k - 1 if k > 1 else 1
        _, idx = jax.lax.top_k(weights, k)
        sel_idx = idx[:, :kk]
        sel = jnp.take_along_axis(x, sel_idx[:, :, None], axis=1)
        h = jax.nn.gelu(jnp.einsum('bkd,dh->bkh', sel, w1) + b1)
        y = jnp.einsum('bkh,hd->bkd', h, w2) + b2
        w_sel = jnp.take_along_axis(weights, sel_idx, axis=1)
        y = y * w_sel[..., None]
        batch_idx = jnp.arange(b)[:, None]
        processed = jnp.zeros_like(x).at[batch_idx, sel_idx].set(y)
        return processed + x

    def _L1_gnn_ref(x, src, dst, edge_type, self_W, self_b, rel_W):
        import jax, jax.numpy as jnp
        import numpy as np
        N_NODES = 3125
        N_EDGES = 25000
        D_IN = 256
        D_OUT = 256
        N_REL = 4
        num_nodes = x.shape[0]
        x_src = x[src]
        msgs = jnp.zeros((src.shape[0], D_OUT), dtype=x.dtype)
        for r in range(N_REL):
            mask = (edge_type == r)[:, None]
            msgs = jnp.where(mask, x_src @ rel_W[r], msgs)
        agg = jax.ops.segment_sum(msgs, dst, num_segments=num_nodes)
        deg = jax.ops.segment_sum(jnp.ones_like(dst, dtype=x.dtype), dst, num_segments=num_nodes)
        deg = jnp.clip(deg, 1.0, None)[:, None]
        return jax.nn.relu(x @ self_W + self_b + agg / deg)

    def _L1_ffn_ref(input_embeddings, router_w, w1, b1, w2, b2):
        import jax, jax.numpy as jnp
        import numpy as np
        NUM_EXPERTS = 8
        TOP_K = 2
        B, S, D = (8, 512, 256)

        def _moe(tokens, router_w, w1, b1, w2, b2):
            N = tokens.shape[0]
            E = router_w.shape[0]
            logits = tokens.astype(jnp.float32) @ router_w.astype(jnp.float32).T
            probs = jax.nn.softmax(logits, axis=-1)
            rw, re = jax.lax.top_k(probs, TOP_K)
            if TOP_K > 1:
                rw = rw / jnp.maximum(rw.sum(-1, keepdims=True), 1e-12)
            rw = rw.astype(tokens.dtype)
            combine = jnp.zeros((N, E), tokens.dtype).at[jnp.arange(N)[:, None], re].set(rw)
            out = tokens
            for e in range(E):
                h = jax.nn.gelu(tokens @ w1[e] + b1[e], approximate=False)
                y = h @ w2[e] + b2[e]
                out = out + combine[:, e:e + 1] * y
            return out
        b, s, d = input_embeddings.shape
        tokens = input_embeddings.reshape(b * s, d)
        return _moe(tokens, router_w, w1, b1, w2, b2).reshape(b, s, d)
    edge_index = jnp.stack([src, dst])
    x = x + _L0_gnn_ref(_layernorm(x, axis=-1), edge_index, L0_gnn_W, L0_gnn_a_l, L0_gnn_a_r)
    x = x + _L0_ffn_ref(_layernorm(x, axis=-1)[None], L0_ffn_attention_mask, L0_ffn_wr, L0_ffn_br, L0_ffn_w1, L0_ffn_b1, L0_ffn_w2, L0_ffn_b2)[0]
    x = x + _L1_gnn_ref(_layernorm(x, axis=-1), src, dst, edge_type_4, L1_gnn_self_W, L1_gnn_self_b, L1_gnn_rel_W)
    x = x + _L1_ffn_ref(_layernorm(x, axis=-1)[None], L1_ffn_router_w, L1_ffn_w1, L1_ffn_b1, L1_ffn_w2, L1_ffn_b2)[0]
    return x

_drawn_inputs = setup_inputs


def setup_inputs(seed=0):
    import zlib

    import numpy as np

    out = dict(_drawn_inputs(seed))
    spreads = {'L0_ffn_b1': (0.0, 0.8),
     'L0_ffn_b2': (0.0, 0.541),
     'L1_ffn_b1': (0.0, 0.475),
     'L1_ffn_b2': (0.0, 0.336)}
    factors = {'L0_ffn_wr': 3.177, 'L0_ffn_w1': 3.824, 'L0_ffn_w2': 3.382, 'L1_gnn_self_b': 3.544}
    for name, (base, spread) in spreads.items():
        noise = np.random.default_rng([zlib.crc32(name.encode()), seed]).standard_normal(out[name].shape)
        drawn = base * np.exp(spread * noise) if base else spread * noise
        out[name] = jnp.asarray(drawn.astype(out[name].dtype))
    for name, factor in factors.items():
        out[name] = (out[name] * factor).astype(out[name].dtype)
    return out
```

```python
from contextlib import ExitStack

import concourse.bass as bass
from concourse import mybir

ALU = mybir.AluOpType
ACT = mybir.ActivationFunctionType
AX = mybir.AxisListType.X
F32 = mybir.dt.float32
F16 = mybir.dt.float16
BF16 = mybir.dt.bfloat16
I32 = mybir.dt.int32
U16 = mybir.dt.uint16
ENG = mybir.EngineType
RMAX = bass.bass_isa.ReduceOp.max

N = 3125
E = 53125
D = 256
NP = 125
NT = N // NP
EC = E // NP
HEADS = 4
HD = D // HEADS
REL = 4
HID = 4 * D
EXP = 8
TOPK = 1561
EPS = 1e-5
SLOPE = 0.2

PAIR = 256
PAIRS = (E + NT * (PAIR - 1)) // PAIR
COLS = 2 * PAIRS
SORT_N = 17
SORT_STEPS = EC // SORT_N
GRP = 8
GRPS = 2
RING = GRP * GRPS
EDGE_STEPS = COLS // RING
AW = 260
U5 = 5
NODE_STEPS = NT // U5
SPLIT = ((0, 375), (375, 250))
BIG = 12582912.0
LOW = 2048

assert NT * NP == N and EC * NP == E and SORT_STEPS * SORT_N == EC and EDGE_STEPS * RING == COLS


class Lane:

    CREDIT = 256

    def __init__(self, nc, eng, sem):
        self.nc, self.eng, self.sem = nc, eng, sem
        self.base, self.n = self.CREDIT, 0
        eng.sem_inc(sem, self.CREDIT)

    def mark(self, ins):
        ins.then_inc(self.sem, 1)
        self.n += 1
        return (self.sem, self.base + self.n)

    def now(self):
        return (self.sem, self.base + self.n)


def wait(eng, *tickets):
    for sem, value in tickets:
        eng.wait_ge(sem, value)


def wait_apart(lane, *tickets):
    wait(lane.eng, *tickets)
    lane.eng.sem_inc(lane.sem, 1)
    lane.n += 1


class loop:

    def __init__(self, nc, steps, per):
        self.nc, self.steps, self.per = nc, steps, per

    def __enter__(self):
        self.ctx = self.nc.Fori(0, self.steps)
        i = self.ctx.__enter__()
        self.start = {}
        for lane, k in self.per.items():
            self.start[lane] = lane.base + lane.n
            lane.base, lane.n = i * k + self.start[lane], 0
        return i

    def __exit__(self, *a):
        if a[0] is None:
            got = [lane.n for lane in self.per]
            want = list(self.per.values())
            assert got == want, f"marks of the body: {got}, stated {want}"
            for lane, k in self.per.items():
                lane.base, lane.n = self.start[lane] + self.steps * k, 0
        return self.ctx.__exit__(*a)


class Dma:

    def __init__(self, sem):
        self.sem, self.total = sem, 0

    def mark(self, ins):
        ins.then_inc(self.sem, 16)
        self.total += 16
        return (self.sem, self.total)


def build(nc, x, src, dst, etype, W, a_l, a_r, wr, br, w1, b1, w2, b2,
          self_W, self_b, rel_W, router, mw1, mb1, mw2, mb2, out):
    with ExitStack() as ctx:
        def sem(name):
            return ctx.enter_context(nc.semaphore(name))

        def sb(name, shape, dt=F32, c=ctx):
            return c.enter_context(nc.sbuf_tensor(name, shape, dt))

        vec, act, pe, pool, sp = nc.vector, nc.scalar, nc.tensor, nc.gpsimd, nc.sync
        V, A, M, P, S = (Lane(nc, e, sem(n)) for e, n in (
            (vec, "vector_done"), (act, "scalar_done"), (pe, "tensor_done"), (pool, "pool_done"), (sp, "stores_done")))

        passed = Lane(nc, pool, sem("pool_passed"))
        ps = ctx.enter_context(nc.psum_tensor("ps", [128, 8, 512], F32))
        h_tab = nc.dram_tensor("h_tab", [N, AW], F32, kind="Internal").ap()
        y_tab = nc.dram_tensor("y_tab", [REL * N, D], F32, kind="Internal").ap()

        ident = sb("ident", [128, 128])
        ones = sb("ones", [128, 128])
        before = sb("before", [128, 128])
        upto = sb("upto", [128, 128])
        lower = sb("lower", [128, 128])
        iota_c = sb("iota_c", [128, COLS], F16)
        iota_r = sb("iota_r", [128, 128], F16)
        iota_n = sb("iota_n", [128, 128])
        zeros_e = sb("zeros_e", [128, EC], F16)
        wait(pool, P.mark(pool.memset(ones[:, :], 1.0)))
        for tile, op, cm in ((ident, ALU.is_equal, -1), (before, ALU.is_gt, -1), (upto, ALU.is_ge, -1), (lower, ALU.is_gt, 1)):
            P.mark(pool.affine_select(tile[:, :], ones[:, :], pattern=[[-cm, 128]], compare_op=op, fill=0.0,
                                      base=0, channel_multiplier=cm))
        for tile, n in ((iota_c, COLS), (iota_r, 128), (iota_n, 128)):
            P.mark(pool.iota(tile[:, :], [[1, n]], base=0, channel_multiplier=0, allow_small_or_imprecise_dtypes=True))
        P.mark(pool.memset(zeros_e[:, :], 0.0))
        t_const = P.now()

        xa = sb("xa", [NP, NT, D])
        acc = sb("acc", [NP, NT * AW])
        acc3 = acc[:, :].rearrange("p (t c) -> p t c", c=AW)
        gath = sb("gath", [128, RING, AW])
        hot = sb("hot", [128, RING, NP])
        at_rows = sb("at_rows", [128, GRPS, GRP], I32)
        stats = sb("stats", [NP, NT, 6])
        mean, var, tmp25, rstd, nmr = (sb(n, [NP, NT]) for n in ("mean", "var", "tmp25", "rstd", "nmr"))
        xs = sb("xs", [NP, U5, D])
        xt = sb("xt", [128, U5, 2, NP])
        slots = {}
        for g in "ab":
            slots[g] = (sb(f"local_{g}", [128, COLS]), sb(f"index_{g}", [128, COLS], I32),
                        sb(f"acc_at_{g}", [1, PAIRS], I32), sb(f"hl_at_{g}", [1, PAIRS], I32))
        hl_parts = sb("hl_parts", [NP, NT * 3 * HEADS], BF16)
        gmax = sb("gmax", [128, HEADS])

        d_in = [Dma(sem(f"load_{k}")) for k in range(14)]
        keys = {"a": sb("src_i", [NP, EC], I32), "b": sb("dst_i", [NP, EC], I32)}
        type_i = sb("type_i", [NP, EC], I32)
        ev = lambda v: v.rearrange("(p c) -> p c", c=EC)
        t_x = d_in[1].mark(sp.dma_start(xa[:, :, :], x.rearrange("(t p) d -> p t d", p=NP)))
        t_src = d_in[0].mark(sp.dma_start(keys["a"][:, :], ev(src)))
        t_dst = d_in[2].mark(sp.dma_start(keys["b"][:, :], ev(dst)))
        t_typ = d_in[3].mark(sp.dma_start(type_i[:, :], ev(etype)))

        def row_stats(t, src_tile):
            return V.mark(vec.bn_stats(stats[:, t, :], src_tile))

        def norm_factors():
            wait(vec, V.now())
            V.mark(vec.tensor_tensor(mean[:, :], stats[:, :, 1], stats[:, :, 4], ALU.add))
            V.mark(vec.tensor_tensor(tmp25[:, :], stats[:, :, 1], stats[:, :, 4], ALU.subtract))
            V.mark(vec.tensor_tensor(var[:, :], stats[:, :, 2], stats[:, :, 5], ALU.add))
            wait(vec, V.now())
            V.mark(vec.scalar_tensor_tensor(tmp25[:, :], tmp25[:, :], 0.25, tmp25[:, :], ALU.mult, ALU.mult))
            V.mark(vec.tensor_scalar(mean[:, :], mean[:, :], -0.5, None, ALU.mult))
            V.mark(vec.tensor_scalar(var[:, :], var[:, :], 1.0 / D, EPS, ALU.mult, ALU.add))
            wait(vec, V.now())
            wait(act, V.mark(vec.tensor_tensor(var[:, :], var[:, :], tmp25[:, :], ALU.add)))
            wait(vec, A.mark(act.activation(tmp25[:, :], var[:, :], ACT.Sqrt)))
            wait(vec, V.mark(vec.reciprocal(rstd[:, :], tmp25[:, :])))
            return V.mark(vec.tensor_tensor(nmr[:, :], mean[:, :], rstd[:, :], ALU.mult))

        def normalise(t, u):
            return V.mark(vec.tensor_scalar(xs[:, u, :], xa[:, t, :], rstd[:, t], nmr[:, t], ALU.mult, ALU.add))

        def transpose_tile(u, t_xs, bank):
            wait(pe, t_xs)
            for k in range(2):
                t = pe.transpose(ps[:, bank, k * NP:(k + 1) * NP], xs[:, u, k * 128:(k + 1) * 128], ident[0:NP, 0:NP])
            wait(act, M.mark(t))
            return A.mark(act.copy(xt[:, u, :, :], ps[:, bank, 0:2 * NP].rearrange("p (k n) -> p k n", k=2)))

        def col(tile, t):
            return tile[:, bass.ds(t, 1)]

        def stored(sems, i):
            for s in sems:
                sp.wait_ge(s, i * 16 + 16)
            sp.sem_inc(S.sem, 1)
            S.n += 1

        def everyone():
            for lane in (V, A, M, P, S):
                for e in (vec, act, pe, pool, sp):
                    wait(e, lane.now())

        def matrix(m):
            return m.rearrange("(k p) n -> p k n", p=128)

        with ExitStack() as sort_ctx:
            def sbs(name, shape, dt=F32):
                return sb(name, shape, dt, sort_ctx)

            w_cat = sbs("w_cat", [128, 2, 264])
            w_t = sbs("w_t", [128, 2, D])
            a_bd = sbs("a_bd", [128, 2, 8])
            hbuf = sbs("hbuf", [NP, U5, AW])
            hl = sbs("hl", [NP, NT, HEADS])
            hr = sbs("hr", [128, NT, HEADS])
            hl_r = sbs("hl_r", [NP, NT, HEADS])
            gm = sbs("gm", [128, HEADS])
            plan = {g: sbs(f"plan_{g}", [NP, 4, EC]) for g in "ab"}
            cnt = sbs("cnt", [NP, NT])
            offs = sbs("offs", [NP, NT])
            tot = sbs("tot", [NT, 4])
            starts = sbs("starts", [NT, NT])
            reach = sbs("reach", [NT, PAIRS])
            pair_tile = sbs("pair_tile", [1, PAIRS])
            key_f, tile_f, pos, tmp_e, oth_f = (sbs(n, [NP, EC]) for n in ("key_f", "tile_f", "pos", "tmp_e", "oth_f"))
            scratch = sbs("scratch", [NP, NT * EC], F16)
            in_tile = scratch[:, :].rearrange("p (q c) -> p q c", q=NT)
            hi_s = sbs("hi_s", [128, COLS])

            wait(sp, P.mark(pool.memset(a_bd[:, :, :], 0.0)))
            t_pos = P.mark(pool.memset(pos[:, :], 0.0))
            t_acc = P.mark(pool.memset(acc[:, :], 0.0))
            t_w = d_in[4].mark(sp.dma_start(w_cat[:, :, 0:D], matrix(W)))
            for h in range(HEADS):
                for k, a in ((0, a_r), (4, a_l)):
                    t_a = d_in[5].mark(sp.dma_start(a_bd[(h % 2) * HD:(h % 2 + 1) * HD, h // 2, k + h:k + h + 1],
                                                    a[0, h, :].rearrange("(d o) -> d o", o=1)))
            wait(vec, t_x)
            for t in range(NT):
                row_stats(t, xa[:, t, :])
            t_norm = norm_factors()

            wait(pe, t_const, t_w, t_a)
            for k in range(2):
                for j in range(2):
                    m = pe.transpose(ps[:, 0, (2 * k + j) * 128:(2 * k + j + 1) * 128], w_cat[:, k, j * 128:(j + 1) * 128], ident[:, :])
            wait(act, M.mark(m))
            t_wt = A.mark(act.copy(w_t[:, :, :].rearrange("p j (k i) -> p j k i", k=2),
                                   ps[:, 0, :].rearrange("p (k j i) -> p j k i", k=2, j=2)))
            wait(pe, t_wt)
            for k in range(2):
                for j in range(2):
                    m = pe.matmul(ps[:, 1, k * 8:k * 8 + 8], w_t[:, j, k * 128:(k + 1) * 128], a_bd[:, j, :],
                                  start=(j == 0), stop=(j == 1))
            wait(act, M.mark(m))
            t_wc = A.mark(act.copy(w_cat[:, :, D:D + 8], ps[:, 1, 0:16].rearrange("p (k c) -> p k c", k=2)))

            wait(pool, P.mark(pool.memset(hr[:, :, :], -3.0e38)))
            s_tab = [sem(f"h_stored_{u}") for u in range(U5)]
            wait(pe, t_wc)
            for e in (act, vec, pool, pe):
                wait(e, t_norm)
            with loop(nc, NODE_STEPS, {M: 2 * U5, A: 4 * U5, P: U5, S: 1}) as i:
                m0, a0, p0, s0 = M.now(), A.now(), P.now(), S.now()
                wait(act, m0)
                t_xs = [A.mark(act.activation(xs[:, u, :], xa[:, bass.ds(i * U5 + u, 1), :].rearrange("p a d -> p (a d)"),
                                              ACT.Identity, bias=col(nmr, i * U5 + u), scale=col(rstd, i * U5 + u)))
                        for u in range(U5)]
                wait(pe, a0)
                for u in range(U5):
                    bank = u % 2
                    t_xt = transpose_tile(u, t_xs[u], bank)
                    wait(pe, t_xt)
                    for k in range(2):
                        m = pe.matmul(ps[0:NP, 2 + bank, 0:264], xt[:, u, k, :], w_cat[:, k, :], start=(k == 0), stop=(k == 1))
                    if u == 0:
                        wait(act, s0)
                        wait(act, p0)
                    wait(act, M.mark(m))
                    t_h = A.mark(act.copy(hbuf[:, u, :], ps[0:NP, 2 + bank, 0:AW]))
                    t_l = A.mark(act.copy(hl[:, bass.ds(i * U5 + u, 1), :].rearrange("p a d -> p (a d)"), ps[0:NP, 2 + bank, AW:264]))
                    wait(sp, t_h)
                    sp.dma_start(h_tab[bass.ds((i * U5 + u) * NP, NP), :], hbuf[:, u, :]).then_inc(s_tab[u], 16)
                    wait(pool, t_h)
                    P.mark(pool.tensor_copy(hr[0:NP, bass.ds(i * U5 + u, 1), :].rearrange("p a d -> p (a d)"), hbuf[:, u, D:AW]))
                stored(s_tab, i)
            t_hr = P.now()
            wait(pool, S.now())

            def plan_sort(g, t_key, t_oth):
                own = lambda: wait(vec, V.now())
                wait(vec, t_key)
                V.mark(vec.tensor_copy(key_f[:, :], keys[g][:, :]))
                own()
                V.mark(vec.tensor_scalar(tile_f[:, :], key_f[:, :], 1.0 / NP, -(NP - 1) / 2 / NP, ALU.mult, ALU.add))
                own()
                V.mark(vec.tensor_scalar(tile_f[:, :], tile_f[:, :], BIG, BIG, ALU.add, ALU.subtract))
                own()
                for q in range(NT):
                    t = V.mark(vec.tensor_scalar(in_tile[:, q, :], tile_f[:, :], float(q), None, ALU.is_equal, ALU.add,
                                                 accum_out=cnt[:, q:q + 1]))
                wait(pe, t)
                wait(vec, M.mark(pe.matmul(ps[0:NT, 4, 0:1], cnt[:, :], ones[0:NP, 0:1], start=True, stop=True)))
                V.mark(vec.tensor_scalar(tot[:, 0:1], ps[0:NT, 4, 0:1], 1.0 / PAIR, (PAIR - 1) / 2 / PAIR, ALU.mult, ALU.add))
                own()
                V.mark(vec.tensor_scalar(tot[:, 1:2], tot[:, 0:1], BIG, BIG, ALU.add, ALU.subtract))
                own()
                t = V.mark(vec.tensor_scalar(starts[:, :], before[0:NT, 0:NT], tot[:, 1:2], float(PAIR), ALU.mult, ALU.mult))
                wait(pe, t)
                m = pe.matmul(ps[0:NT, 4, 8:9], upto[0:NT, 0:NT], tot[:, 1:2], start=True, stop=True)
                wait(vec, M.mark(m))
                V.mark(vec.tensor_copy(tot[:, 2:3], ps[0:NT, 4, 8:9]))
                pe.matmul(ps[0:NP, 7, 0:NT], before[0:NP, 0:NP], cnt[:, :], start=True, stop=False)
                m = pe.matmul(ps[0:NP, 7, 0:NT], ones[0:NT, 0:NP], starts[:, :], start=False, stop=True)
                wait(vec, M.mark(m))
                V.mark(vec.tensor_scalar(offs[:, :], ps[0:NP, 7, 0:NT], -1.0, None, ALU.add))
                own()
                t = V.mark(vec.tensor_scalar(reach[:, :], iota_c[0:NT, 0:PAIRS], tot[:, 2:3], None, ALU.is_ge))
                wait(pe, t)
                wait(vec, M.mark(pe.matmul(ps[0:1, 4, 0:PAIRS], ones[0:NT, 0:1], reach[:, :], start=True, stop=True)))
                V.mark(vec.tensor_scalar(pair_tile[:, :], ps[0:1, 4, 0:PAIRS], float(NT - 1), None, ALU.min))
                own()
                V.mark(vec.tensor_scalar(slots[g][2][:, :], pair_tile[:, :], float(AW), None, ALU.mult))
                V.mark(vec.tensor_scalar(slots[g][3][:, :], pair_tile[:, :], float(3 * HEADS), None, ALU.mult))
                for q in range(NT):
                    buf = ps[0:NP, 5 + q % 2, 0:EC]
                    V.mark(vec.tensor_tensor_scan(buf, in_tile[:, q, :], zeros_e[0:NP, :], offs[:, q:q + 1], ALU.add, ALU.add))
                    own()
                    V.mark(vec.copy_predicated(pos[:, :], in_tile[:, q, :].bitcast(U16), buf))
                own()
                row, column, pay1, pay2 = (plan[g][:, k, :] for k in range(4))
                V.mark(vec.tensor_scalar(tmp_e[:, :], pos[:, :], 1.0 / 128, -63.5 / 128, ALU.mult, ALU.add))
                own()
                V.mark(vec.tensor_scalar(column, tmp_e[:, :], BIG, BIG, ALU.add, ALU.subtract))
                own()
                V.mark(vec.scalar_tensor_tensor(row, column, -128.0, pos[:, :], ALU.mult, ALU.add))
                V.mark(vec.scalar_tensor_tensor(key_f[:, :], tile_f[:, :], -float(NP), key_f[:, :], ALU.mult, ALU.add))
                wait(vec, t_oth)
                V.mark(vec.tensor_scalar(tmp_e[:, :], oth_f[:, :], 1.0 / LOW, -(LOW - 1) / 2 / LOW, ALU.mult, ALU.add))
                own()
                V.mark(vec.tensor_scalar(tmp_e[:, :], tmp_e[:, :], BIG, BIG, ALU.add, ALU.subtract))
                own()
                V.mark(vec.scalar_tensor_tensor(pay2, tmp_e[:, :], -float(LOW), oth_f[:, :], ALU.mult, ALU.add))
                V.mark(vec.scalar_tensor_tensor(pay1, tmp_e[:, :], 128.0, key_f[:, :], ALU.mult, ALU.add))
                own()
                return V.mark(vec.tensor_scalar(pay1, pay1, 1.0, None, ALU.add))

            wait(vec, t_const, t_pos, t_dst)
            t_oth = V.mark(vec.tensor_copy(oth_f[:, :], keys["b"][:, :]))
            t_plan_a = plan_sort("a", t_src, t_oth)
            wait(vec, t_typ)
            V.mark(vec.tensor_copy(tmp_e[:, :], type_i[:, :]))
            V.mark(vec.tensor_copy(key_f[:, :], keys["a"][:, :]))
            wait(vec, V.now())
            t_oth = V.mark(vec.scalar_tensor_tensor(oth_f[:, :], tmp_e[:, :], float(N), key_f[:, :], ALU.mult, ALU.add))
            wait(vec, t_oth)
            t_plan_b = plan_sort("b", t_dst, t_oth)

            hot_c = sbs("hot_c", [NP, SORT_N, COLS], F16)
            hot_r = sbs("hot_r", [NP, SORT_N, 128], F16)
            pay = sbs("pay", [NP, 2, SORT_N, 128], F16)
            stage_v, stage_a, stage_p = (sbs(f"stage_{e}", [NP, 4, SORT_N]) for e in "vap")
            CHUNKS = ((0, 5), (5, 9), (9, 13), (13, 17))
            moved = Lane(nc, pe, sem("columns_moved"))
            weighed = Lane(nc, act, sem("payloads_weighed"))
            PAY_V, PAY_P = 3, 3

            def permute_open():
                wait(pe, t_const)
                for k in range(2):
                    pe.matmul(ps[:, 6 + k, 0:COLS], zeros_e[0:NP, 0:128], iota_c[0:NP, :], start=True, stop=False,
                              skip_group_check=True)

            def permute_close():
                for k in range(2):
                    m = pe.matmul(ps[:, 6 + k, 0:COLS], zeros_e[0:NP, 0:128], iota_c[0:NP, :], start=False, stop=True,
                                  skip_group_check=True)
                return M.mark(m)

            def permute_parts(i, g, by_v, by_p):
                by_a = SORT_N - by_v - by_p
                moved0, weighed0 = moved.now(), weighed.now()
                tick = {}
                at = bass.ds(i * SORT_N, SORT_N)

                def scalars():
                    wait(vec, V.now())
                    t = V.mark(vec.tensor_copy(stage_v[:, :, :], plan[g][:, :, at]))
                    wait(act, weighed0)
                    ta = weighed.mark(act.copy(stage_a[:, 2:4, :], plan[g][:, 2:4, at]))
                    wait(act, ta)
                    if by_p:
                        wait(pool, P.now())
                        wait_apart(passed, P.mark(pool.tensor_copy(stage_p[:, :, :], plan[g][:, :, at])), moved0)
                        for j in range(by_a + by_v, SORT_N):
                            for k in range(2):
                                tp = P.mark(pool.tensor_scalar(pay[:, k, j, :], iota_r[0:NP, :], stage_p[:, 0, j:j + 1],
                                                               stage_p[:, 2 + k, j:j + 1], ALU.is_equal, ALU.mult))
                            tick["p", j] = tp
                    wait(vec, t, weighed0, moved0)
                    tick["rows"] = V.mark(vec.tensor_tensor(
                        hot_r[:, 0:by_a, :], iota_r[0:NP, :].unsqueeze(1).to_broadcast([NP, by_a, 128]),
                        stage_v[:, 0, 0:by_a].unsqueeze(2).to_broadcast([NP, by_a, 128]), ALU.is_equal))

                def on_v(c):
                    lo, hi = CHUNKS[c]
                    for j in range(lo, hi):
                        t = vec.tensor_scalar(hot_c[:, j, :], iota_c[0:NP, :], stage_v[:, 1, j:j + 1], None, ALU.is_equal)
                        if by_a <= j < by_a + by_v:
                            for k in range(2):
                                t = vec.tensor_scalar(pay[:, k, j, :], iota_r[0:NP, :], stage_v[:, 0, j:j + 1],
                                                      stage_v[:, 2 + k, j:j + 1], ALU.is_equal, ALU.mult)
                    tick["v", c] = V.mark(t)

                def on_a(c):
                    lo, hi = CHUNKS[c]
                    if c == 0:
                        wait(act, tick["rows"], moved0)
                    for j in range(lo, min(hi, by_a)):
                        for k in range(2):
                            t = act.mul(pay[:, k, j, :], hot_r[:, j, :], stage_a[:, 2 + k, j:j + 1])
                    if lo < by_a:
                        tick["a", c] = weighed.mark(t)

                def on_pe(c):
                    lo, hi = CHUNKS[c]
                    wait(pe, tick["v", c])
                    if ("a", c) in tick:
                        wait(pe, tick["a", c])
                    for j in range(lo, hi):
                        if ("p", j) in tick:
                            wait(pe, tick["p", j])
                        for k in range(2):
                            m = pe.matmul(ps[:, 6 + k, 0:COLS], pay[:, k, j, :], hot_c[:, j, :], start=False, stop=False,
                                          skip_group_check=True)
                    moved.mark(m)

                return scalars, on_v, on_a, on_pe

            def unpack(g, t_moved):
                local, index = slots[g][0], slots[g][1]
                wait(vec, t_moved, V.now())
                V.mark(vec.tensor_scalar(hi_s[:, :], ps[:, 6, 0:COLS], 1.0 / 128, -(NP / 2) / 128, ALU.mult, ALU.add))
                wait(vec, V.now())
                V.mark(vec.tensor_scalar(hi_s[:, :], hi_s[:, :], BIG, BIG, ALU.add, ALU.subtract))
                wait(vec, V.now())
                V.mark(vec.scalar_tensor_tensor(index[:, :], hi_s[:, :], float(LOW), ps[:, 7, 0:COLS], ALU.mult, ALU.add))
                V.mark(vec.scalar_tensor_tensor(local[:, :], hi_s[:, :], -128.0, ps[:, 6, 0:COLS], ALU.mult, ALU.add))
                wait(vec, V.now())
                return V.mark(vec.tensor_scalar(local[:, :], local[:, :], -1.0, None, ALU.add))

            wait(pe, A.now(), V.now())
            permute_open()
            wait(act, t_plan_a)
            wait(pool, t_plan_a)
            with loop(nc, SORT_STEPS, {V: 2 + len(CHUNKS), P: 1 + 2 * PAY_P, passed: 1, moved: len(CHUNKS), weighed: 1 + 3}) as i:
                scalars, on_v, on_a, on_pe = permute_parts(i, "a", PAY_V, PAY_P)
                scalars()
                for c in range(len(CHUNKS)):
                    on_v(c)
                    on_a(c)
                    on_pe(c)
            t_slots_a = unpack("a", permute_close())

            parts = hl_parts[:, :].rearrange("p (t h c) -> p t h c", t=NT, h=HEADS)
            wait(vec, A.now())
            wait(vec, V.mark(vec.tensor_copy(parts[:, :, :, 0], hl[:, :, :])))
            wait(vec, V.mark(vec.tensor_tensor(hl_r[:, :, :], hl[:, :, :], parts[:, :, :, 0], ALU.subtract)))
            wait(vec, V.mark(vec.tensor_copy(parts[:, :, :, 1], hl_r[:, :, :])))
            wait(vec, V.mark(vec.tensor_tensor(hl_r[:, :, :], hl_r[:, :, :], parts[:, :, :, 1], ALU.subtract)))
            t_parts = V.mark(vec.tensor_copy(parts[:, :, :, 2], hl_r[:, :, :]))
            wait(vec, t_hr)
            t = V.mark(vec.tensor_reduce(gm[:, :], hr[:, :, :].rearrange("p t h -> p h t"), AX, ALU.max))
            wait(pool, t)
            t_gmax = P.mark(pool.partition_all_reduce(gmax[:, :], gm[:, :], 128, RMAX))

            s_gath = [sem(f"gathered_{k}") for k in range(RING)]
            freed = [Lane(nc, vec, sem(f"group_freed_{g}")) for g in range(GRPS)]
            hot_t = sbs("hot_t", [NP, GRPS, GRP, 128], BF16)
            hle = sbs("hle", [128, GRPS, GRP * HEADS])
            score = sbs("score", [128, GRPS, 2, GRP * HEADS])
            expo = sbs("expo", [128, GRPS, GRP * HEADS])
            hl_bc = gmax[:, :].unsqueeze(1).to_broadcast([128, GRP, HEADS])

            def gather(i, g, table, width, idx):
                wait(pool, freed[g].now())
                wait_apart(passed, P.mark(pool.tensor_copy(at_rows[:, g, :], idx[:, bass.ds(i * RING + g * GRP, GRP)])))
                for s in range(g * GRP, (g + 1) * GRP):
                    pool.indirect_dma_start(gath[:, s, 0:width], None, table,
                                            bass.IndirectOffsetOnAxis(ap=at_rows[:, g, s % GRP:s % GRP + 1], axis=0)
                                            ).then_inc(s_gath[s], 16)

            def gathered(eng, turn, lo, hi):
                for s in range(lo, hi):
                    eng.wait_ge(s_gath[s], turn * 16 + 16)

            def one_hots(i, g, local):
                at = local[:, bass.ds(i * RING + g * GRP, GRP)]
                return V.mark(vec.tensor_tensor(hot[:, g * GRP:(g + 1) * GRP, :], iota_n[:, 0:NP].unsqueeze(1).to_broadcast([128, GRP, NP]),
                                                at.unsqueeze(2).to_broadcast([128, GRP, NP]), ALU.is_equal))

            def pair_offsets(engine, table, i, top):
                return nc.values_load_multi_w_load_instructions(
                    table[0:1, bass.ds(i * (RING // 2), RING // 2)], engines=[engine], min_val=0, max_val=top,
                    skip_runtime_bounds_check_because="the tile is the minimum of a count and NT - 1")[1]

            def sum_pair(q, width, t_emptied):
                wait(pe, t_emptied)
                for s in (2 * q, 2 * q + 1):
                    m = pe.matmul(ps[0:NP, 4 + q % 2, 0:width], hot[:, s, :], gath[:, s, 0:width], start=(s == 2 * q), stop=(s == 2 * q + 1))
                return M.mark(m)

            def add_pair(q, offset, width, t_sum):
                wait(vec, t_sum, V.now())
                at = acc[:, bass.ds(offset, width)]
                return V.mark(vec.tensor_tensor(at, at, ps[0:NP, 4 + q % 2, 0:width], ALU.add))

            def attention_body(i, with_sort):
                v0, m0, a0 = V.now(), M.now(), A.now()
                for g in range(GRPS):
                    gather(i, g, h_tab, AW, slots["a"][1])
                v_off = pair_offsets(ENG.DVE, slots["a"][2], i, (NT - 1) * AW)
                p_off = pair_offsets(ENG.PE, slots["a"][3], i, (NT - 1) * 3 * HEADS)
                wait(vec, m0)
                t_hot = [one_hots(i, g, slots["a"][0]) for g in range(GRPS)]
                if with_sort:
                    scalars, on_v, on_a, on_pe = permute_parts(i, "b", 0, 0)
                    scalars()
                    on_v(0)
                    on_v(1)
                t_copy = [a0, a0]
                t_pick = []
                for g in range(GRPS):
                    wait(pe, t_hot[g])
                    for half in range(2):
                        wait(pe, t_copy[half])
                        for s in range(4):
                            m = pe.transpose(ps[0:NP, half, s * 128:(s + 1) * 128], hot[:, g * GRP + half * 4 + s, :], ident[:, :])
                        wait(act, M.mark(m))
                        t_copy[half] = A.mark(act.copy(hot_t[:, g, half * 4:half * 4 + 4, :],
                                                       ps[0:NP, half, :].rearrange("p (s e) -> p s e", s=4)))
                    wait(pe, *t_copy)
                    for s in range(GRP):
                        m = pe.matmul(ps[:, 2 + g, s * 12:s * 12 + 12], hot_t[:, g, s, :],
                                      hl_parts[:, bass.ds(p_off[(g * GRP + s) // 2], 12)], start=True, stop=True)
                    t_pick.append(M.mark(m))
                if with_sort:
                    for c in (0, 1):
                        on_a(c)
                        on_pe(c)
                t_sums = {}
                t_add = {0: v0, 1: v0}
                for g in range(GRPS):
                    lo, hi = g * GRP, (g + 1) * GRP
                    wait(vec, t_pick[g])
                    three = lambda tile: tile.rearrange("p (s h) -> p s h", h=HEADS)
                    wait(vec, V.mark(vec.tensor_reduce(hle[:, g, :], ps[:, 2 + g, 0:GRP * 12].rearrange("p (s c) -> p s c", c=3), AX, ALU.add)))
                    V.mark(vec.tensor_tensor(three(score[:, g, 1, :]), three(hle[:, g, :]), hl_bc, ALU.add))
                    gathered(vec, i, lo, hi)
                    V.mark(vec.tensor_tensor(three(score[:, g, 0, :]), three(hle[:, g, :]), gath[:, lo:hi, D:AW], ALU.add))
                    wait(vec, V.now())
                    V.mark(vec.scalar_tensor_tensor(score[:, g, :, :], score[:, g, :, :], SLOPE, score[:, g, :, :], ALU.mult, ALU.max))
                    wait(vec, V.now())
                    t = V.mark(vec.tensor_tensor(expo[:, g, :], score[:, g, 0, :], score[:, g, 1, :], ALU.subtract))
                    wait(act, t)
                    t = A.mark(act.activation(gath[:, lo:hi, D:AW], three(expo[:, g, :]), ACT.Exp))
                    wait(vec, t)
                    for half in range(2):
                        a, b = lo + 4 * half, lo + 4 * half + 4
                        rows = gath[:, a:b, 0:D].rearrange("p s (h d) -> p s h d", h=HEADS)
                        t = V.mark(vec.tensor_tensor(rows, rows, gath[:, a:b, D:AW].unsqueeze(3).to_broadcast([128, 4, HEADS, HD]), ALU.mult))
                        wait(pe, t)
                        for q in (a // 2, a // 2 + 1):
                            t_sums[q] = (q, t)
                    if with_sort:
                        on_v(2 + g)
                        on_a(2 + g)
                    for q in range(lo // 2, hi // 2):
                        t = sum_pair(q, AW, t_add[q % 2])
                        t_add[q % 2] = add_pair(q, v_off[q], AW, t)
                    freed[g].mark(vec.nop())
                    if with_sort:
                        on_pe(2 + g)

            for e in (act, pe, pool, vec):
                wait(e, t_slots_a, t_plan_b, t_parts, t_gmax, P.now(), t_acc)
            permute_open()
            SORT_MARKS = {V: 2 + len(CHUNKS), moved: len(CHUNKS), weighed: 1 + len(CHUNKS)}
            BODY = {V: 24, P: GRPS, passed: GRPS, M: 14, A: 6, freed[0]: 1, freed[1]: 1}
            with loop(nc, SORT_STEPS, {**BODY, **SORT_MARKS, V: BODY[V] + SORT_MARKS[V]}) as i:
                attention_body(i, True)
            t_slots_b = unpack("b", permute_close())
            with loop(nc, EDGE_STEPS - SORT_STEPS, BODY) as i:
                attention_body(i + SORT_STEPS, False)

            everyone()

        flat = lambda tile, t: tile[:, bass.ds(t, 1), :].rearrange("p a d -> p (a d)")
        acc_cols = lambda t, c, n: acc[:, bass.ds(t * AW + c, n)]

        def norm_body(i, banks, full=None, add_back=False, after=()):
            m0, a0, p0 = M.now(), A.now(), P.now()
            wait(vec, m0, p0, a0)
            t_xs = [V.mark(vec.tensor_scalar(xs[:, u, :], flat(xa, i * U5 + u), col(rstd, i * U5 + u), col(nmr, i * U5 + u),
                                             ALU.mult, ALU.add)) for u in range(U5)]
            wait(act, m0, p0)
            t_xt = []
            for u in range(U5):
                wait(pe, t_xt[u - len(banks)] if u >= len(banks) else a0)
                t_xt.append(transpose_tile(u, t_xs[u], banks[u % len(banks)]))
                if add_back:
                    wait(pool, t_xs[u])
                    P.mark(pool.tensor_tensor(flat(xa, i * U5 + u), flat(xa, i * U5 + u), xs[:, u, :], ALU.add))
                if full is not None:
                    wait(pool, t_xt[u])
                    P.mark(pool.tensor_copy(full[:, :, bass.ds((i * U5 + u) * NP, NP)], xt[:, u, :, :]))
            return t_xt

        def row_bcast(tile, row, load, k):
            return load.mark(sp.dma_start(tile, row.rearrange("(o d) -> o d", o=1).to_broadcast([k, row.shape[0]])))

        with ExitStack() as ffn_ctx:
            def sbf(name, shape, dt=F32):
                return sb(name, shape, dt, ffn_ctx)

            xn_t = sbf("xn_t", [128, 2, N])
            hid = sbf("hid", [128, HID // 128, U5 * NP])
            w1_s = sbf("w1_s", [128, 2, HID])
            w2_s = sbf("w2_s", [128, HID // 128, D])
            b1_s = sbf("b1_s", [128, HID // 128])
            b2_s = sbf("b2_s", [1, D])
            wr_s = sbf("wr_s", [128, 2])
            br_s = sbf("br_s", [1, 1])
            w_row = sbf("w_row", [1, N])
            w_all = sbf("w_all", [128, N])
            w_col = sbf("w_col", [NP, NT])
            above = sbf("above", [NP, NT, 3])
            junk = sbf("junk", [NP, N], BF16)
            same = sbf("same", [NP, NP])
            gate = sbf("gate", [NP, NT])
            dinv = sbf("dinv", [NP, NT, HEADS])
            t_w1 = d_in[6].mark(sp.dma_start(w1_s[:, :, :], matrix(w1)))
            d_in[7].mark(sp.dma_start(w2_s[:, :, :], matrix(w2)))
            t_w2 = d_in[7].mark(sp.dma_start(b1_s[:, :], b1.rearrange("(k p) -> p k", p=128), allow_slow_non_contiguous=True))
            d_in[8].mark(sp.dma_start(b2_s[:, :], b2.rearrange("(o d) -> o d", o=1)))
            d_in[8].mark(sp.dma_start(wr_s[:, :], wr.rearrange("(k p) o -> p (k o)", p=128), allow_slow_non_contiguous=True))
            t_wr = d_in[8].mark(sp.dma_start(br_s[:, :], br.rearrange("(o d) -> o d", o=1)))

            V.mark(vec.tensor_scalar(dinv[:, :, :], acc3[:, :, D:AW], 1e-38, None, ALU.max))
            wait(vec, V.now())
            V.mark(vec.reciprocal(dinv[:, :, :], dinv[:, :, :]))
            wait(vec, V.now())
            for i in range(NODE_STEPS):
                at = slice(i * U5, (i + 1) * U5)
                rows = acc3[:, at, 0:D].rearrange("p t (h d) -> p t h d", h=HEADS)
                wait(vec, V.mark(vec.tensor_tensor(rows, rows, dinv[:, at, :].unsqueeze(3).to_broadcast([NP, U5, HEADS, HD]), ALU.mult)))
                wait(vec, V.mark(vec.tensor_tensor(xa[:, at, :], xa[:, at, :], acc3[:, at, 0:D], ALU.add)))
                for t in range(i * U5, (i + 1) * U5):
                    row_stats(t, xa[:, t, :])
            t_norm = norm_factors()
            for e in (vec, act, pool, pe):
                wait(e, t_norm, t_wr, t_w1, t_w2)
            with loop(nc, NODE_STEPS, {V: U5, M: U5, A: U5, P: 2 * U5}) as i:
                norm_body(i, (0, 1), full=xn_t, add_back=True)

            wait(pe, P.now(), A.now())
            for c in range(10):
                n = 313 if c % 2 == 0 else 312
                lo = c // 2 * 625 + c % 2 * 313
                if c >= 2:
                    wait(pe, t_c[c - 2])
                else:
                    t_c = []
                for k in range(2):
                    m = pe.matmul(ps[0:1, c % 2, 0:n], wr_s[:, k:k + 1], xn_t[:, k, lo:lo + n], start=(k == 0), stop=(k == 1))
                wait(act, M.mark(m))
                t_c.append(A.mark(act.activation(w_row[:, lo:lo + n], ps[0:1, c % 2, 0:n], ACT.Identity, bias=br_s[:, 0:1])))
            wait(pe, t_c[-1])
            wait(pool, t_c[-1])
            t_all = P.mark(pool.partition_broadcast(w_all[:, :], w_row[0:1, :], 128))
            for t in range(NT):
                m = pe.transpose(ps[0:NP, 0, t:t + 1], w_row[0:1, t * NP:(t + 1) * NP], ident[0:1, 0:1])
            wait(act, M.mark(m))
            t_col = A.mark(act.copy(w_col[:, :], ps[0:NP, 0, 0:NT]))

            wait(pe, t_col)
            with loop(nc, NODE_STEPS, {M: 16 + U5, A: 16 + U5}) as i:
                a0 = A.now()
                t_g = []
                for c in range(HID // 128):
                    for half, (lo, n) in enumerate(SPLIT):
                        b = (2 * c + half) % 4
                        wait(pe, t_g[-4] if len(t_g) >= 4 else a0)
                        for k in range(2):
                            m = pe.matmul(ps[:, b, 0:n], w1_s[:, k, c * 128:(c + 1) * 128],
                                          xn_t[:, k, bass.ds(i * (U5 * NP) + lo, n)], start=(k == 0), stop=(k == 1))
                        wait(act, M.mark(m))
                        t_g.append(A.mark(act.activation(hid[:, c, lo:lo + n], ps[:, b, 0:n], ACT.Gelu_apprx_tanh,
                                                         bias=b1_s[:, c:c + 1])))
                wait(pe, t_g[-1])
                t_y = []
                for u in range(U5):
                    b = 4 + u % 2
                    if u >= 2:
                        wait(pe, t_y[u - 2])
                    for c in range(HID // 128):
                        pe.matmul(ps[0:NP, b, 0:D], hid[:, c, u * NP:(u + 1) * NP], w2_s[:, c, :], start=(c == 0), stop=False)
                    m = pe.matmul(ps[0:NP, b, 0:D], ones[0:1, 0:NP], b2_s[0:1, :], start=False, stop=True)
                    wait(act, M.mark(m))
                    t_y.append(A.mark(act.copy(acc_cols(i * U5 + u, 0, D), ps[0:NP, b, 0:D])))
            wait(vec, t_all, t_col)
            for t in range(NT):
                lo, hi = t * NP, (t + 1) * NP
                w = w_col[:, t:t + 1]
                if t:
                    V.mark(vec.tensor_scalar(junk[:, 0:lo], w_all[0:NP, 0:lo], w, None, ALU.is_ge, ALU.add, accum_out=above[:, t, 0:1]))
                else:
                    V.mark(vec.memset(above[:, 0, 0:1], 0.0))
                V.mark(vec.tensor_scalar(junk[:, lo:], w_all[0:NP, lo:], w, None, ALU.is_gt, ALU.add, accum_out=above[:, t, 1:2]))
                wait(vec, V.now())
                V.mark(vec.scalar_tensor_tensor(same[:, :], w_all[0:NP, lo:hi], w, lower[0:NP, 0:NP], ALU.is_equal, ALU.mult,
                                                accum_out=above[:, t, 2:3]))
                wait(vec, V.now())
            V.mark(vec.tensor_reduce(gate[:, :], above[:, :, :], AX, ALU.add))
            wait(vec, V.now())
            V.mark(vec.scalar_tensor_tensor(gate[:, :], gate[:, :], TOPK - 0.5, w_col[:, :], ALU.is_lt, ALU.mult))
            wait(vec, V.now(), A.now())
            with loop(nc, NODE_STEPS, {V: 2 * U5}) as i:
                t_x = [V.mark(vec.scalar_tensor_tensor(flat(xa, i * U5 + u), acc_cols(i * U5 + u, 0, D), col(gate, i * U5 + u),
                                                       flat(xa, i * U5 + u), ALU.mult, ALU.add)) for u in range(U5)]
                for u in range(U5):
                    wait(vec, t_x[u])
                    V.mark(vec.bn_stats(flat(stats, i * U5 + u), flat(xa, i * U5 + u)))
            everyone()

        xb = sb("xb", [NP, NT, D])

        with ExitStack() as tab_ctx:
            def sbt(name, shape, dt=F32):
                return sb(name, shape, dt, tab_ctx)

            rel_s = sbt("rel_s", [128, 2, REL, D])
            self_s = sbt("self_s", [128, 2, D])
            sb_s = sbt("sb_s", [NP, D])
            ybuf = sbt("ybuf", [NP, U5, REL, D])
            t_rel = d_in[9].mark(sp.dma_start(self_s[:, :, :], matrix(self_W)))
            for r in range(REL):
                t_rel = d_in[9].mark(sp.dma_start(rel_s[:, :, r, :], matrix(rel_W[r])))
            t_sb = row_bcast(sb_s[:, :], self_b, d_in[10], NP)
            t_acc = P.mark(pool.memset(acc[:, :], 0.0))
            t_one = P.mark(pool.memset(gath[:, :, D:AW], 1.0))
            t_norm = norm_factors()
            wait(vec, t_sb)
            for e in (vec, act, pool, pe):
                wait(e, t_norm, t_rel)
            y_rows = y_tab.rearrange("(r n) d -> n r d", r=REL)
            s_y = [sem(f"y_stored_{u}") for u in range(U5)]
            with loop(nc, NODE_STEPS, {V: 2 * U5, M: 3 * U5, A: 2 * U5, S: 1}) as i:
                v0, s0, a0 = V.now(), S.now(), A.now()
                t_xt = norm_body(i, (0, 1))
                t_y, t_self = [], []
                wait(act, s0)
                for u in range(U5):
                    wait(pe, t_xt[-1], t_y[-1] if t_y else a0)
                    for half in range(2):
                        for k in range(2):
                            m = pe.matmul(ps[0:NP, 2 + half, :], xt[:, u, k, :], rel_s[:, k, 2 * half:2 * half + 2, :].rearrange("p r d -> p (r d)"),
                                          start=(k == 0), stop=(k == 1))
                    wait(act, M.mark(m))
                    t_y.append(A.mark(act.copy(ybuf[:, u, :, :].rearrange("p (a r) d -> p a (r d)", a=2), ps[0:NP, 2:4, :])))
                    wait(pe, t_self[-1] if t_self else v0)
                    for k in range(2):
                        m = pe.matmul(ps[0:NP, 4, 0:D], xt[:, u, k, :], self_s[:, k, :], start=(k == 0), stop=(k == 1))
                    wait(vec, M.mark(m))
                    t_self.append(V.mark(vec.tensor_tensor(flat(xb, i * U5 + u), ps[0:NP, 4, 0:D], sb_s[:, :], ALU.add)))
                    wait(sp, t_y[-1])
                    sp.dma_start(y_rows[bass.ds((i * U5 + u) * NP, NP), :, :], ybuf[:, u, :, :]).then_inc(s_y[u], 16)
                stored(s_y, i)
            everyone()

        BODY = {V: GRPS + RING // 2, P: GRPS, passed: GRPS, M: RING // 2, freed[0]: 1, freed[1]: 1}
        with loop(nc, EDGE_STEPS, BODY) as i:
            v0, m0 = V.now(), M.now()
            for g in range(GRPS):
                gather(i, g, y_tab, D, slots["b"][1])
            v_off = pair_offsets(ENG.DVE, slots["b"][2], i, (NT - 1) * AW)
            wait(vec, m0)
            t_hot = [one_hots(i, g, slots["b"][0]) for g in range(GRPS)]
            t_add = {0: v0, 1: v0}
            for g in range(GRPS):
                wait(pe, t_hot[g])
                for q in range(g * GRP // 2, (g + 1) * GRP // 2):
                    gathered(pe, i + EDGE_STEPS, 2 * q, 2 * q + 2)
                    t = sum_pair(q, D + 1, t_add[q % 2])
                    t_add[q % 2] = add_pair(q, v_off[q], D + 1, t)
                freed[g].mark(vec.nop())
        everyone()

        with ExitStack() as moe_ctx:
            def sbm(name, shape, dt=F32):
                return sb(name, shape, dt, moe_ctx)

            mw1_s = sbm("mw1_s", [128, EXP, 2, D])
            mw2_s = sbm("mw2_s", [128, EXP, 2, D])
            mb1_s = sbm("mb1_s", [128, EXP, 2])
            mb2_s = sbm("mb2_s", [EXP, D])
            r_s = sbm("r_s", [EXP, D])
            r_t = sbm("r_t", [128, 2, EXP])
            xn_t = sbm("xn3_t", [128, 2, N])
            hid = sbm("moe_hid", [128, 2, 2, U5 * NP])
            logit, prob, comb = (sbm(n, [NP, NT, EXP]) for n in ("logit", "prob", "comb"))
            over, tie = (acc[:, k * NT * EXP * EXP:(k + 1) * NT * EXP * EXP].rearrange("p (t e f) -> p t e f", t=NT, e=EXP)
                         for k in range(2))
            less = sbm("less", [128, EXP, EXP])
            comb_t = sbm("comb_t", [EXP, U5, NP])
            s1, s2 = (sbm(n, [NP, NT]) for n in ("s1", "s2"))
            for e in range(EXP):
                t_m1 = d_in[11].mark(sp.dma_start(mw1_s[:, e, :, :], matrix(mw1[e])))
                t_m2 = d_in[12].mark(sp.dma_start(mw2_s[:, e, :, :], matrix(mw2[e])))
            d_in[13].mark(sp.dma_start(mb2_s[:, :], mb2))
            d_in[13].mark(sp.dma_start(r_s[:, :], router))
            t_mb = d_in[13].mark(sp.dma_start(mb1_s[:, :, :], mb1.rearrange("e (k p) -> p e k", p=128), allow_slow_non_contiguous=True))
            wait(pool, P.mark(pool.memset(less[:, :, :], 1.0)))
            t_less = P.mark(pool.affine_select(less[:, :, :], less[:, :, :], pattern=[[1, EXP], [-1, EXP]], compare_op=ALU.is_gt,
                                               fill=0.0, base=0, channel_multiplier=0))
            wait(pe, t_mb, t_m1, t_m2)
            wait(pe, V.now(), A.now())
            for k in range(2):
                m = pe.transpose(ps[:, 0, k * EXP:(k + 1) * EXP], r_s[:, k * 128:(k + 1) * 128], ident[0:EXP, 0:EXP])
            wait(act, M.mark(m), V.now())
            t_rt = A.mark(act.copy(r_t[:, :, :], ps[:, 0, 0:2 * EXP].rearrange("p (k e) -> p k e", k=2)))

            V.mark(vec.tensor_scalar(s1[:, :], acc3[:, :, D], 1.0, None, ALU.max))
            wait(vec, V.now())
            V.mark(vec.reciprocal(s2[:, :], s1[:, :]))
            wait(vec, V.now())
            with loop(nc, NODE_STEPS, {V: 3 * U5}) as i:
                t1 = [V.mark(vec.scalar_tensor_tensor(flat(xb, i * U5 + u), acc_cols(i * U5 + u, 0, D), col(s2, i * U5 + u),
                                                      flat(xb, i * U5 + u), ALU.mult, ALU.add)) for u in range(U5)]
                t2 = []
                for u in range(U5):
                    wait(vec, t1[u])
                    t2.append(V.mark(vec.scalar_tensor_tensor(flat(xa, i * U5 + u), flat(xb, i * U5 + u), 0.0,
                                                              flat(xa, i * U5 + u), ALU.max, ALU.add)))
                for u in range(U5):
                    wait(vec, t2[u])
                    V.mark(vec.bn_stats(flat(stats, i * U5 + u), flat(xa, i * U5 + u)))
            t_norm = norm_factors()
            wait(act, t_mb)
            wait(vec, t_less)
            for e in (vec, act, pool, pe):
                wait(e, t_norm, t_rt)
            with loop(nc, NODE_STEPS, {V: U5, M: 2 * U5, A: 2 * U5, P: 2 * U5}) as i:
                a0 = A.now()
                t_xt = norm_body(i, (0, 1), full=xn_t, add_back=True)
                t_l = []
                for u in range(U5):
                    wait(pe, t_xt[u], t_l[u - 2] if u >= 2 else a0)
                    for k in range(2):
                        m = pe.matmul(ps[0:NP, 2 + u % 2, 0:EXP], xt[:, u, k, :], r_t[:, k, :], start=(k == 0), stop=(k == 1))
                    wait(act, M.mark(m))
                    t_l.append(A.mark(act.copy(flat(logit, i * U5 + u), ps[0:NP, 2 + u % 2, 0:EXP])))
            own = lambda: wait(vec, V.now())
            b8 = lambda tile: tile[:, :].unsqueeze(2).to_broadcast([NP, NT, EXP])
            wait(vec, A.now())
            V.mark(vec.tensor_reduce(s1[:, :], logit[:, :, :], AX, ALU.max))
            own()
            wait(act, V.mark(vec.tensor_tensor(logit[:, :, :], logit[:, :, :], b8(s1), ALU.subtract)))
            wait(vec, A.mark(act.activation(prob[:, :, :], logit[:, :, :], ACT.Exp)))
            V.mark(vec.tensor_reduce(s1[:, :], prob[:, :, :], AX, ALU.add))
            own()
            V.mark(vec.reciprocal(s2[:, :], s1[:, :]))
            own()
            V.mark(vec.tensor_tensor(prob[:, :, :], prob[:, :, :], b8(s2), ALU.mult))
            own()
            mine = prob[:, :, :].unsqueeze(3).to_broadcast([NP, NT, EXP, EXP])
            other = prob[:, :, :].unsqueeze(2).to_broadcast([NP, NT, EXP, EXP])
            first = less[0:NP, :, :].rearrange("p e f -> p (e f)").unsqueeze(1).to_broadcast([NP, NT, EXP * EXP])
            pairs = lambda tile: tile[:, :, :, :].rearrange("p t e f -> p t (e f)")
            V.mark(vec.tensor_tensor(over[:, :, :, :], other, mine, ALU.is_gt))
            V.mark(vec.tensor_tensor(tie[:, :, :, :], other, mine, ALU.is_equal))
            own()
            V.mark(vec.tensor_tensor(pairs(tie), pairs(tie), first, ALU.mult))
            own()
            V.mark(vec.tensor_tensor(over[:, :, :, :], over[:, :, :, :], tie[:, :, :, :], ALU.add))
            own()
            V.mark(vec.tensor_reduce(comb[:, :, :], over[:, :, :, :], AX, ALU.add))
            own()
            V.mark(vec.scalar_tensor_tensor(comb[:, :, :], comb[:, :, :], 1.5, prob[:, :, :], ALU.is_lt, ALU.mult))
            own()
            V.mark(vec.tensor_reduce(s1[:, :], comb[:, :, :], AX, ALU.add))
            own()
            V.mark(vec.tensor_scalar(s1[:, :], s1[:, :], 1e-12, None, ALU.max))
            own()
            V.mark(vec.reciprocal(s2[:, :], s1[:, :]))
            own()
            V.mark(vec.tensor_tensor(comb[:, :, :], comb[:, :, :], b8(s2), ALU.mult))
            t_comb = V.now()

            out_rows = out.rearrange("(t p) d -> p t d", p=NP)
            s_out = sem("out_stored")
            wait(pool, t_comb)
            wait(vec, t_comb)
            wait(pe, P.now())
            wait(act, P.now())
            o_buf = xs
            with loop(nc, NODE_STEPS, {V: U5 * (EXP + 1), M: 2 * U5 + EXP * (4 + U5), A: U5 + EXP * 4, P: U5, S: 1}) as i:
                v0, a0, m0, s0, p0 = V.now(), A.now(), M.now(), S.now(), P.now()
                wait(pool, m0)
                t_cb = []
                for u in range(U5):
                    t_cb.append(P.mark(pool.tensor_copy(logit[:, u, :], flat(comb, i * U5 + u))))
                wait(vec, s0)
                last = []
                for u in range(U5):
                    wait(pe, t_cb[u], a0, v0)
                    wait(act, M.mark(pe.transpose(ps[0:EXP, 0, 0:NP], logit[:, u, :], ident[0:NP, 0:NP])))
                    wait(pe, A.mark(act.copy(comb_t[:, u, :], ps[0:EXP, 0, 0:NP])))
                    if u:
                        wait(pe, last[-1])
                    m = pe.matmul(ps[0:NP, 6, 0:D], comb_t[:, u, :], mb2_s[:, :], start=True, stop=True)
                    wait(vec, M.mark(m))
                    last.append(V.mark(vec.tensor_tensor(o_buf[:, u, :], ps[0:NP, 6, 0:D], flat(xa, i * U5 + u), ALU.add)))
                t_g, t_v = [], []
                for e in range(EXP):
                    for c in range(2):
                        for half, (lo, n) in enumerate(SPLIT):
                            b = 2 * c + half
                            wait(pe, t_g[-4] if e else a0)
                            for k in range(2):
                                m = pe.matmul(ps[:, b, 0:n], mw1_s[:, e, k, c * 128:(c + 1) * 128],
                                              xn_t[:, k, bass.ds(i * (U5 * NP) + lo, n)], start=(k == 0), stop=(k == 1))
                            wait(act, M.mark(m))
                            t_g.append(A.mark(act.activation(hid[:, e % 2, c, lo:lo + n], ps[:, b, 0:n], ACT.Gelu,
                                                             bias=mb1_s[:, e, c:c + 1])))
                    wait(pe, t_g[-1])
                    for u in range(U5):
                        b = 4 + len(t_v) % 3
                        wait(pe, t_v[-3] if len(t_v) >= 3 else last[-1])
                        for c in range(2):
                            m = pe.matmul(ps[0:NP, b, 0:D], hid[:, e % 2, c, u * NP:(u + 1) * NP], mw2_s[:, e, c, :],
                                          start=(c == 0), stop=(c == 1))
                        wait(vec, M.mark(m), last[u])
                        t = V.mark(vec.scalar_tensor_tensor(o_buf[:, u, :], ps[0:NP, b, 0:D], comb[:, bass.ds(i * U5 + u, 1), e],
                                                            o_buf[:, u, :], ALU.mult, ALU.add))
                        t_v.append(t)
                        last[u] = t
                wait(sp, last[-1])
                sp.dma_start(out_rows[:, bass.ds(i * U5, U5), :], o_buf[:, :, :]).then_inc(s_out, 16)
                stored([s_out], i)
            everyone()



_INS = ["x", "src", "dst", "edge_type_4", "L0_gnn_W", "L0_gnn_a_l", "L0_gnn_a_r", "L0_ffn_wr", "L0_ffn_br",
        "L0_ffn_w1", "L0_ffn_b1", "L0_ffn_w2", "L0_ffn_b2", "L1_gnn_self_W", "L1_gnn_self_b", "L1_gnn_rel_W",
        "L1_ffn_router_w", "L1_ffn_w1", "L1_ffn_b1", "L1_ffn_w2", "L1_ffn_b2"]


def kernel(**inputs):
    import numpy as _np
    import concourse.bacc as _bacc
    from concourse import mybir as _mybir
    from concourse.bass_utils import run_bass_kernel_spmd as _run

    nc = _bacc.Bacc("TRN2", target_bir_lowering=False, num_devices=1)
    arrays, args = {}, []
    for name in _INS:
        a = _np.ascontiguousarray(inputs[name])
        arrays[f"in_{name}"] = a
        args.append(nc.dram_tensor(f"in_{name}", a.shape, _mybir.dt.from_np(a.dtype), kind="ExternalInput").ap())
    args.append(nc.dram_tensor("out_0", (N, D), F32, kind="ExternalOutput").ap())
    build(nc, *args)
    r = _run(nc, [arrays], core_ids=[0])
    return r.results[0]["out_0"]
```

```python
from contextlib import ExitStack

import concourse.bass as bass
from concourse import mybir

ALU = mybir.AluOpType
ACT = mybir.ActivationFunctionType
AX = mybir.AxisListType.X
F32 = mybir.dt.float32
F16 = mybir.dt.float16
BF16 = mybir.dt.bfloat16
I32 = mybir.dt.int32
U16 = mybir.dt.uint16
ENG = mybir.EngineType
RMAX = bass.bass_isa.ReduceOp.max

N = 3125
E = 53125
D = 256
NP = 125
NT = N // NP
EC = E // NP
HEADS = 4
HD = D // HEADS
REL = 4
HID = 4 * D
EXP = 8
TOPK = 1561
EPS = 1e-5
SLOPE = 0.2

PAIR = 256
PAIRS = (E + NT * (PAIR - 1)) // PAIR
COLS = 2 * PAIRS
SORT_N = 17
SORT_STEPS = EC // SORT_N
GRP = 8
GRPS = 2
RING = GRP * GRPS
EDGE_STEPS = COLS // RING
LEAD = GRP // 2
AW = 260
U5 = 5
NODE_STEPS = NT // U5
SPLIT = ((0, 375), (375, 250))
BIG = 12582912.0
LOW = 2048

assert NT * NP == N and EC * NP == E and SORT_STEPS * SORT_N == EC and EDGE_STEPS * RING == COLS


class Lane:

    CREDIT = 256

    def __init__(self, nc, eng, sem):
        self.nc, self.eng, self.sem = nc, eng, sem
        self.base, self.n, self.per = self.CREDIT, 0, 0
        eng.sem_inc(sem, self.CREDIT)

    def mark(self, ins):
        ins.then_inc(self.sem, 1)
        self.n += 1
        return (self.sem, self.base + self.n)

    def now(self):
        return (self.sem, self.base + self.n)

    def last(self, k):
        return (self.sem, self.base + (k - self.per))


def wait(eng, *tickets):
    for sem, value in tickets:
        eng.wait_ge(sem, value)


def wait_apart(lane, *tickets):
    wait(lane.eng, *tickets)
    lane.eng.sem_inc(lane.sem, 1)
    lane.n += 1


class loop:

    def __init__(self, nc, steps, per):
        self.nc, self.steps, self.per = nc, steps, per

    def __enter__(self):
        self.ctx = self.nc.Fori(0, self.steps)
        i = self.ctx.__enter__()
        self.start = {}
        for lane, k in self.per.items():
            self.start[lane] = lane.base + lane.n
            lane.base, lane.n, lane.per = i * k + self.start[lane], 0, k
        return i

    def __exit__(self, *a):
        if a[0] is None:
            got = [lane.n for lane in self.per]
            want = list(self.per.values())
            assert got == want, f"marks of the body: {got}, stated {want}"
            for lane, k in self.per.items():
                lane.base, lane.n = self.start[lane] + self.steps * k, 0
        return self.ctx.__exit__(*a)


class Dma:

    def __init__(self, sem):
        self.sem, self.total = sem, 0

    def mark(self, ins):
        ins.then_inc(self.sem, 16)
        self.total += 16
        return (self.sem, self.total)


def build(nc, x, src, dst, etype, W, a_l, a_r, wr, br, w1, b1, w2, b2,
          self_W, self_b, rel_W, router, mw1, mb1, mw2, mb2, out):
    with ExitStack() as ctx:
        def sem(name):
            return ctx.enter_context(nc.semaphore(name))

        def sb(name, shape, dt=F32, c=ctx):
            return c.enter_context(nc.sbuf_tensor(name, shape, dt))

        vec, act, pe, pool, sp = nc.vector, nc.scalar, nc.tensor, nc.gpsimd, nc.sync
        V, A, M, P, S = (Lane(nc, e, sem(n)) for e, n in (
            (vec, "vector_done"), (act, "scalar_done"), (pe, "tensor_done"), (pool, "pool_done"), (sp, "stores_done")))

        passed = Lane(nc, pool, sem("pool_passed"))
        ps = ctx.enter_context(nc.psum_tensor("ps", [128, 8, 512], F32))
        h_tab = nc.dram_tensor("h_tab", [N, AW], F32, kind="Internal").ap()
        y_tab = nc.dram_tensor("y_tab", [REL * N, D], F32, kind="Internal").ap()

        ident = sb("ident", [128, 128])
        ones = sb("ones", [128, 128])
        before = sb("before", [128, 128])
        upto = sb("upto", [128, 128])
        lower = sb("lower", [128, 128])
        iota_c = sb("iota_c", [128, COLS], F16)
        iota_r = sb("iota_r", [128, 128], F16)
        iota_n = sb("iota_n", [128, 128])
        zeros_e = sb("zeros_e", [128, EC], F16)
        wait(pool, P.mark(pool.memset(ones[:, :], 1.0)))
        for tile, op, cm in ((ident, ALU.is_equal, -1), (before, ALU.is_gt, -1), (upto, ALU.is_ge, -1), (lower, ALU.is_gt, 1)):
            P.mark(pool.affine_select(tile[:, :], ones[:, :], pattern=[[-cm, 128]], compare_op=op, fill=0.0,
                                      base=0, channel_multiplier=cm))
        for tile, n in ((iota_c, COLS), (iota_r, 128), (iota_n, 128)):
            P.mark(pool.iota(tile[:, :], [[1, n]], base=0, channel_multiplier=0, allow_small_or_imprecise_dtypes=True))
        P.mark(pool.memset(zeros_e[:, :], 0.0))
        t_const = P.now()

        xa = sb("xa", [NP, NT, D])
        acc = sb("acc", [NP, NT * AW])
        acc3 = acc[:, :].rearrange("p (t c) -> p t c", c=AW)
        gath = sb("gath", [128, RING, AW])
        hot = sb("hot", [128, RING, NP])
        at_rows = sb("at_rows", [128, GRPS, GRP], I32)
        stats = sb("stats", [NP, NT, 6])
        mean, var, tmp25, rstd, nmr = (sb(n, [NP, NT]) for n in ("mean", "var", "tmp25", "rstd", "nmr"))
        xs = sb("xs", [NP, U5, D])
        xt = sb("xt", [128, U5, 2, NP])
        slots = {}
        for g in "ab":
            slots[g] = (sb(f"local_{g}", [128, COLS]), sb(f"index_{g}", [128, COLS], I32),
                        sb(f"acc_at_{g}", [1, LEAD + PAIRS], I32), sb(f"hl_at_{g}", [1, LEAD + PAIRS], I32))
        hl_parts = sb("hl_parts", [NP, NT * 3 * HEADS], BF16)
        gmax = sb("gmax", [128, HEADS])

        d_in = [Dma(sem(f"load_{k}")) for k in range(14)]
        keys = {"a": sb("src_i", [NP, EC], I32), "b": sb("dst_i", [NP, EC], I32)}
        type_i = sb("type_i", [NP, EC], I32)
        ev = lambda v: v.rearrange("(p c) -> p c", c=EC)
        t_x = d_in[1].mark(sp.dma_start(xa[:, :, :], x.rearrange("(t p) d -> p t d", p=NP)))
        t_src = d_in[0].mark(sp.dma_start(keys["a"][:, :], ev(src)))
        t_dst = d_in[2].mark(sp.dma_start(keys["b"][:, :], ev(dst)))
        t_typ = d_in[3].mark(sp.dma_start(type_i[:, :], ev(etype)))

        def row_stats(t, src_tile):
            return V.mark(vec.bn_stats(stats[:, t, :], src_tile))

        def norm_factors():
            wait(vec, V.now())
            V.mark(vec.tensor_tensor(mean[:, :], stats[:, :, 1], stats[:, :, 4], ALU.add))
            V.mark(vec.tensor_tensor(tmp25[:, :], stats[:, :, 1], stats[:, :, 4], ALU.subtract))
            V.mark(vec.tensor_tensor(var[:, :], stats[:, :, 2], stats[:, :, 5], ALU.add))
            wait(vec, V.now())
            V.mark(vec.scalar_tensor_tensor(tmp25[:, :], tmp25[:, :], 0.25, tmp25[:, :], ALU.mult, ALU.mult))
            V.mark(vec.tensor_scalar(mean[:, :], mean[:, :], -0.5, None, ALU.mult))
            V.mark(vec.tensor_scalar(var[:, :], var[:, :], 1.0 / D, EPS, ALU.mult, ALU.add))
            wait(vec, V.now())
            wait(act, V.mark(vec.tensor_tensor(var[:, :], var[:, :], tmp25[:, :], ALU.add)))
            wait(vec, A.mark(act.activation(tmp25[:, :], var[:, :], ACT.Sqrt)))
            wait(vec, V.mark(vec.reciprocal(rstd[:, :], tmp25[:, :])))
            return V.mark(vec.tensor_tensor(nmr[:, :], mean[:, :], rstd[:, :], ALU.mult))

        def normalise(t, u):
            return V.mark(vec.tensor_scalar(xs[:, u, :], xa[:, t, :], rstd[:, t], nmr[:, t], ALU.mult, ALU.add))

        def transpose_tile(u, t_xs, bank):
            wait(pe, t_xs)
            for k in range(2):
                t = pe.transpose(ps[:, bank, k * NP:(k + 1) * NP], xs[:, u, k * 128:(k + 1) * 128], ident[0:NP, 0:NP])
            wait(act, M.mark(t))
            return A.mark(act.copy(xt[:, u, :, :], ps[:, bank, 0:2 * NP].rearrange("p (k n) -> p k n", k=2)))

        def col(tile, t):
            return tile[:, bass.ds(t, 1)]

        def stored(sems, i):
            for s in sems:
                sp.wait_ge(s, i * 16 + 16)
            sp.sem_inc(S.sem, 1)
            S.n += 1

        def everyone(*more):
            for lane in (V, A, M, P, S, *more):
                for e in (vec, act, pe, pool, sp):
                    wait(e, lane.now())

        def matrix(m):
            return m.rearrange("(k p) n -> p k n", p=128)

        with ExitStack() as sort_ctx:
            def sbs(name, shape, dt=F32):
                return sb(name, shape, dt, sort_ctx)

            w_cat = sbs("w_cat", [128, 2, 264])
            w_t = sbs("w_t", [128, 2, D])
            a_bd = sbs("a_bd", [128, 2, 8])
            hbuf = sbs("hbuf", [NP, U5, AW])
            hl = sbs("hl", [NP, NT, HEADS])
            hr = sbs("hr", [128, NT, HEADS])
            hl_r = sbs("hl_r", [NP, NT, HEADS])
            gm = sbs("gm", [128, HEADS])
            plan = {g: sbs(f"plan_{g}", [NP, 4, EC]) for g in "ab"}
            cnt = sbs("cnt", [NP, NT])
            offs = sbs("offs", [NP, NT])
            tot = sbs("tot", [NT, 4])
            starts = sbs("starts", [NT, NT])
            reach = sbs("reach", [NT, PAIRS])
            pair_tile = sbs("pair_tile", [1, PAIRS])
            key_f, tile_f, pos, tmp_e, oth_f = (sbs(n, [NP, EC]) for n in ("key_f", "tile_f", "pos", "tmp_e", "oth_f"))
            scratch = sbs("scratch", [NP, NT * EC], F16)
            in_tile = scratch[:, :].rearrange("p (q c) -> p q c", q=NT)
            hi_s = sbs("hi_s", [128, COLS])

            wait(sp, P.mark(pool.memset(a_bd[:, :, :], 0.0)))
            t_pos = P.mark(pool.memset(pos[:, :], 0.0))
            for g in "ab":
                P.mark(pool.memset(slots[g][2][:, 0:LEAD], 0))
                P.mark(pool.memset(slots[g][3][:, 0:LEAD], 0))
            t_acc = P.mark(pool.memset(acc[:, :], 0.0))
            t_w = d_in[4].mark(sp.dma_start(w_cat[:, :, 0:D], matrix(W)))
            for h in range(HEADS):
                for k, a in ((0, a_r), (4, a_l)):
                    t_a = d_in[5].mark(sp.dma_start(a_bd[(h % 2) * HD:(h % 2 + 1) * HD, h // 2, k + h:k + h + 1],
                                                    a[0, h, :].rearrange("(d o) -> d o", o=1)))
            wait(vec, t_x)
            for t in range(NT):
                row_stats(t, xa[:, t, :])
            t_norm = norm_factors()

            wait(pe, t_const, t_w, t_a)
            for k in range(2):
                for j in range(2):
                    m = pe.transpose(ps[:, 0, (2 * k + j) * 128:(2 * k + j + 1) * 128], w_cat[:, k, j * 128:(j + 1) * 128], ident[:, :])
            wait(act, M.mark(m))
            t_wt = A.mark(act.copy(w_t[:, :, :].rearrange("p j (k i) -> p j k i", k=2),
                                   ps[:, 0, :].rearrange("p (k j i) -> p j k i", k=2, j=2)))
            wait(pe, t_wt)
            for k in range(2):
                for j in range(2):
                    m = pe.matmul(ps[:, 1, k * 8:k * 8 + 8], w_t[:, j, k * 128:(k + 1) * 128], a_bd[:, j, :],
                                  start=(j == 0), stop=(j == 1))
            wait(act, M.mark(m))
            t_wc = A.mark(act.copy(w_cat[:, :, D:D + 8], ps[:, 1, 0:16].rearrange("p (k c) -> p k c", k=2)))

            wait(pool, P.mark(pool.memset(hr[:, :, :], -3.0e38)))
            s_tab = [sem(f"h_stored_{u}") for u in range(U5)]
            wait(pe, t_wc)
            for e in (act, vec, pool, pe):
                wait(e, t_norm)
            with loop(nc, NODE_STEPS, {M: 2 * U5, A: 4 * U5, P: U5, S: 1}) as i:
                m0, a0, p0, s0 = M.now(), A.now(), P.now(), S.now()
                wait(act, m0)
                t_xs = [A.mark(act.activation(xs[:, u, :], xa[:, bass.ds(i * U5 + u, 1), :].rearrange("p a d -> p (a d)"),
                                              ACT.Identity, bias=col(nmr, i * U5 + u), scale=col(rstd, i * U5 + u)))
                        for u in range(U5)]
                wait(pe, a0)
                for u in range(U5):
                    bank = u % 2
                    t_xt = transpose_tile(u, t_xs[u], bank)
                    wait(pe, t_xt)
                    for k in range(2):
                        m = pe.matmul(ps[0:NP, 2 + bank, 0:264], xt[:, u, k, :], w_cat[:, k, :], start=(k == 0), stop=(k == 1))
                    if u == 0:
                        wait(act, s0)
                        wait(act, p0)
                    wait(act, M.mark(m))
                    t_h = A.mark(act.copy(hbuf[:, u, :], ps[0:NP, 2 + bank, 0:AW]))
                    t_l = A.mark(act.copy(hl[:, bass.ds(i * U5 + u, 1), :].rearrange("p a d -> p (a d)"), ps[0:NP, 2 + bank, AW:264]))
                    wait(sp, t_h)
                    sp.dma_start(h_tab[bass.ds((i * U5 + u) * NP, NP), :], hbuf[:, u, :]).then_inc(s_tab[u], 16)
                    wait(pool, t_h)
                    P.mark(pool.tensor_copy(hr[0:NP, bass.ds(i * U5 + u, 1), :].rearrange("p a d -> p (a d)"), hbuf[:, u, D:AW]))
                stored(s_tab, i)
            t_hr = P.now()
            wait(pool, S.now())

            def plan_sort(g, t_key, t_oth):
                own = lambda: wait(vec, V.now())
                wait(vec, t_key)
                V.mark(vec.tensor_copy(key_f[:, :], keys[g][:, :]))
                own()
                V.mark(vec.tensor_scalar(tile_f[:, :], key_f[:, :], 1.0 / NP, -(NP - 1) / 2 / NP, ALU.mult, ALU.add))
                own()
                V.mark(vec.tensor_scalar(tile_f[:, :], tile_f[:, :], BIG, BIG, ALU.add, ALU.subtract))
                own()
                for q in range(NT):
                    t = V.mark(vec.tensor_scalar(in_tile[:, q, :], tile_f[:, :], float(q), None, ALU.is_equal, ALU.add,
                                                 accum_out=cnt[:, q:q + 1]))
                wait(pe, t)
                wait(vec, M.mark(pe.matmul(ps[0:NT, 4, 0:1], cnt[:, :], ones[0:NP, 0:1], start=True, stop=True)))
                V.mark(vec.tensor_scalar(tot[:, 0:1], ps[0:NT, 4, 0:1], 1.0 / PAIR, (PAIR - 1) / 2 / PAIR, ALU.mult, ALU.add))
                own()
                V.mark(vec.tensor_scalar(tot[:, 1:2], tot[:, 0:1], BIG, BIG, ALU.add, ALU.subtract))
                own()
                t = V.mark(vec.tensor_scalar(starts[:, :], before[0:NT, 0:NT], tot[:, 1:2], float(PAIR), ALU.mult, ALU.mult))
                wait(pe, t)
                m = pe.matmul(ps[0:NT, 4, 8:9], upto[0:NT, 0:NT], tot[:, 1:2], start=True, stop=True)
                wait(vec, M.mark(m))
                V.mark(vec.tensor_copy(tot[:, 2:3], ps[0:NT, 4, 8:9]))
                pe.matmul(ps[0:NP, 7, 0:NT], before[0:NP, 0:NP], cnt[:, :], start=True, stop=False)
                m = pe.matmul(ps[0:NP, 7, 0:NT], ones[0:NT, 0:NP], starts[:, :], start=False, stop=True)
                wait(vec, M.mark(m))
                V.mark(vec.tensor_scalar(offs[:, :], ps[0:NP, 7, 0:NT], -1.0, None, ALU.add))
                own()
                t = V.mark(vec.tensor_scalar(reach[:, :], iota_c[0:NT, 0:PAIRS], tot[:, 2:3], None, ALU.is_ge))
                wait(pe, t)
                wait(vec, M.mark(pe.matmul(ps[0:1, 4, 0:PAIRS], ones[0:NT, 0:1], reach[:, :], start=True, stop=True)))
                V.mark(vec.tensor_scalar(pair_tile[:, :], ps[0:1, 4, 0:PAIRS], float(NT - 1), None, ALU.min))
                own()
                V.mark(vec.tensor_scalar(slots[g][2][:, LEAD:], pair_tile[:, :], float(AW), None, ALU.mult))
                V.mark(vec.tensor_scalar(slots[g][3][:, LEAD:], pair_tile[:, :], float(3 * HEADS), None, ALU.mult))
                for q in range(NT):
                    buf = ps[0:NP, 5 + q % 2, 0:EC]
                    V.mark(vec.tensor_tensor_scan(buf, in_tile[:, q, :], zeros_e[0:NP, :], offs[:, q:q + 1], ALU.add, ALU.add))
                    own()
                    V.mark(vec.copy_predicated(pos[:, :], in_tile[:, q, :].bitcast(U16), buf))
                own()
                row, column, pay1, pay2 = (plan[g][:, k, :] for k in range(4))
                V.mark(vec.tensor_scalar(tmp_e[:, :], pos[:, :], 1.0 / 128, -63.5 / 128, ALU.mult, ALU.add))
                own()
                V.mark(vec.tensor_scalar(column, tmp_e[:, :], BIG, BIG, ALU.add, ALU.subtract))
                own()
                V.mark(vec.scalar_tensor_tensor(row, column, -128.0, pos[:, :], ALU.mult, ALU.add))
                V.mark(vec.scalar_tensor_tensor(key_f[:, :], tile_f[:, :], -float(NP), key_f[:, :], ALU.mult, ALU.add))
                wait(vec, t_oth)
                V.mark(vec.tensor_scalar(tmp_e[:, :], oth_f[:, :], 1.0 / LOW, -(LOW - 1) / 2 / LOW, ALU.mult, ALU.add))
                own()
                V.mark(vec.tensor_scalar(tmp_e[:, :], tmp_e[:, :], BIG, BIG, ALU.add, ALU.subtract))
                own()
                V.mark(vec.scalar_tensor_tensor(pay2, tmp_e[:, :], -float(LOW), oth_f[:, :], ALU.mult, ALU.add))
                V.mark(vec.scalar_tensor_tensor(pay1, tmp_e[:, :], 128.0, key_f[:, :], ALU.mult, ALU.add))
                own()
                return V.mark(vec.tensor_scalar(pay1, pay1, 1.0, None, ALU.add))

            wait(vec, t_const, t_pos, t_dst)
            t_oth = V.mark(vec.tensor_copy(oth_f[:, :], keys["b"][:, :]))
            t_plan_a = plan_sort("a", t_src, t_oth)
            wait(vec, t_typ)
            V.mark(vec.tensor_copy(tmp_e[:, :], type_i[:, :]))
            V.mark(vec.tensor_copy(key_f[:, :], keys["a"][:, :]))
            wait(vec, V.now())
            t_oth = V.mark(vec.scalar_tensor_tensor(oth_f[:, :], tmp_e[:, :], float(N), key_f[:, :], ALU.mult, ALU.add))
            wait(vec, t_oth)
            t_plan_b = plan_sort("b", t_dst, t_oth)

            hot_c = sbs("hot_c", [NP, SORT_N, COLS], F16)
            hot_r = sbs("hot_r", [NP, SORT_N, 128], F16)
            pay = sbs("pay", [NP, 2, SORT_N, 128], F16)
            stage_v, stage_a, stage_p = (sbs(f"stage_{e}", [NP, 4, SORT_N]) for e in "vap")
            CHUNKS = ((0, 5), (5, 9), (9, 13), (13, 17))
            moved = Lane(nc, pe, sem("columns_moved"))
            weighed = Lane(nc, act, sem("payloads_weighed"))
            PAY_V, PAY_P = 3, 3

            def permute_open():
                wait(pe, t_const)
                for k in range(2):
                    pe.matmul(ps[:, 6 + k, 0:COLS], zeros_e[0:NP, 0:128], iota_c[0:NP, :], start=True, stop=False,
                              skip_group_check=True)

            def permute_close():
                for k in range(2):
                    m = pe.matmul(ps[:, 6 + k, 0:COLS], zeros_e[0:NP, 0:128], iota_c[0:NP, :], start=False, stop=True,
                                  skip_group_check=True)
                return M.mark(m)

            def permute_parts(i, g, by_v, by_p):
                by_a = SORT_N - by_v - by_p
                tick = {}
                at = bass.ds(i * SORT_N, SORT_N)

                def scalars():
                    wait(vec, V.now())
                    tick["stage"] = V.mark(vec.tensor_copy(stage_v[:, :, :], plan[g][:, :, at]))
                    wait(act, weighed.now())
                    wait(act, weighed.mark(act.copy(stage_a[:, 2:4, :], plan[g][:, 2:4, at])))
                    if by_p:
                        wait(pool, P.now())
                        wait_apart(passed, P.mark(pool.tensor_copy(stage_p[:, :, :], plan[g][:, :, at])), moved.last(len(CHUNKS)))
                        for j in range(by_a + by_v, SORT_N):
                            for k in range(2):
                                tp = P.mark(pool.tensor_scalar(pay[:, k, j, :], iota_r[0:NP, :], stage_p[:, 0, j:j + 1],
                                                               stage_p[:, 2 + k, j:j + 1], ALU.is_equal, ALU.mult))
                            tick["p", j] = tp

                def on_v(c):
                    lo, hi = CHUNKS[c]
                    wait(vec, tick["stage"])
                    n = min(hi, by_a) - lo
                    if n > 0:
                        wait(vec, weighed.last(2 + c))
                        tick["rows", c] = V.mark(vec.tensor_tensor(
                            hot_r[:, lo:lo + n, :], iota_r[0:NP, :].unsqueeze(1).to_broadcast([NP, n, 128]),
                            stage_v[:, 0, lo:lo + n].unsqueeze(2).to_broadcast([NP, n, 128]), ALU.is_equal))
                    wait(vec, moved.last(c + 1))
                    for j in range(lo, hi):
                        t = vec.tensor_scalar(hot_c[:, j, :], iota_c[0:NP, :], stage_v[:, 1, j:j + 1], None, ALU.is_equal)
                        if by_a <= j < by_a + by_v:
                            for k in range(2):
                                t = vec.tensor_scalar(pay[:, k, j, :], iota_r[0:NP, :], stage_v[:, 0, j:j + 1],
                                                      stage_v[:, 2 + k, j:j + 1], ALU.is_equal, ALU.mult)
                    tick["v", c] = V.mark(t)

                def on_a(c):
                    lo, hi = CHUNKS[c]
                    if lo < by_a:
                        wait(act, tick["rows", c], moved.last(c + 1))
                        for j in range(lo, min(hi, by_a)):
                            for k in range(2):
                                t = act.mul(pay[:, k, j, :], hot_r[:, j, :], stage_a[:, 2 + k, j:j + 1])
                        tick["a", c] = weighed.mark(t)

                def on_pe(c):
                    lo, hi = CHUNKS[c]
                    wait(pe, tick["v", c])
                    if ("a", c) in tick:
                        wait(pe, tick["a", c])
                    for j in range(lo, hi):
                        if ("p", j) in tick:
                            wait(pe, tick["p", j])
                        for k in range(2):
                            m = pe.matmul(ps[:, 6 + k, 0:COLS], pay[:, k, j, :], hot_c[:, j, :], start=False, stop=False,
                                          skip_group_check=True)
                    moved.mark(m)

                return scalars, on_v, on_a, on_pe

            def unpack(g, t_moved):
                local, index = slots[g][0], slots[g][1]
                wait(vec, t_moved, V.now())
                V.mark(vec.tensor_scalar(hi_s[:, :], ps[:, 6, 0:COLS], 1.0 / 128, -(NP / 2) / 128, ALU.mult, ALU.add))
                wait(vec, V.now())
                V.mark(vec.tensor_scalar(hi_s[:, :], hi_s[:, :], BIG, BIG, ALU.add, ALU.subtract))
                wait(vec, V.now())
                V.mark(vec.scalar_tensor_tensor(index[:, :], hi_s[:, :], float(LOW), ps[:, 7, 0:COLS], ALU.mult, ALU.add))
                V.mark(vec.scalar_tensor_tensor(local[:, :], hi_s[:, :], -128.0, ps[:, 6, 0:COLS], ALU.mult, ALU.add))
                wait(vec, V.now())
                return V.mark(vec.tensor_scalar(local[:, :], local[:, :], -1.0, None, ALU.add))

            wait(pe, A.now(), V.now())
            permute_open()
            wait(act, t_plan_a)
            wait(pool, t_plan_a)
            with loop(nc, SORT_STEPS, {V: 1 + 3 + len(CHUNKS), P: 1 + 2 * PAY_P, passed: 1, moved: len(CHUNKS), weighed: 1 + 3}) as i:
                scalars, on_v, on_a, on_pe = permute_parts(i, "a", PAY_V, PAY_P)
                scalars()
                for c in range(len(CHUNKS)):
                    on_v(c)
                    on_a(c)
                    on_pe(c)
            t_slots_a = unpack("a", permute_close())

            parts = hl_parts[:, :].rearrange("p (t h c) -> p t h c", t=NT, h=HEADS)
            wait(vec, A.now())
            wait(vec, V.mark(vec.tensor_copy(parts[:, :, :, 0], hl[:, :, :])))
            wait(vec, V.mark(vec.tensor_tensor(hl_r[:, :, :], hl[:, :, :], parts[:, :, :, 0], ALU.subtract)))
            wait(vec, V.mark(vec.tensor_copy(parts[:, :, :, 1], hl_r[:, :, :])))
            wait(vec, V.mark(vec.tensor_tensor(hl_r[:, :, :], hl_r[:, :, :], parts[:, :, :, 1], ALU.subtract)))
            t_parts = V.mark(vec.tensor_copy(parts[:, :, :, 2], hl_r[:, :, :]))
            wait(vec, t_hr)
            t = V.mark(vec.tensor_reduce(gm[:, :], hr[:, :, :].rearrange("p t h -> p h t"), AX, ALU.max))
            wait(pool, t)
            t_gmax = P.mark(pool.partition_all_reduce(gmax[:, :], gm[:, :], 128, RMAX))

            s_gath = [sem(f"gathered_{k}") for k in range(RING)]
            summed = Lane(nc, pe, sem("pairs_summed"))
            added = Lane(nc, vec, sem("pairs_added"))
            copied = Lane(nc, act, sem("transposes_copied"))
            picked_read = Lane(nc, vec, sem("picks_read"))
            hot_t = sbs("hot_t", [NP, GRPS, GRP, 128], BF16)
            hle = sbs("hle", [128, GRPS, GRP * HEADS])
            score = sbs("score", [128, GRPS, 2, GRP * HEADS])
            expo = sbs("expo", [128, GRPS, GRP * HEADS])
            hl_bc = gmax[:, :].unsqueeze(1).to_broadcast([128, GRP, HEADS])

            def gather(i, g, table, width, idx, t_used):
                wait(pool, t_used[0])
                wait_apart(passed, P.mark(pool.tensor_copy(at_rows[:, g, :], idx[:, bass.ds(i * RING + g * GRP, GRP)])))
                gather_rows(g, table, width, 0, GRP // 2)
                wait_apart(passed, t_used[1])
                gather_rows(g, table, width, GRP // 2, GRP)

            def gather_rows(g, table, width, lo=0, hi=GRP):
                for s in range(g * GRP + lo, g * GRP + hi):
                    pool.indirect_dma_start(gath[:, s, 0:width], None, table,
                                            bass.IndirectOffsetOnAxis(ap=at_rows[:, g, s % GRP:s % GRP + 1], axis=0)
                                            ).then_inc(s_gath[s], 16)

            def gathered(eng, turn, lo, hi):
                for s in range(lo, hi):
                    eng.wait_ge(s_gath[s], turn * 16 + 16)

            def one_hots(i, g, local, t_used):
                at = local[:, bass.ds(i * RING + g * GRP, GRP)]
                wait(vec, t_used)
                return V.mark(vec.tensor_tensor(hot[:, g * GRP:(g + 1) * GRP, :], iota_n[:, 0:NP].unsqueeze(1).to_broadcast([128, GRP, NP]),
                                                at.unsqueeze(2).to_broadcast([128, GRP, NP]), ALU.is_equal))

            def pair_offsets(engine, table, at, top, n=RING // 2):
                return nc.values_load_multi_w_load_instructions(
                    table[0:1, bass.ds(at, n)], engines=[engine], min_val=0, max_val=top,
                    skip_runtime_bounds_check_because="the tile is the minimum of a count and NT - 1")[1]

            def sum_pair(q, width, t_emptied):
                wait(pe, t_emptied)
                for s in (2 * q, 2 * q + 1):
                    m = pe.matmul(ps[0:NP, 4 + q % 2, 0:width], hot[:, s, :], gath[:, s, 0:width], start=(s == 2 * q), stop=(s == 2 * q + 1))
                return summed.mark(m)

            def add_pair(q, offset, width, t_sum):
                wait(vec, t_sum, added.now())
                at = acc[:, bass.ds(offset, width)]
                return added.mark(vec.tensor_tensor(at, at, ps[0:NP, 4 + q % 2, 0:width], ALU.add))

            def transpose_hot(g, t_hot, t_free):
                wait(pe, t_hot)
                t = []
                for half in range(2):
                    wait(pe, t_free[half])
                    for s in range(4):
                        m = pe.transpose(ps[0:NP, half, s * 128:(s + 1) * 128], hot[:, g * GRP + half * 4 + s, :], ident[:, :])
                    wait(act, M.mark(m))
                    t.append(copied.mark(act.copy(hot_t[:, g, half * 4:half * 4 + 4, :],
                                                  ps[0:NP, half, :].rearrange("p (s e) -> p s e", s=4))))
                return t

            def pick_hl(g, offsets, t_copied, t_read):
                wait(pe, t_read, *t_copied)
                for s in range(GRP):
                    m = pe.matmul(ps[:, 2 + g, s * 12:s * 12 + 12], hot_t[:, g, s, :],
                                  hl_parts[:, bass.ds(offsets[s // 2], 12)], start=True, stop=True)
                return M.mark(m)

            def weights(g, turn, t_pick):
                lo, hi = g * GRP, (g + 1) * GRP
                three = lambda tile: tile.rearrange("p (s h) -> p s h", h=HEADS)
                wait(vec, t_pick, V.now())
                wait(vec, picked_read.mark(vec.tensor_reduce(hle[:, g, :], ps[:, 2 + g, 0:GRP * 12].rearrange("p (s c) -> p s c", c=3), AX, ALU.add)))
                V.mark(vec.tensor_tensor(three(score[:, g, 1, :]), three(hle[:, g, :]), hl_bc, ALU.add))
                gathered(vec, turn, lo, hi)
                V.mark(vec.tensor_tensor(three(score[:, g, 0, :]), three(hle[:, g, :]), gath[:, lo:hi, D:AW], ALU.add))
                wait(vec, V.now())
                V.mark(vec.scalar_tensor_tensor(score[:, g, :, :], score[:, g, :, :], SLOPE, score[:, g, :, :], ALU.mult, ALU.max))
                wait(vec, V.now())
                wait(act, V.mark(vec.tensor_tensor(expo[:, g, :], score[:, g, 0, :], score[:, g, 1, :], ALU.subtract)))
                return A.mark(act.activation(gath[:, lo:hi, D:AW], three(expo[:, g, :]), ACT.Exp))

            def weigh(g, t_w):
                wait(vec, t_w)
                t = []
                for a in (g * GRP, g * GRP + 4):
                    rows = gath[:, a:a + 4, 0:D].rearrange("p s (h d) -> p s h d", h=HEADS)
                    t.append(V.mark(vec.tensor_tensor(rows, rows, gath[:, a:a + 4, D:AW].unsqueeze(3).to_broadcast([128, 4, HEADS, HD]), ALU.mult)))
                return t

            def two_sums(g, half, t_rows, t_added):
                wait(pe, t_rows[half])
                q = (g * GRP + 4 * half) // 2
                return [sum_pair(q + k, AW, t_added[k]) for k in range(2)]

            def two_adds(g, half, offsets, t_sums):
                q = (g * GRP + 4 * half) // 2
                return [add_pair(q + k, offsets[2 * half + k], AW, t_sums[k]) for k in range(2)]

            def attention_body(i, with_sort):
                HALF = RING // 4
                m0 = M.now()
                gather(i, 0, h_tab, AW, slots["a"][1], [summed.last(2 * HALF - 2), summed.last(2 * HALF)])
                v_off = pair_offsets(ENG.DVE, slots["a"][2], i * (RING // 2), (NT - 1) * AW)
                p_off = pair_offsets(ENG.PE, slots["a"][3], i * (RING // 2) + LEAD, (NT - 1) * 3 * HEADS)
                if with_sort:
                    scalars, on_v, on_a, on_pe = permute_parts(i, "b", 0, 0)
                    scalars()
                t_added = [added.last(2 * HALF - 1), added.last(2 * HALF)]
                t_read = [picked_read.last(2), None]
                t_free = [copied.last(3), copied.last(4)]
                t_pick = {1: m0}
                for n, (late, early) in enumerate(((1, 0), (0, 1))):
                    t_w = weights(late, i, t_pick[late])
                    if n == 0:
                        t_read[1] = picked_read.now()
                        t_hot = one_hots(i, early, slots["a"][0], summed.last(2 * HALF))
                    else:
                        t_hot = one_hots(i, early, slots["a"][0], t_used)
                    t_free = transpose_hot(early, t_hot, t_free)
                    t_rows = weigh(late, t_w)
                    off = v_off[n * HALF:(n + 1) * HALF]
                    t_sums = two_sums(late, 0, t_rows, t_added)
                    t_half = t_sums[-1]
                    t_pick[early] = pick_hl(early, p_off[early * HALF:(early + 1) * HALF], t_free, t_read[early])
                    if with_sort:
                        on_v(2 * n)
                        on_a(2 * n)
                    t_added = two_adds(late, 0, off, t_sums)
                    t_sums = two_sums(late, 1, t_rows, t_added)
                    if with_sort:
                        on_pe(2 * n)
                        on_v(2 * n + 1)
                        on_a(2 * n + 1)
                    t_added = two_adds(late, 1, off, t_sums)
                    if with_sort:
                        on_pe(2 * n + 1)
                    if n == 0:
                        t_used = t_sums[-1]
                        gather(i, 1, h_tab, AW, slots["a"][1], [t_half, t_used])

            for e in (act, pe, pool, vec):
                wait(e, t_slots_a, t_plan_b, t_parts, t_gmax, P.now(), t_acc)
            V.mark(vec.memset(hot[:, GRP:, :], 0.0))
            wait(pool, P.mark(pool.memset(at_rows[:, 1, :], 0)))
            gather_rows(1, h_tab, AW)
            M.mark(pe.matmul(ps[:, 3, 0:GRP * 12], zeros_e[0:NP, 0:128], zeros_e[0:NP, 0:GRP * 12], start=True, stop=True))
            permute_open()
            wait(pe, V.now())
            SORT_MARKS = {moved: len(CHUNKS), weighed: 1 + len(CHUNKS)}
            BODY = {V: 2 * 7, P: GRPS, passed: 2 * GRPS, M: 6, A: 2, copied: 4, picked_read: 2, summed: 8, added: 8}
            with loop(nc, SORT_STEPS, {**BODY, **SORT_MARKS, V: BODY[V] + 1 + 2 * len(CHUNKS)}) as i:
                attention_body(i, True)
            t_slots_b = unpack("b", permute_close())
            with loop(nc, EDGE_STEPS - SORT_STEPS, BODY) as i:
                attention_body(i + SORT_STEPS, False)
            last_off = pair_offsets(ENG.DVE, slots["a"][2], PAIRS, (NT - 1) * AW, LEAD)
            t_rows = weigh(1, weights(1, EDGE_STEPS, M.now()))
            t_added = [added.now(), added.now()]
            for half in range(2):
                t_added = two_adds(1, half, last_off, two_sums(1, half, t_rows, t_added))

            everyone(added)

        flat = lambda tile, t: tile[:, bass.ds(t, 1), :].rearrange("p a d -> p (a d)")
        acc_cols = lambda t, c, n: acc[:, bass.ds(t * AW + c, n)]

        def norm_body(i, banks, full=None, add_back=False, after=()):
            m0, a0, p0 = M.now(), A.now(), P.now()
            wait(vec, m0, p0, a0)
            t_xs = [V.mark(vec.tensor_scalar(xs[:, u, :], flat(xa, i * U5 + u), col(rstd, i * U5 + u), col(nmr, i * U5 + u),
                                             ALU.mult, ALU.add)) for u in range(U5)]
            wait(act, m0, p0)
            t_xt = []
            for u in range(U5):
                wait(pe, t_xt[u - len(banks)] if u >= len(banks) else a0)
                t_xt.append(transpose_tile(u, t_xs[u], banks[u % len(banks)]))
                if add_back:
                    wait(pool, t_xs[u])
                    P.mark(pool.tensor_tensor(flat(xa, i * U5 + u), flat(xa, i * U5 + u), xs[:, u, :], ALU.add))
                if full is not None:
                    wait(pool, t_xt[u])
                    P.mark(pool.tensor_copy(full[:, :, bass.ds((i * U5 + u) * NP, NP)], xt[:, u, :, :]))
            return t_xt

        def row_bcast(tile, row, load, k):
            return load.mark(sp.dma_start(tile, row.rearrange("(o d) -> o d", o=1).to_broadcast([k, row.shape[0]])))

        with ExitStack() as ffn_ctx:
            def sbf(name, shape, dt=F32):
                return sb(name, shape, dt, ffn_ctx)

            xn_t = sbf("xn_t", [128, 2, N])
            hid = sbf("hid", [128, HID // 128, U5 * NP])
            w1_s = sbf("w1_s", [128, 2, HID])
            w2_s = sbf("w2_s", [128, HID // 128, D])
            b1_s = sbf("b1_s", [128, HID // 128])
            b2_s = sbf("b2_s", [1, D])
            wr_s = sbf("wr_s", [128, 2])
            br_s = sbf("br_s", [1, 1])
            w_row = sbf("w_row", [1, N])
            w_all = sbf("w_all", [128, N])
            w_col = sbf("w_col", [NP, NT])
            above = sbf("above", [NP, NT, 3])
            junk = sbf("junk", [NP, N], BF16)
            same = sbf("same", [NP, NP])
            gate = sbf("gate", [NP, NT])
            dinv = sbf("dinv", [NP, NT, HEADS])
            t_w1 = d_in[6].mark(sp.dma_start(w1_s[:, :, :], matrix(w1)))
            d_in[7].mark(sp.dma_start(w2_s[:, :, :], matrix(w2)))
            t_w2 = d_in[7].mark(sp.dma_start(b1_s[:, :], b1.rearrange("(k p) -> p k", p=128), allow_slow_non_contiguous=True))
            d_in[8].mark(sp.dma_start(b2_s[:, :], b2.rearrange("(o d) -> o d", o=1)))
            d_in[8].mark(sp.dma_start(wr_s[:, :], wr.rearrange("(k p) o -> p (k o)", p=128), allow_slow_non_contiguous=True))
            t_wr = d_in[8].mark(sp.dma_start(br_s[:, :], br.rearrange("(o d) -> o d", o=1)))

            V.mark(vec.tensor_scalar(dinv[:, :, :], acc3[:, :, D:AW], 1e-38, None, ALU.max))
            wait(vec, V.now())
            V.mark(vec.reciprocal(dinv[:, :, :], dinv[:, :, :]))
            wait(vec, V.now())
            for i in range(NODE_STEPS):
                at = slice(i * U5, (i + 1) * U5)
                rows = acc3[:, at, 0:D].rearrange("p t (h d) -> p t h d", h=HEADS)
                wait(vec, V.mark(vec.tensor_tensor(rows, rows, dinv[:, at, :].unsqueeze(3).to_broadcast([NP, U5, HEADS, HD]), ALU.mult)))
                wait(vec, V.mark(vec.tensor_tensor(xa[:, at, :], xa[:, at, :], acc3[:, at, 0:D], ALU.add)))
                for t in range(i * U5, (i + 1) * U5):
                    row_stats(t, xa[:, t, :])
            t_norm = norm_factors()
            for e in (vec, act, pool, pe):
                wait(e, t_norm, t_wr, t_w1, t_w2)
            with loop(nc, NODE_STEPS, {V: U5, M: U5, A: U5, P: 2 * U5}) as i:
                norm_body(i, (0, 1), full=xn_t, add_back=True)

            wait(pe, P.now(), A.now())
            for c in range(10):
                n = 313 if c % 2 == 0 else 312
                lo = c // 2 * 625 + c % 2 * 313
                if c >= 2:
                    wait(pe, t_c[c - 2])
                else:
                    t_c = []
                for k in range(2):
                    m = pe.matmul(ps[0:1, c % 2, 0:n], wr_s[:, k:k + 1], xn_t[:, k, lo:lo + n], start=(k == 0), stop=(k == 1))
                wait(act, M.mark(m))
                t_c.append(A.mark(act.activation(w_row[:, lo:lo + n], ps[0:1, c % 2, 0:n], ACT.Identity, bias=br_s[:, 0:1])))
            wait(pe, t_c[-1])
            wait(pool, t_c[-1])
            t_all = P.mark(pool.partition_broadcast(w_all[:, :], w_row[0:1, :], 128))
            for t in range(NT):
                m = pe.transpose(ps[0:NP, 0, t:t + 1], w_row[0:1, t * NP:(t + 1) * NP], ident[0:1, 0:1])
            wait(act, M.mark(m))
            t_col = A.mark(act.copy(w_col[:, :], ps[0:NP, 0, 0:NT]))

            wait(pe, t_col)
            with loop(nc, NODE_STEPS, {M: 16 + U5, A: 16 + U5}) as i:
                a0 = A.now()
                t_g = []
                for c in range(HID // 128):
                    for half, (lo, n) in enumerate(SPLIT):
                        b = (2 * c + half) % 4
                        wait(pe, t_g[-4] if len(t_g) >= 4 else a0)
                        for k in range(2):
                            m = pe.matmul(ps[:, b, 0:n], w1_s[:, k, c * 128:(c + 1) * 128],
                                          xn_t[:, k, bass.ds(i * (U5 * NP) + lo, n)], start=(k == 0), stop=(k == 1))
                        wait(act, M.mark(m))
                        t_g.append(A.mark(act.activation(hid[:, c, lo:lo + n], ps[:, b, 0:n], ACT.Gelu_apprx_tanh,
                                                         bias=b1_s[:, c:c + 1])))
                wait(pe, t_g[-1])
                t_y = []
                for u in range(U5):
                    b = 4 + u % 2
                    if u >= 2:
                        wait(pe, t_y[u - 2])
                    for c in range(HID // 128):
                        pe.matmul(ps[0:NP, b, 0:D], hid[:, c, u * NP:(u + 1) * NP], w2_s[:, c, :], start=(c == 0), stop=False)
                    m = pe.matmul(ps[0:NP, b, 0:D], ones[0:1, 0:NP], b2_s[0:1, :], start=False, stop=True)
                    wait(act, M.mark(m))
                    t_y.append(A.mark(act.copy(acc_cols(i * U5 + u, 0, D), ps[0:NP, b, 0:D])))
            wait(vec, t_all, t_col)
            for t in range(NT):
                lo, hi = t * NP, (t + 1) * NP
                w = w_col[:, t:t + 1]
                if t:
                    V.mark(vec.tensor_scalar(junk[:, 0:lo], w_all[0:NP, 0:lo], w, None, ALU.is_ge, ALU.add, accum_out=above[:, t, 0:1]))
                else:
                    V.mark(vec.memset(above[:, 0, 0:1], 0.0))
                V.mark(vec.tensor_scalar(junk[:, lo:], w_all[0:NP, lo:], w, None, ALU.is_gt, ALU.add, accum_out=above[:, t, 1:2]))
                wait(vec, V.now())
                V.mark(vec.scalar_tensor_tensor(same[:, :], w_all[0:NP, lo:hi], w, lower[0:NP, 0:NP], ALU.is_equal, ALU.mult,
                                                accum_out=above[:, t, 2:3]))
                wait(vec, V.now())
            V.mark(vec.tensor_reduce(gate[:, :], above[:, :, :], AX, ALU.add))
            wait(vec, V.now())
            V.mark(vec.scalar_tensor_tensor(gate[:, :], gate[:, :], TOPK - 0.5, w_col[:, :], ALU.is_lt, ALU.mult))
            wait(vec, V.now(), A.now())
            with loop(nc, NODE_STEPS, {V: 2 * U5}) as i:
                t_x = [V.mark(vec.scalar_tensor_tensor(flat(xa, i * U5 + u), acc_cols(i * U5 + u, 0, D), col(gate, i * U5 + u),
                                                       flat(xa, i * U5 + u), ALU.mult, ALU.add)) for u in range(U5)]
                for u in range(U5):
                    wait(vec, t_x[u])
                    V.mark(vec.bn_stats(flat(stats, i * U5 + u), flat(xa, i * U5 + u)))
            everyone()

        xb = sb("xb", [NP, NT, D])

        with ExitStack() as tab_ctx:
            def sbt(name, shape, dt=F32):
                return sb(name, shape, dt, tab_ctx)

            rel_s = sbt("rel_s", [128, 2, REL, D])
            self_s = sbt("self_s", [128, 2, D])
            sb_s = sbt("sb_s", [NP, D])
            ybuf = sbt("ybuf", [NP, U5, REL, D])
            t_rel = d_in[9].mark(sp.dma_start(self_s[:, :, :], matrix(self_W)))
            for r in range(REL):
                t_rel = d_in[9].mark(sp.dma_start(rel_s[:, :, r, :], matrix(rel_W[r])))
            t_sb = row_bcast(sb_s[:, :], self_b, d_in[10], NP)
            t_acc = P.mark(pool.memset(acc[:, :], 0.0))
            t_one = P.mark(pool.memset(gath[:, :, D:AW], 1.0))
            t_norm = norm_factors()
            wait(vec, t_sb)
            for e in (vec, act, pool, pe):
                wait(e, t_norm, t_rel)
            y_rows = y_tab.rearrange("(r n) d -> n r d", r=REL)
            s_y = [sem(f"y_stored_{u}") for u in range(U5)]
            with loop(nc, NODE_STEPS, {V: 2 * U5, M: 3 * U5, A: 2 * U5, S: 1}) as i:
                v0, s0, a0 = V.now(), S.now(), A.now()
                t_xt = norm_body(i, (0, 1))
                t_y, t_self = [], []
                wait(act, s0)
                for u in range(U5):
                    wait(pe, t_xt[-1], t_y[-1] if t_y else a0)
                    for half in range(2):
                        for k in range(2):
                            m = pe.matmul(ps[0:NP, 2 + half, :], xt[:, u, k, :], rel_s[:, k, 2 * half:2 * half + 2, :].rearrange("p r d -> p (r d)"),
                                          start=(k == 0), stop=(k == 1))
                    wait(act, M.mark(m))
                    t_y.append(A.mark(act.copy(ybuf[:, u, :, :].rearrange("p (a r) d -> p a (r d)", a=2), ps[0:NP, 2:4, :])))
                    wait(pe, t_self[-1] if t_self else v0)
                    for k in range(2):
                        m = pe.matmul(ps[0:NP, 4, 0:D], xt[:, u, k, :], self_s[:, k, :], start=(k == 0), stop=(k == 1))
                    wait(vec, M.mark(m))
                    t_self.append(V.mark(vec.tensor_tensor(flat(xb, i * U5 + u), ps[0:NP, 4, 0:D], sb_s[:, :], ALU.add)))
                    wait(sp, t_y[-1])
                    sp.dma_start(y_rows[bass.ds((i * U5 + u) * NP, NP), :, :], ybuf[:, u, :, :]).then_inc(s_y[u], 16)
                stored(s_y, i)
            everyone()

        with loop(nc, EDGE_STEPS, {V: GRPS, added: 8, P: GRPS, passed: 2 * GRPS, summed: 8}) as i:
            used = [summed.last(4), summed.last(8)]
            for g in range(GRPS):
                gather(i, g, y_tab, D, slots["b"][1], [used[g], used[g]])
            v_off = pair_offsets(ENG.DVE, slots["b"][2], i * (RING // 2) + LEAD, (NT - 1) * AW)
            t_hot = [one_hots(i, g, slots["b"][0], used[g]) for g in range(GRPS)]
            t_add = [added.last(7), added.last(8)]
            for g in range(GRPS):
                wait(pe, t_hot[g])
                for q in range(g * GRP // 2, (g + 1) * GRP // 2):
                    gathered(pe, i + EDGE_STEPS + g, 2 * q, 2 * q + 2)
                    t = sum_pair(q, D + 1, t_add[q % 2])
                    t_add[q % 2] = add_pair(q, v_off[q], D + 1, t)
        everyone(added)

        with ExitStack() as moe_ctx:
            def sbm(name, shape, dt=F32):
                return sb(name, shape, dt, moe_ctx)

            mw1_s = sbm("mw1_s", [128, EXP, 2, D])
            mw2_s = sbm("mw2_s", [128, EXP, 2, D])
            mb1_s = sbm("mb1_s", [128, EXP, 2])
            mb2_s = sbm("mb2_s", [EXP, D])
            r_s = sbm("r_s", [EXP, D])
            r_t = sbm("r_t", [128, 2, EXP])
            xn_t = sbm("xn3_t", [128, 2, N])
            hid = sbm("moe_hid", [128, 2, 2, U5 * NP])
            logit, prob, comb = (sbm(n, [NP, NT, EXP]) for n in ("logit", "prob", "comb"))
            over, tie = (acc[:, k * NT * EXP * EXP:(k + 1) * NT * EXP * EXP].rearrange("p (t e f) -> p t e f", t=NT, e=EXP)
                         for k in range(2))
            less = sbm("less", [128, EXP, EXP])
            comb_t = sbm("comb_t", [EXP, U5, NP])
            s1, s2 = (sbm(n, [NP, NT]) for n in ("s1", "s2"))
            for e in range(EXP):
                t_m1 = d_in[11].mark(sp.dma_start(mw1_s[:, e, :, :], matrix(mw1[e])))
                t_m2 = d_in[12].mark(sp.dma_start(mw2_s[:, e, :, :], matrix(mw2[e])))
            d_in[13].mark(sp.dma_start(mb2_s[:, :], mb2))
            d_in[13].mark(sp.dma_start(r_s[:, :], router))
            t_mb = d_in[13].mark(sp.dma_start(mb1_s[:, :, :], mb1.rearrange("e (k p) -> p e k", p=128), allow_slow_non_contiguous=True))
            wait(pool, P.mark(pool.memset(less[:, :, :], 1.0)))
            t_less = P.mark(pool.affine_select(less[:, :, :], less[:, :, :], pattern=[[1, EXP], [-1, EXP]], compare_op=ALU.is_gt,
                                               fill=0.0, base=0, channel_multiplier=0))
            wait(pe, t_mb, t_m1, t_m2)
            wait(pe, V.now(), A.now())
            for k in range(2):
                m = pe.transpose(ps[:, 0, k * EXP:(k + 1) * EXP], r_s[:, k * 128:(k + 1) * 128], ident[0:EXP, 0:EXP])
            wait(act, M.mark(m), V.now())
            t_rt = A.mark(act.copy(r_t[:, :, :], ps[:, 0, 0:2 * EXP].rearrange("p (k e) -> p k e", k=2)))

            V.mark(vec.tensor_scalar(s1[:, :], acc3[:, :, D], 1.0, None, ALU.max))
            wait(vec, V.now())
            V.mark(vec.reciprocal(s2[:, :], s1[:, :]))
            wait(vec, V.now())
            with loop(nc, NODE_STEPS, {V: 3 * U5}) as i:
                t1 = [V.mark(vec.scalar_tensor_tensor(flat(xb, i * U5 + u), acc_cols(i * U5 + u, 0, D), col(s2, i * U5 + u),
                                                      flat(xb, i * U5 + u), ALU.mult, ALU.add)) for u in range(U5)]
                t2 = []
                for u in range(U5):
                    wait(vec, t1[u])
                    t2.append(V.mark(vec.scalar_tensor_tensor(flat(xa, i * U5 + u), flat(xb, i * U5 + u), 0.0,
                                                              flat(xa, i * U5 + u), ALU.max, ALU.add)))
                for u in range(U5):
                    wait(vec, t2[u])
                    V.mark(vec.bn_stats(flat(stats, i * U5 + u), flat(xa, i * U5 + u)))
            t_norm = norm_factors()
            wait(act, t_mb)
            wait(vec, t_less)
            for e in (vec, act, pool, pe):
                wait(e, t_norm, t_rt)
            with loop(nc, NODE_STEPS, {V: U5, M: 2 * U5, A: 2 * U5, P: 2 * U5}) as i:
                a0 = A.now()
                t_xt = norm_body(i, (0, 1), full=xn_t, add_back=True)
                t_l = []
                for u in range(U5):
                    wait(pe, t_xt[u], t_l[u - 2] if u >= 2 else a0)
                    for k in range(2):
                        m = pe.matmul(ps[0:NP, 2 + u % 2, 0:EXP], xt[:, u, k, :], r_t[:, k, :], start=(k == 0), stop=(k == 1))
                    wait(act, M.mark(m))
                    t_l.append(A.mark(act.copy(flat(logit, i * U5 + u), ps[0:NP, 2 + u % 2, 0:EXP])))
            own = lambda: wait(vec, V.now())
            b8 = lambda tile: tile[:, :].unsqueeze(2).to_broadcast([NP, NT, EXP])
            wait(vec, A.now())
            V.mark(vec.tensor_reduce(s1[:, :], logit[:, :, :], AX, ALU.max))
            own()
            wait(act, V.mark(vec.tensor_tensor(logit[:, :, :], logit[:, :, :], b8(s1), ALU.subtract)))
            wait(vec, A.mark(act.activation(prob[:, :, :], logit[:, :, :], ACT.Exp)))
            V.mark(vec.tensor_reduce(s1[:, :], prob[:, :, :], AX, ALU.add))
            own()
            V.mark(vec.reciprocal(s2[:, :], s1[:, :]))
            own()
            V.mark(vec.tensor_tensor(prob[:, :, :], prob[:, :, :], b8(s2), ALU.mult))
            own()
            mine = prob[:, :, :].unsqueeze(3).to_broadcast([NP, NT, EXP, EXP])
            other = prob[:, :, :].unsqueeze(2).to_broadcast([NP, NT, EXP, EXP])
            first = less[0:NP, :, :].rearrange("p e f -> p (e f)").unsqueeze(1).to_broadcast([NP, NT, EXP * EXP])
            pairs = lambda tile: tile[:, :, :, :].rearrange("p t e f -> p t (e f)")
            V.mark(vec.tensor_tensor(over[:, :, :, :], other, mine, ALU.is_gt))
            V.mark(vec.tensor_tensor(tie[:, :, :, :], other, mine, ALU.is_equal))
            own()
            V.mark(vec.tensor_tensor(pairs(tie), pairs(tie), first, ALU.mult))
            own()
            V.mark(vec.tensor_tensor(over[:, :, :, :], over[:, :, :, :], tie[:, :, :, :], ALU.add))
            own()
            V.mark(vec.tensor_reduce(comb[:, :, :], over[:, :, :, :], AX, ALU.add))
            own()
            V.mark(vec.scalar_tensor_tensor(comb[:, :, :], comb[:, :, :], 1.5, prob[:, :, :], ALU.is_lt, ALU.mult))
            own()
            V.mark(vec.tensor_reduce(s1[:, :], comb[:, :, :], AX, ALU.add))
            own()
            V.mark(vec.tensor_scalar(s1[:, :], s1[:, :], 1e-12, None, ALU.max))
            own()
            V.mark(vec.reciprocal(s2[:, :], s1[:, :]))
            own()
            V.mark(vec.tensor_tensor(comb[:, :, :], comb[:, :, :], b8(s2), ALU.mult))
            t_comb = V.now()

            out_rows = out.rearrange("(t p) d -> p t d", p=NP)
            s_out = sem("out_stored")
            wait(pool, t_comb)
            wait(vec, t_comb)
            wait(pe, P.now())
            wait(act, P.now())
            o_buf = xs
            with loop(nc, NODE_STEPS, {V: U5 * (EXP + 1), M: 2 * U5 + EXP * (4 + U5), A: U5 + EXP * 4, P: U5, S: 1}) as i:
                v0, a0, m0, s0, p0 = V.now(), A.now(), M.now(), S.now(), P.now()
                wait(pool, m0)
                t_cb = []
                for u in range(U5):
                    t_cb.append(P.mark(pool.tensor_copy(logit[:, u, :], flat(comb, i * U5 + u))))
                wait(vec, s0)
                last = []
                for u in range(U5):
                    wait(pe, t_cb[u], a0, v0)
                    wait(act, M.mark(pe.transpose(ps[0:EXP, 0, 0:NP], logit[:, u, :], ident[0:NP, 0:NP])))
                    wait(pe, A.mark(act.copy(comb_t[:, u, :], ps[0:EXP, 0, 0:NP])))
                    if u:
                        wait(pe, last[-1])
                    m = pe.matmul(ps[0:NP, 6, 0:D], comb_t[:, u, :], mb2_s[:, :], start=True, stop=True)
                    wait(vec, M.mark(m))
                    last.append(V.mark(vec.tensor_tensor(o_buf[:, u, :], ps[0:NP, 6, 0:D], flat(xa, i * U5 + u), ALU.add)))
                t_g, t_v = [], []
                for e in range(EXP):
                    for c in range(2):
                        for half, (lo, n) in enumerate(SPLIT):
                            b = 2 * c + half
                            wait(pe, t_g[-4] if e else a0)
                            for k in range(2):
                                m = pe.matmul(ps[:, b, 0:n], mw1_s[:, e, k, c * 128:(c + 1) * 128],
                                              xn_t[:, k, bass.ds(i * (U5 * NP) + lo, n)], start=(k == 0), stop=(k == 1))
                            wait(act, M.mark(m))
                            t_g.append(A.mark(act.activation(hid[:, e % 2, c, lo:lo + n], ps[:, b, 0:n], ACT.Gelu,
                                                             bias=mb1_s[:, e, c:c + 1])))
                    wait(pe, t_g[-1])
                    for u in range(U5):
                        b = 4 + len(t_v) % 3
                        wait(pe, t_v[-3] if len(t_v) >= 3 else last[-1])
                        for c in range(2):
                            m = pe.matmul(ps[0:NP, b, 0:D], hid[:, e % 2, c, u * NP:(u + 1) * NP], mw2_s[:, e, c, :],
                                          start=(c == 0), stop=(c == 1))
                        wait(vec, M.mark(m), last[u])
                        t = V.mark(vec.scalar_tensor_tensor(o_buf[:, u, :], ps[0:NP, b, 0:D], comb[:, bass.ds(i * U5 + u, 1), e],
                                                            o_buf[:, u, :], ALU.mult, ALU.add))
                        t_v.append(t)
                        last[u] = t
                wait(sp, last[-1])
                sp.dma_start(out_rows[:, bass.ds(i * U5, U5), :], o_buf[:, :, :]).then_inc(s_out, 16)
                stored([s_out], i)
            everyone()



_INS = ["x", "src", "dst", "edge_type_4", "L0_gnn_W", "L0_gnn_a_l", "L0_gnn_a_r", "L0_ffn_wr", "L0_ffn_br",
        "L0_ffn_w1", "L0_ffn_b1", "L0_ffn_w2", "L0_ffn_b2", "L1_gnn_self_W", "L1_gnn_self_b", "L1_gnn_rel_W",
        "L1_ffn_router_w", "L1_ffn_w1", "L1_ffn_b1", "L1_ffn_w2", "L1_ffn_b2"]


def kernel(**inputs):
    import numpy as _np
    import concourse.bacc as _bacc
    from concourse import mybir as _mybir
    from concourse.bass_utils import run_bass_kernel_spmd as _run

    nc = _bacc.Bacc("TRN2", target_bir_lowering=False, num_devices=1)
    arrays, args = {}, []
    for name in _INS:
        a = _np.ascontiguousarray(inputs[name])
        arrays[f"in_{name}"] = a
        args.append(nc.dram_tensor(f"in_{name}", a.shape, _mybir.dt.from_np(a.dtype), kind="ExternalInput").ap())
    args.append(nc.dram_tensor("out_0", (N, D), F32, kind="ExternalOutput").ap())
    build(nc, *args)
    r = _run(nc, [arrays], core_ids=[0])
    return r.results[0]["out_0"]
```

```python
from contextlib import ExitStack

import concourse.bass as bass
from concourse import mybir

ALU = mybir.AluOpType
ACT = mybir.ActivationFunctionType
AX = mybir.AxisListType.X
F32 = mybir.dt.float32
F16 = mybir.dt.float16
BF16 = mybir.dt.bfloat16
I32 = mybir.dt.int32
U16 = mybir.dt.uint16
ENG = mybir.EngineType
RMAX = bass.bass_isa.ReduceOp.max

N = 3125
E = 53125
D = 256
NP = 125
NT = N // NP
EC = E // NP
HEADS = 4
HD = D // HEADS
REL = 4
HID = 4 * D
EXP = 8
TOPK = 1561
EPS = 1e-5
SLOPE = 0.2

PAIR = 256
PAIRS = (E + NT * (PAIR - 1)) // PAIR
COLS = 2 * PAIRS
SORT_N = 17
SORT_STEPS = EC // SORT_N
GRP = 8
GRPS = 2
RING = GRP * GRPS
EDGE_STEPS = COLS // RING
LEAD = GRP // 2
AW = 260
U5 = 5
NODE_STEPS = NT // U5
SPLIT = ((0, 375), (375, 250))
BIG = 12582912.0
MOE_TILES = (2 * N + EXP * 127) // 128
MOE_BODY = 14
MOE_ROW = 16
MOE_STEPS = MOE_TILES // MOE_BODY
W1B = 2 * D + D + 2
LOW = 2048

assert NT * NP == N and EC * NP == E and SORT_STEPS * SORT_N == EC and EDGE_STEPS * RING == COLS and EDGE_STEPS >= NT
assert MOE_STEPS * MOE_BODY == MOE_TILES


class Lane:

    CREDIT = 256

    def __init__(self, nc, eng, sem):
        self.nc, self.eng, self.sem = nc, eng, sem
        self.base, self.n, self.per = self.CREDIT, 0, 0
        eng.sem_inc(sem, self.CREDIT)

    def mark(self, ins):
        ins.then_inc(self.sem, 1)
        self.n += 1
        return (self.sem, self.base + self.n)

    def now(self):
        return (self.sem, self.base + self.n)

    def last(self, k):
        return (self.sem, self.base + (k - self.per))


def wait(eng, *tickets):
    for sem, value in tickets:
        eng.wait_ge(sem, value)


def wait_apart(lane, *tickets):
    wait(lane.eng, *tickets)
    lane.eng.sem_inc(lane.sem, 1)
    lane.n += 1


class loop:

    def __init__(self, nc, steps, per):
        self.nc, self.steps, self.per = nc, steps, per

    def __enter__(self):
        self.ctx = self.nc.Fori(0, self.steps)
        i = self.ctx.__enter__()
        self.start = {}
        for lane, k in self.per.items():
            self.start[lane] = lane.base + lane.n
            lane.base, lane.n, lane.per = i * k + self.start[lane], 0, k
        return i

    def __exit__(self, *a):
        if a[0] is None:
            got = [lane.n for lane in self.per]
            want = list(self.per.values())
            assert got == want, f"marks of the body: {got}, stated {want}"
            for lane, k in self.per.items():
                lane.base, lane.n = self.start[lane] + self.steps * k, 0
        return self.ctx.__exit__(*a)


class Dma:

    def __init__(self, sem):
        self.sem, self.total = sem, 0

    def mark(self, ins):
        ins.then_inc(self.sem, 16)
        self.total += 16
        return (self.sem, self.total)


def build(nc, x, src, dst, etype, W, a_l, a_r, wr, br, w1, b1, w2, b2,
          self_W, self_b, rel_W, router, mw1, mb1, mw2, mb2, out):
    with ExitStack() as ctx:
        def sem(name):
            return ctx.enter_context(nc.semaphore(name))

        def sb(name, shape, dt=F32, c=ctx):
            return c.enter_context(nc.sbuf_tensor(name, shape, dt))

        vec, act, pe, pool, sp = nc.vector, nc.scalar, nc.tensor, nc.gpsimd, nc.sync
        V, A, M, P, S = (Lane(nc, e, sem(n)) for e, n in (
            (vec, "vector_done"), (act, "scalar_done"), (pe, "tensor_done"), (pool, "pool_done"), (sp, "stores_done")))

        turned_x, xt_in, x_added = (Lane(nc, e, sem(n)) for e, n in ((pe, "x_turned"), (act, "xt_copied"), (pool, "x_added")))
        passed = Lane(nc, pool, sem("pool_passed"))
        ps = ctx.enter_context(nc.psum_tensor("ps", [128, 8, 512], F32))
        h_tab = nc.dram_tensor("h_tab", [N, AW], F32, kind="Internal").ap()
        y_tab = nc.dram_tensor("y_tab", [REL * N, D], F32, kind="Internal").ap()
        w_tab = nc.dram_tensor("w_tab", [N], F32, kind="Internal").ap()
        xn_tab = nc.dram_tensor("xn_tab", [N, D], F32, kind="Internal").ap()
        y_nodes = nc.dram_tensor("y_nodes", [2 * N + MOE_TILES * 128, D], F32, kind="Internal").ap()

        ident = sb("ident", [128, 128])
        ones = sb("ones", [128, 128])
        before = sb("before", [128, 128])
        upto = sb("upto", [128, 128])
        lower = sb("lower", [128, 128])
        iota_c = sb("iota_c", [128, COLS], F16)
        iota_r = sb("iota_r", [128, 128], F16)
        iota_n = sb("iota_n", [128, 128])
        zeros_e = sb("zeros_e", [128, EC], F16)
        wait(pool, P.mark(pool.memset(ones[:, :], 1.0)))
        for tile, op, cm in ((ident, ALU.is_equal, -1), (before, ALU.is_gt, -1), (upto, ALU.is_ge, -1), (lower, ALU.is_gt, 1)):
            P.mark(pool.affine_select(tile[:, :], ones[:, :], pattern=[[-cm, 128]], compare_op=op, fill=0.0,
                                      base=0, channel_multiplier=cm))
        for tile, n in ((iota_c, COLS), (iota_r, 128), (iota_n, 128)):
            P.mark(pool.iota(tile[:, :], [[1, n]], base=0, channel_multiplier=0, allow_small_or_imprecise_dtypes=True))
        P.mark(pool.memset(zeros_e[:, :], 0.0))
        t_const = P.now()

        xa = sb("xa", [NP, NT, D])
        acc = sb("acc", [NP, NT * AW])
        acc3 = acc[:, :].rearrange("p (t c) -> p t c", c=AW)
        gath = sb("gath", [128, RING, AW])
        hot = sb("hot", [128, RING, NP])
        at_rows = sb("at_rows", [128, GRPS, GRP], I32)
        stats = sb("stats", [NP, NT, 6])
        first_root = sb("first_root", [1, 1])
        mean, var, tmp25, rstd, nmr = (sb(n, [NP, NT]) for n in ("mean", "var", "tmp25", "rstd", "nmr"))
        xs = sb("xs", [NP, U5, D])
        xt = sb("xt", [128, U5, 2, NP])
        slots = {}
        for g in "ab":
            slots[g] = (sb(f"local_{g}", [128, COLS]), sb(f"index_{g}", [128, COLS], I32),
                        sb(f"acc_at_{g}", [1, LEAD + PAIRS], I32), sb(f"hl_at_{g}", [1, LEAD + PAIRS], I32))
        hl_parts = sb("hl_parts", [NP, NT * 3 * HEADS], BF16)
        gmax = sb("gmax", [128, HEADS])

        d_in = [Dma(sem(f"load_{k}")) for k in range(14)]
        keys = {"a": sb("src_i", [NP, EC], I32), "b": sb("dst_i", [NP, EC], I32)}
        type_i = sb("type_i", [NP, EC], I32)
        ev = lambda v: v.rearrange("(p c) -> p c", c=EC)
        t_src = d_in[0].mark(sp.dma_start(keys["a"][:, :], ev(src)))
        t_dst = d_in[2].mark(sp.dma_start(keys["b"][:, :], ev(dst)))
        t_typ = d_in[3].mark(sp.dma_start(type_i[:, :], ev(etype)))

        def row_stats(t, src_tile):
            return V.mark(vec.bn_stats(stats[:, t, :], src_tile))

        def norm_factors():
            wait(act, A.now(), t_const)
            A.mark(act.activation(first_root[:, :], ones[0:1, 0:1], ACT.Sqrt))
            wait(vec, V.now())
            V.mark(vec.tensor_tensor(mean[:, :], stats[:, :, 1], stats[:, :, 4], ALU.add))
            V.mark(vec.tensor_tensor(tmp25[:, :], stats[:, :, 1], stats[:, :, 4], ALU.subtract))
            V.mark(vec.tensor_tensor(var[:, :], stats[:, :, 2], stats[:, :, 5], ALU.add))
            wait(vec, V.now())
            V.mark(vec.scalar_tensor_tensor(tmp25[:, :], tmp25[:, :], 0.25, tmp25[:, :], ALU.mult, ALU.mult))
            V.mark(vec.tensor_scalar(mean[:, :], mean[:, :], -0.5, None, ALU.mult))
            V.mark(vec.tensor_scalar(var[:, :], var[:, :], 1.0 / D, EPS, ALU.mult, ALU.add))
            wait(vec, V.now())
            wait(act, V.mark(vec.tensor_tensor(var[:, :], var[:, :], tmp25[:, :], ALU.add)))
            wait(vec, A.mark(act.activation(tmp25[:, :], var[:, :], ACT.Sqrt)))
            wait(vec, V.mark(vec.reciprocal(rstd[:, :], tmp25[:, :])))
            return V.mark(vec.tensor_tensor(nmr[:, :], mean[:, :], rstd[:, :], ALU.mult))

        def col(tile, t):
            return tile[:, bass.ds(t, 1)]

        def stored(sems, i):
            for s in sems:
                sp.wait_ge(s, i * 16 + 16)
            sp.sem_inc(S.sem, 1)
            S.n += 1

        def everyone(*more):
            for lane in (V, A, M, P, S, *more):
                for e in (vec, act, pe, pool, sp):
                    wait(e, lane.now())

        def matrix(m):
            return m.rearrange("(k p) n -> p k n", p=128)

        with ExitStack() as sort_ctx:
            def sbs(name, shape, dt=F32):
                return sb(name, shape, dt, sort_ctx)

            w_cat = sbs("w_cat", [128, 2, 264])
            w_t = sbs("w_t", [128, 2, D])
            a_bd = sbs("a_bd", [128, 2, 8])
            hbuf = sbs("hbuf", [NP, U5, AW])
            hrl = sbs("hrl", [128, NT, 2 * HEADS])
            hl_r = sbs("hl_r", [NP, NT, HEADS])
            gm = sbs("gm", [128, HEADS])
            plan = {g: sbs(f"plan_{g}", [NP, 4, EC]) for g in "ab"}
            cnt = sbs("cnt", [NP, NT])
            offs = sbs("offs", [NP, NT])
            tot = sbs("tot", [NT, 4])
            starts = sbs("starts", [NT, NT])
            reach = sbs("reach", [NT, PAIRS])
            pair_tile = sbs("pair_tile", [1, PAIRS])
            key_f, tile_f, pos, tmp_e, oth_f = (sbs(n, [NP, EC]) for n in ("key_f", "tile_f", "pos", "tmp_e", "oth_f"))
            scratch = sbs("scratch", [NP, NT * EC], F16)
            in_tile = scratch[:, :].rearrange("p (q c) -> p q c", q=NT)
            hi_s = sbs("hi_s", [128, COLS])

            own = lambda: wait(vec, V.now())

            def count_tiles(g, t_key):
                wait(vec, t_key)
                V.mark(vec.tensor_copy(key_f[:, :], keys[g][:, :]))
                own()
                V.mark(vec.tensor_scalar(tile_f[:, :], key_f[:, :], 1.0 / NP, -(NP - 1) / 2 / NP, ALU.mult, ALU.add))
                own()
                V.mark(vec.tensor_scalar(tile_f[:, :], tile_f[:, :], BIG, BIG, ALU.add, ALU.subtract))
                own()
                for q in range(NT):
                    t = V.mark(vec.tensor_scalar(in_tile[:, q, :], tile_f[:, :], float(q), None, ALU.is_equal, ALU.add,
                                                 accum_out=cnt[:, q:q + 1]))
                return t

            def tile_starts(g, t):
                wait(pe, t)
                wait(vec, M.mark(pe.matmul(ps[0:NT, 4, 0:1], cnt[:, :], ones[0:NP, 0:1], start=True, stop=True)))
                V.mark(vec.tensor_scalar(tot[:, 0:1], ps[0:NT, 4, 0:1], 1.0 / PAIR, (PAIR - 1) / 2 / PAIR, ALU.mult, ALU.add))
                own()
                V.mark(vec.tensor_scalar(tot[:, 1:2], tot[:, 0:1], BIG, BIG, ALU.add, ALU.subtract))
                own()
                t = V.mark(vec.tensor_scalar(starts[:, :], before[0:NT, 0:NT], tot[:, 1:2], float(PAIR), ALU.mult, ALU.mult))
                wait(pe, t)
                m = pe.matmul(ps[0:NT, 4, 8:9], upto[0:NT, 0:NT], tot[:, 1:2], start=True, stop=True)
                wait(vec, M.mark(m))
                V.mark(vec.tensor_copy(tot[:, 2:3], ps[0:NT, 4, 8:9]))
                pe.matmul(ps[0:NP, 7, 0:NT], before[0:NP, 0:NP], cnt[:, :], start=True, stop=False)
                m = pe.matmul(ps[0:NP, 7, 0:NT], ones[0:NT, 0:NP], starts[:, :], start=False, stop=True)
                wait(vec, M.mark(m))
                V.mark(vec.tensor_scalar(offs[:, :], ps[0:NP, 7, 0:NT], -1.0, None, ALU.add))
                own()
                t = V.mark(vec.tensor_scalar(reach[:, :], iota_c[0:NT, 0:PAIRS], tot[:, 2:3], None, ALU.is_ge))
                wait(pe, t)
                wait(vec, M.mark(pe.matmul(ps[0:1, 4, 0:PAIRS], ones[0:NT, 0:1], reach[:, :], start=True, stop=True)))
                V.mark(vec.tensor_scalar(pair_tile[:, :], ps[0:1, 4, 0:PAIRS], float(NT - 1), None, ALU.min))
                own()
                V.mark(vec.tensor_scalar(slots[g][2][:, LEAD:], pair_tile[:, :], float(AW), None, ALU.mult))
                V.mark(vec.tensor_scalar(slots[g][3][:, LEAD:], pair_tile[:, :], float(3 * HEADS), None, ALU.mult))

            def plan_sort(g, t_oth):
                for q in range(NT):
                    buf = ps[0:NP, 5 + q % 2, 0:EC]
                    V.mark(vec.tensor_tensor_scan(buf, in_tile[:, q, :], zeros_e[0:NP, :], offs[:, q:q + 1], ALU.add, ALU.add))
                    own()
                    V.mark(vec.copy_predicated(pos[:, :], in_tile[:, q, :].bitcast(U16), buf))
                own()
                row, column, pay1, pay2 = (plan[g][:, k, :] for k in range(4))
                V.mark(vec.tensor_scalar(tmp_e[:, :], pos[:, :], 1.0 / 128, -63.5 / 128, ALU.mult, ALU.add))
                own()
                V.mark(vec.tensor_scalar(column, tmp_e[:, :], BIG, BIG, ALU.add, ALU.subtract))
                own()
                V.mark(vec.scalar_tensor_tensor(row, column, -128.0, pos[:, :], ALU.mult, ALU.add))
                V.mark(vec.scalar_tensor_tensor(key_f[:, :], tile_f[:, :], -float(NP), key_f[:, :], ALU.mult, ALU.add))
                wait(vec, t_oth)
                V.mark(vec.tensor_scalar(tmp_e[:, :], oth_f[:, :], 1.0 / LOW, -(LOW - 1) / 2 / LOW, ALU.mult, ALU.add))
                own()
                V.mark(vec.tensor_scalar(tmp_e[:, :], tmp_e[:, :], BIG, BIG, ALU.add, ALU.subtract))
                own()
                V.mark(vec.scalar_tensor_tensor(pay2, tmp_e[:, :], -float(LOW), oth_f[:, :], ALU.mult, ALU.add))
                V.mark(vec.scalar_tensor_tensor(pay1, tmp_e[:, :], 128.0, key_f[:, :], ALU.mult, ALU.add))
                own()
                return V.mark(vec.tensor_scalar(pay1, pay1, 1.0, None, ALU.add))

            t_zero = P.mark(pool.memset(pos[:, :], 0.0))
            wait(sp, P.mark(pool.memset(a_bd[:, :, :], 0.0)))
            t_w = d_in[4].mark(sp.dma_start(w_cat[:, :, 0:D], matrix(W)))
            for h in range(HEADS):
                for k, a in ((0, a_r), (4, a_l)):
                    t_a = d_in[5].mark(sp.dma_start(a_bd[(h % 2) * HD:(h % 2 + 1) * HD, h // 2, k + h:k + h + 1],
                                                    a[0, h, :].rearrange("(d o) -> d o", o=1)))
            t_x = d_in[1].mark(sp.dma_start(xa[:, :, :], x.rearrange("(t p) d -> p t d", p=NP)))
            for g in "ab":
                P.mark(pool.memset(slots[g][2][:, 0:LEAD], 0))
                P.mark(pool.memset(slots[g][3][:, 0:LEAD], 0))
            t_hrl = P.mark(pool.memset(hrl[:, :, :], -3.0e38))
            t_acc = P.mark(pool.memset(acc[:, :], 0.0))

            wait(vec, t_const, t_zero, t_dst)
            t_oth = V.mark(vec.tensor_copy(oth_f[:, :], keys["b"][:, :]))
            tile_starts("a", count_tiles("a", t_src))

            wait(vec, t_x)
            for t in range(NT):
                row_stats(t, xa[:, t, :])
            t_norm = norm_factors()

            wait(pe, t_const, t_w, t_a)
            for k in range(2):
                for j in range(2):
                    m = pe.transpose(ps[:, 0, (2 * k + j) * 128:(2 * k + j + 1) * 128], w_cat[:, k, j * 128:(j + 1) * 128], ident[:, :])
            wait(act, M.mark(m))
            t_wt = A.mark(act.copy(w_t[:, :, :].rearrange("p j (k i) -> p j k i", k=2),
                                   ps[:, 0, :].rearrange("p (k j i) -> p j k i", k=2, j=2)))
            wait(pe, t_wt)
            for k in range(2):
                for j in range(2):
                    m = pe.matmul(ps[:, 1, k * 8:k * 8 + 8], w_t[:, j, k * 128:(k + 1) * 128], a_bd[:, j, :],
                                  start=(j == 0), stop=(j == 1))
            wait(act, M.mark(m))
            t_wc = A.mark(act.copy(w_cat[:, :, D:D + 8], ps[:, 1, 0:16].rearrange("p (k c) -> p k c", k=2)))

            s_tab = [sem(f"h_stored_{u}") for u in range(U5)]
            wait(pe, t_wc)
            for e in (act, pe):
                wait(e, t_norm, t_hrl)
            h_made = Lane(nc, pe, sem("h_made"))
            normed, h_out = (Lane(nc, act, sem(n)) for n in ("x_normed", "h_copied"))
            with loop(nc, NODE_STEPS, {**{lane: U5 for lane in (turned_x, h_made, normed, xt_in, h_out)}, S: 2}) as i:
                s_now, x0, h0 = [S.last(1), S.last(2)], xt_in.now(), h_out.now()
                t_n, t_t, t_xt, t_m, t_h = ([] for _ in range(5))
                for step in range(U5 + 2):
                    u = step
                    if u < U5:
                        wait(act, turned_x.last(u + 1))
                        t_n.append(normed.mark(act.activation(xs[:, u, :], xa[:, bass.ds(i * U5 + u, 1), :].rearrange("p a d -> p (a d)"),
                                                              ACT.Identity, bias=col(nmr, i * U5 + u), scale=col(rstd, i * U5 + u))))
                    u = step - 1
                    if 0 <= u < U5:
                        wait(pe, t_n[u], t_xt[u - 2] if u >= 2 else x0)
                        for k in range(2):
                            m = pe.transpose(ps[:, u % 2, k * NP:(k + 1) * NP], xs[:, u, k * 128:(k + 1) * 128], ident[0:NP, 0:NP])
                        t_t.append(turned_x.mark(m))
                        wait(act, t_t[u], h_made.last(u + 1))
                        t_xt.append(xt_in.mark(act.copy(xt[:, u, :, :], ps[:, u % 2, 0:2 * NP].rearrange("p (k n) -> p k n", k=2))))
                    u = step - 2
                    if u >= 0:
                        wait(pe, t_xt[u], t_h[u - 2] if u >= 2 else h0)
                        for k in range(2):
                            m = pe.matmul(ps[0:NP, 2 + u % 2, 0:264], xt[:, u, k, :], w_cat[:, k, :], start=(k == 0), stop=(k == 1))
                        t_m.append(h_made.mark(m))
                        wait(act, t_m[u], s_now[u // 2 > 0])
                        act.copy(hbuf[:, u, :], ps[0:NP, 2 + u % 2, 0:AW])
                        t_h.append(h_out.mark(act.copy(hrl[0:NP, bass.ds(i * U5 + u, 1), :].rearrange("p a d -> p (a d)"), ps[0:NP, 2 + u % 2, D:264])))
                        wait(sp, t_h[u])
                        sp.dma_start(h_tab[bass.ds((i * U5 + u) * NP, NP), :], hbuf[:, u, :]).then_inc(s_tab[u], 16)
                        if u == 2:
                            stored(s_tab[:2], i)
                stored(s_tab[2:], i)
            t_hl = h_out.now()
            wait(pool, S.now())

            t_plan_a = plan_sort("a", t_oth)
            wait(vec, t_typ)
            V.mark(vec.tensor_copy(tmp_e[:, :], type_i[:, :]))
            V.mark(vec.tensor_copy(key_f[:, :], keys["a"][:, :]))
            own()
            t_oth = V.mark(vec.scalar_tensor_tensor(oth_f[:, :], tmp_e[:, :], float(N), key_f[:, :], ALU.mult, ALU.add))
            own()
            t_cnt = count_tiles("b", t_dst)
            tile_starts("b", t_cnt)
            t_plan_b = plan_sort("b", t_oth)

            hot_c = sbs("hot_c", [NP, SORT_N, COLS], F16)
            hot_r = sbs("hot_r", [NP, SORT_N, 128], F16)
            pay = sbs("pay", [NP, 2, SORT_N, 128], F16)
            stage_v, stage_a, stage_p = (sbs(f"stage_{e}", [NP, 4, SORT_N]) for e in "vap")
            CHUNKS = ((0, 5), (5, 9), (9, 13), (13, 17))
            moved = Lane(nc, pe, sem("columns_moved"))
            weighed = Lane(nc, act, sem("payloads_weighed"))
            PAY_V, PAY_P = 2, 3

            def permute_open():
                wait(pe, t_const)
                for k in range(2):
                    pe.matmul(ps[:, 6 + k, 0:COLS], zeros_e[0:NP, 0:128], iota_c[0:NP, :], start=True, stop=False,
                              skip_group_check=True)

            def permute_close():
                for k in range(2):
                    m = pe.matmul(ps[:, 6 + k, 0:COLS], zeros_e[0:NP, 0:128], iota_c[0:NP, :], start=False, stop=True,
                                  skip_group_check=True)
                return M.mark(m)

            def permute_parts(i, g, by_v, by_p):
                by_a = SORT_N - by_v - by_p
                tick = {}
                at = bass.ds(i * SORT_N, SORT_N)

                def scalars():
                    wait(vec, V.now())
                    tick["stage"] = V.mark(vec.tensor_copy(stage_v[:, :, :], plan[g][:, :, at]))
                    wait(act, weighed.now())
                    wait(act, weighed.mark(act.copy(stage_a[:, 2:4, :], plan[g][:, 2:4, at])))
                    if by_p:
                        wait(pool, P.now())
                        wait_apart(passed, P.mark(pool.tensor_copy(stage_p[:, :, :], plan[g][:, :, at])), moved.last(len(CHUNKS)))
                        for j in range(by_a + by_v, SORT_N):
                            for k in range(2):
                                tp = P.mark(pool.tensor_scalar(pay[:, k, j, :], iota_r[0:NP, :], stage_p[:, 0, j:j + 1],
                                                               stage_p[:, 2 + k, j:j + 1], ALU.is_equal, ALU.mult))
                            tick["p", j] = tp

                def on_v(c):
                    lo, hi = CHUNKS[c]
                    wait(vec, tick["stage"])
                    n = min(hi, by_a) - lo
                    if n > 0:
                        wait(vec, weighed.last(2 + c))
                        tick["rows", c] = V.mark(vec.tensor_tensor(
                            hot_r[:, lo:lo + n, :], iota_r[0:NP, :].unsqueeze(1).to_broadcast([NP, n, 128]),
                            stage_v[:, 0, lo:lo + n].unsqueeze(2).to_broadcast([NP, n, 128]), ALU.is_equal))
                        yield
                    wait(vec, moved.last(c + 1))
                    for j in range(lo, hi):
                        t = vec.tensor_scalar(hot_c[:, j, :], iota_c[0:NP, :], stage_v[:, 1, j:j + 1], None, ALU.is_equal)
                        if by_a <= j < by_a + by_v:
                            for k in range(2):
                                t = vec.tensor_scalar(pay[:, k, j, :], iota_r[0:NP, :], stage_v[:, 0, j:j + 1],
                                                      stage_v[:, 2 + k, j:j + 1], ALU.is_equal, ALU.mult)
                        if j == hi - 1:
                            tick["v", c] = V.mark(t)
                        yield

                def on_a(c):
                    lo, hi = CHUNKS[c]
                    if lo < by_a:
                        wait(act, tick["rows", c], moved.last(c + 1))
                        for j in range(lo, min(hi, by_a)):
                            for k in range(2):
                                t = act.mul(pay[:, k, j, :], hot_r[:, j, :], stage_a[:, 2 + k, j:j + 1])
                        tick["a", c] = weighed.mark(t)

                def on_pe(c):
                    lo, hi = CHUNKS[c]
                    wait(pe, tick["v", c])
                    if ("a", c) in tick:
                        wait(pe, tick["a", c])
                    for j in range(lo, hi):
                        if ("p", j) in tick:
                            wait(pe, tick["p", j])
                        for k in range(2):
                            m = pe.matmul(ps[:, 6 + k, 0:COLS], pay[:, k, j, :], hot_c[:, j, :], start=False, stop=False,
                                          skip_group_check=True)
                    moved.mark(m)

                return scalars, on_v, on_a, on_pe

            def unpack(g, t_moved):
                local, index = slots[g][0], slots[g][1]
                wait(vec, t_moved, V.now())
                V.mark(vec.tensor_scalar(hi_s[:, :], ps[:, 6, 0:COLS], 1.0 / 128, -(NP / 2) / 128, ALU.mult, ALU.add))
                wait(vec, V.now())
                V.mark(vec.tensor_scalar(hi_s[:, :], hi_s[:, :], BIG, BIG, ALU.add, ALU.subtract))
                wait(vec, V.now())
                V.mark(vec.scalar_tensor_tensor(index[:, :], hi_s[:, :], float(LOW), ps[:, 7, 0:COLS], ALU.mult, ALU.add))
                V.mark(vec.scalar_tensor_tensor(local[:, :], hi_s[:, :], -128.0, ps[:, 6, 0:COLS], ALU.mult, ALU.add))
                wait(vec, V.now())
                return V.mark(vec.tensor_scalar(local[:, :], local[:, :], -1.0, None, ALU.add))

            wait(pe, A.now(), V.now())
            permute_open()
            wait(act, t_plan_a)
            wait(pool, t_plan_a)
            with loop(nc, SORT_STEPS, {V: 1 + 3 + len(CHUNKS), P: 1 + 2 * PAY_P, passed: 1, moved: len(CHUNKS), weighed: 1 + 3}) as i:
                scalars, on_v, on_a, on_pe = permute_parts(i, "a", PAY_V, PAY_P)
                scalars()
                for c in range(len(CHUNKS)):
                    for _ in on_v(c):
                        pass
                    on_a(c)
                    on_pe(c)
            t_slots_a = unpack("a", permute_close())

            parts = hl_parts[:, :].rearrange("p (t h c) -> p t h c", t=NT, h=HEADS)
            hl = hrl[0:NP, :, HEADS:]
            wait(vec, t_hl)
            wait(vec, V.mark(vec.tensor_copy(parts[:, :, :, 0], hl[:, :, :])))
            wait(vec, V.mark(vec.tensor_tensor(hl_r[:, :, :], hl[:, :, :], parts[:, :, :, 0], ALU.subtract)))
            wait(vec, V.mark(vec.tensor_copy(parts[:, :, :, 1], hl_r[:, :, :])))
            wait(vec, V.mark(vec.tensor_tensor(hl_r[:, :, :], hl_r[:, :, :], parts[:, :, :, 1], ALU.subtract)))
            t_parts = V.mark(vec.tensor_copy(parts[:, :, :, 2], hl_r[:, :, :]))
            t = V.mark(vec.tensor_reduce(gm[:, :], hrl[:, :, 0:HEADS].rearrange("p t h -> p h t"), AX, ALU.max))
            wait(pool, t)
            t_gmax = P.mark(pool.partition_all_reduce(gmax[:, :], gm[:, :], 128, RMAX))

            s_gath = [sem(f"gathered_{k}") for k in range(RING)]
            summed = Lane(nc, pe, sem("pairs_summed"))
            added = Lane(nc, vec, sem("pairs_added"))
            copied = Lane(nc, act, sem("transposes_copied"))
            picked_read = Lane(nc, vec, sem("picks_read"))
            hot_t = sbs("hot_t", [NP, GRPS, GRP, 128], BF16)
            hle = sbs("hle", [128, GRPS, GRP * HEADS])
            score = sbs("score", [128, GRPS, 2, GRP * HEADS])
            expo = sbs("expo", [128, GRPS, GRP * HEADS])
            hl_bc = gmax[:, :].unsqueeze(1).to_broadcast([128, GRP, HEADS])

            def gather(i, g, table, width, idx, t_used):
                wait(pool, t_used[0])
                wait_apart(passed, P.mark(pool.tensor_copy(at_rows[:, g, :], idx[:, bass.ds(i * RING + g * GRP, GRP)])))
                gather_rows(g, table, width, 0, GRP // 2)
                wait_apart(passed, t_used[1])
                gather_rows(g, table, width, GRP // 2, GRP)

            def gather_rows(g, table, width, lo=0, hi=GRP):
                for s in range(g * GRP + lo, g * GRP + hi):
                    pool.indirect_dma_start(gath[:, s, 0:width], None, table,
                                            bass.IndirectOffsetOnAxis(ap=at_rows[:, g, s % GRP:s % GRP + 1], axis=0)
                                            ).then_inc(s_gath[s], 16)

            def gathered(eng, turn, lo, hi):
                for s in range(lo, hi):
                    eng.wait_ge(s_gath[s], turn * 16 + 16)

            def one_hots(i, g, local, t_used):
                at = local[:, bass.ds(i * RING + g * GRP, GRP)]
                wait(vec, t_used)
                return V.mark(vec.tensor_tensor(hot[:, g * GRP:(g + 1) * GRP, :], iota_n[:, 0:NP].unsqueeze(1).to_broadcast([128, GRP, NP]),
                                                at.unsqueeze(2).to_broadcast([128, GRP, NP]), ALU.is_equal))

            def pair_offsets(engine, table, at, top, n=RING // 2):
                return nc.values_load_multi_w_load_instructions(
                    table[0:1, bass.ds(at, n)], engines=[engine], min_val=0, max_val=top,
                    skip_runtime_bounds_check_because="the tile is the minimum of a count and NT - 1")[1]

            def sum_pair(q, width, t_emptied):
                wait(pe, t_emptied)
                for s in (2 * q, 2 * q + 1):
                    m = pe.matmul(ps[0:NP, 4 + q % 2, 0:width], hot[:, s, :], gath[:, s, 0:width], start=(s == 2 * q), stop=(s == 2 * q + 1))
                return summed.mark(m)

            def add_pair(q, offset, width, t_sum):
                wait(vec, t_sum, added.now())
                at = acc[:, bass.ds(offset, width)]
                return added.mark(vec.tensor_tensor(at, at, ps[0:NP, 4 + q % 2, 0:width], ALU.add))

            def transpose_hot(g, t_hot, t_free):
                wait(pe, t_hot)
                t = []
                for half in range(2):
                    wait(pe, t_free[half])
                    for s in range(4):
                        m = pe.transpose(ps[0:NP, half, s * 128:(s + 1) * 128], hot[:, g * GRP + half * 4 + s, :], ident[:, :])
                    wait(act, M.mark(m))
                    t.append(copied.mark(act.copy(hot_t[:, g, half * 4:half * 4 + 4, :],
                                                  ps[0:NP, half, :].rearrange("p (s e) -> p s e", s=4))))
                return t

            def pick_hl(g, offsets, t_copied, t_read):
                wait(pe, t_read, *t_copied)
                for s in range(GRP):
                    m = pe.matmul(ps[:, 2 + g, s * 12:s * 12 + 12], hot_t[:, g, s, :],
                                  hl_parts[:, bass.ds(offsets[s // 2], 12)], start=True, stop=True)
                return M.mark(m)

            def weights(g, turn, t_pick, between=iter(())):
                lo, hi = g * GRP, (g + 1) * GRP
                three = lambda tile: tile.rearrange("p (s h) -> p s h", h=HEADS)
                wait(vec, t_pick, V.now())
                t = picked_read.mark(vec.tensor_reduce(hle[:, g, :], ps[:, 2 + g, 0:GRP * 12].rearrange("p (s c) -> p s c", c=3), AX, ALU.add))
                next(between, None)
                wait(vec, t)
                V.mark(vec.tensor_tensor(three(score[:, g, 1, :]), three(hle[:, g, :]), hl_bc, ALU.add))
                gathered(vec, turn, lo, hi)
                t = V.mark(vec.tensor_tensor(three(score[:, g, 0, :]), three(hle[:, g, :]), gath[:, lo:hi, D:AW], ALU.add))
                next(between, None)
                wait(vec, t)
                t = V.mark(vec.scalar_tensor_tensor(score[:, g, :, :], score[:, g, :, :], SLOPE, score[:, g, :, :], ALU.mult, ALU.max))
                next(between, None)
                wait(vec, t)
                wait(act, V.mark(vec.tensor_tensor(expo[:, g, :], score[:, g, 0, :], score[:, g, 1, :], ALU.subtract)))
                return A.mark(act.activation(gath[:, lo:hi, D:AW], three(expo[:, g, :]), ACT.Exp))

            def weigh(g, t_w):
                wait(vec, t_w)
                t = []
                for a in (g * GRP, g * GRP + 4):
                    rows = gath[:, a:a + 4, 0:D].rearrange("p s (h d) -> p s h d", h=HEADS)
                    t.append(V.mark(vec.tensor_tensor(rows, rows, gath[:, a:a + 4, D:AW].unsqueeze(3).to_broadcast([128, 4, HEADS, HD]), ALU.mult)))
                return t

            def two_sums(g, half, t_rows, t_added):
                wait(pe, t_rows[half])
                q = (g * GRP + 4 * half) // 2
                return [sum_pair(q + k, AW, t_added[k]) for k in range(2)]

            def two_adds(g, half, offsets, t_sums, between=iter(())):
                q = (g * GRP + 4 * half) // 2
                t = []
                for k in range(2):
                    t.append(add_pair(q + k, offsets[2 * half + k], AW, t_sums[k]))
                    next(between, None)
                return t

            FIRST_STEPS = 2

            def attention_body(i, with_sort):
                HALF = RING // 4
                m0 = M.now()
                gather(i, 0, h_tab, AW, slots["a"][1], [summed.last(2 * HALF - 2), summed.last(2 * HALF)])
                p_off = pair_offsets(ENG.PE, slots["a"][3], i * (RING // 2) + LEAD, (NT - 1) * 3 * HEADS)
                if with_sort:
                    scalars, on_v, on_a, on_pe = permute_parts(i, "b", 0, 0)
                    scalars()
                t_added = [added.last(2 * HALF - 1), added.last(2 * HALF)]
                t_read = [picked_read.last(2), None]
                t_free = [copied.last(3), copied.last(4)]
                t_pick = {1: m0}
                for n, (late, early) in enumerate(((1, 0), (0, 1))):
                    steps = [on_v(2 * n), on_v(2 * n + 1)] if with_sort else [iter(()), iter(())]
                    t_w = weights(late, i, t_pick[late], steps[0])
                    if n == 0:
                        t_read[1] = picked_read.now()
                        t_hot = one_hots(i, early, slots["a"][0], summed.last(2 * HALF))
                    else:
                        t_hot = one_hots(i, early, slots["a"][0], t_used)
                    t_free = transpose_hot(early, t_hot, t_free)
                    t_rows = weigh(late, t_w)
                    if n == 0:
                        v_off = pair_offsets(ENG.DVE, slots["a"][2], i * (RING // 2), (NT - 1) * AW)
                    off = v_off[n * HALF:(n + 1) * HALF]
                    t_sums = two_sums(late, 0, t_rows, t_added)
                    t_half = t_sums[-1]
                    t_pick[early] = pick_hl(early, p_off[early * HALF:(early + 1) * HALF], t_free, t_read[early])
                    for _ in steps[0]:
                        pass
                    if with_sort:
                        on_a(2 * n)
                    t_added = two_adds(late, 0, off, t_sums, steps[1])
                    t_sums = two_sums(late, 1, t_rows, t_added)
                    for _ in range(FIRST_STEPS):
                        next(steps[1], None)
                    if with_sort:
                        on_pe(2 * n)
                        on_a(2 * n + 1)
                    t_added = two_adds(late, 1, off, t_sums, steps[1])
                    for _ in steps[1]:
                        pass
                    if with_sort:
                        on_pe(2 * n + 1)
                    if n == 0:
                        t_used = t_sums[-1]
                        gather(i, 1, h_tab, AW, slots["a"][1], [t_half, t_used])

            for e in (act, pe, pool, vec):
                wait(e, t_slots_a, t_plan_b, t_parts, t_gmax, P.now(), t_acc)
            V.mark(vec.memset(hot[:, GRP:, :], 0.0))
            wait(pool, P.mark(pool.memset(at_rows[:, 1, :], 0)))
            gather_rows(1, h_tab, AW)
            M.mark(pe.matmul(ps[:, 3, 0:GRP * 12], zeros_e[0:NP, 0:128], zeros_e[0:NP, 0:GRP * 12], start=True, stop=True))
            permute_open()
            wait(pe, V.now())
            SORT_MARKS = {moved: len(CHUNKS), weighed: 1 + len(CHUNKS)}
            BODY = {V: 2 * 7, P: GRPS, passed: 2 * GRPS, M: 6, A: 2, copied: 4, picked_read: 2, summed: 8, added: 8}
            with loop(nc, SORT_STEPS, {**BODY, **SORT_MARKS, V: BODY[V] + 1 + 2 * len(CHUNKS)}) as i:
                attention_body(i, True)
            t_slots_b = unpack("b", permute_close())
            with loop(nc, EDGE_STEPS - SORT_STEPS, BODY) as i:
                attention_body(i + SORT_STEPS, False)
            last_off = pair_offsets(ENG.DVE, slots["a"][2], PAIRS, (NT - 1) * AW, LEAD)
            t_rows = weigh(1, weights(1, EDGE_STEPS, M.now()))
            t_added = [added.now(), added.now()]
            for half in range(2):
                t_added = two_adds(1, half, last_off, two_sums(1, half, t_rows, t_added))

            everyone(added)

        flat = lambda tile, t: tile[:, bass.ds(t, 1), :].rearrange("p a d -> p (a d)")
        acc_cols = lambda t, c, n: acc[:, bass.ds(t * AW + c, n)]

        def norm_steps(i, to=None, add_back=False, t_stored=None, t_used=None):
            t_n, t_t, x0 = {}, {}, xt_in.now()

            def norm(u):
                wait(vec, turned_x.last(u + 1))
                if add_back:
                    wait(vec, x_added.last(u + 1))
                if t_stored:
                    wait(vec, t_stored(u))
                t_n[u] = V.mark(vec.tensor_scalar(xs[:, u, :], flat(xa, i * U5 + u), col(rstd, i * U5 + u), col(nmr, i * U5 + u),
                                                  ALU.mult, ALU.add))
                if add_back:
                    wait(pool, t_n[u])
                    x_added.mark(pool.tensor_tensor(flat(xa, i * U5 + u), flat(xa, i * U5 + u), xs[:, u, :], ALU.add))
                return t_n[u]

            def turn(u):
                wait(pe, t_n[u], t_t[u - 2] if u >= 2 else x0)
                for k in range(2):
                    m = pe.transpose(ps[:, u % 2, k * NP:(k + 1) * NP], xs[:, u, k * 128:(k + 1) * 128], ident[0:NP, 0:NP])
                wait(act, turned_x.mark(m))
                if t_used:
                    wait(act, t_used(u))
                t_t[u] = xt_in.mark(act.copy(xt[:, u, :, :] if to is None else to[:, :, bass.ds((i * U5 + u) * NP, NP)],
                                             ps[:, u % 2, 0:2 * NP].rearrange("p (k n) -> p k n", k=2)))
                return t_t[u]

            return norm, turn

        def row_bcast(tile, row, load, k):
            return load.mark(sp.dma_start(tile, row.rearrange("(o d) -> o d", o=1).to_broadcast([k, row.shape[0]])))

        wide = sb("wide", [128, NT * D])
        xn_t = wide[:, 0:2 * N].rearrange("p (k n) -> p k n", k=2)
        xb = wide[0:NP, :].rearrange("p (t d) -> p t d", d=D)
        self_s = sb("self_s", [128, 2, D])
        sb_s = sb("sb_s", [NP, D])
        tab_ctx = ctx.enter_context(ExitStack())
        rel_s = sb("rel_s", [128, 2, REL, D], c=tab_ctx)

        with ExitStack() as ffn_ctx:
            def sbf(name, shape, dt=F32):
                return sb(name, shape, dt, ffn_ctx)

            hid = sbf("hid", [128, HID // 128, U5 * NP])
            w1_s = sbf("w1_s", [128, 2, HID])
            w2_s = sbf("w2_s", [128, HID // 128, D])
            b1_s = sbf("b1_s", [128, HID // 128])
            b2_s = sbf("b2_s", [NP, D])
            wr_s = sbf("wr_s", [NP, D])
            br_s = sbf("br_s", [NP, 1])
            w_turned = sbf("w_turned", [NT, NP])
            w_dot = sbf("w_dot", [NP, NT])
            w_all = sbf("w_all", [NP, N])
            junk_d = sbf("junk_d", [NP, D])
            w_col = sbf("w_col", [NP, NT])
            above = sbf("above", [NP, NT, 3])
            junk = sbf("junk", [NP, N], BF16)
            same = sbf("same", [NP, NP])
            gate = sbf("gate", [NP, NT])
            dinv = sbf("dinv", [NP, NT, HEADS])
            t_w1 = d_in[6].mark(sp.dma_start(w1_s[:, :, :], matrix(w1)))
            d_in[7].mark(sp.dma_start(w2_s[:, :, :], matrix(w2)))
            t_w2 = d_in[7].mark(sp.dma_start(b1_s[:, :], b1.rearrange("(k p) -> p k", p=128), allow_slow_non_contiguous=True))
            row_bcast(b2_s[:, :], b2, d_in[8], NP)
            row_bcast(wr_s[:, :], wr.rearrange("d o -> (d o)"), d_in[8], NP)
            t_wr = row_bcast(br_s[:, :], br, d_in[8], NP)

            t_rel = d_in[9].mark(sp.dma_start(self_s[:, :, :], matrix(self_W)))
            for r in range(REL):
                t_rel = d_in[9].mark(sp.dma_start(rel_s[:, :, r, :], matrix(rel_W[r])))
            t_sb = row_bcast(sb_s[:, :], self_b, d_in[10], NP)

            V.mark(vec.tensor_scalar(dinv[:, :, :], acc3[:, :, D:AW], 1e-38, None, ALU.max))
            wait(vec, V.now())
            V.mark(vec.reciprocal(dinv[:, :, :], dinv[:, :, :]))
            wait(vec, V.now())
            t_x1 = []
            for i in range(NODE_STEPS + 1):
                at = slice(i * U5, (i + 1) * U5)
                if i < NODE_STEPS:
                    rows = acc3[:, at, 0:D].rearrange("p t (h d) -> p t h d", h=HEADS)
                    wait(pool, V.mark(vec.tensor_tensor(rows, rows, dinv[:, at, :].unsqueeze(3).to_broadcast([NP, U5, HEADS, HD]), ALU.mult)))
                    t_x1.append(P.mark(pool.tensor_tensor(xa[:, at, :], xa[:, at, :], acc3[:, at, 0:D], ALU.add)))
                if i:
                    wait(vec, t_x1[i - 1])
                    for t in range((i - 1) * U5, i * U5):
                        row_stats(t, xa[:, t, :])
            t_norm = norm_factors()
            for e in (vec, act, pool, pe):
                wait(e, t_norm, t_wr, t_w1, t_w2)
            dotted = Lane(nc, vec, sem("routing_products"))
            with loop(nc, NODE_STEPS, {V: U5, turned_x: U5, xt_in: U5, x_added: U5, dotted: U5}) as i:
                norm, turn = norm_steps(i, to=xn_t, add_back=True, t_stored=lambda u: dotted.last(u + 1))
                t_xs = []
                for step in range(U5 + 1):
                    if step < U5:
                        t_xs.append(norm(step))
                    if step:
                        turn(step - 1)
                        wait(vec, t_xs[step - 1], dotted.now())
                        dotted.mark(vec.scalar_tensor_tensor(junk_d[:, :], xs[:, step - 1, :], 1.0, wr_s[:, :], ALU.mult, ALU.mult,
                                                             accum_out=col(w_dot, i * U5 + step - 1)))

            wait(vec, dotted.now())
            t_col = V.mark(vec.tensor_scalar(w_col[:, :], w_dot[:, :], br_s[:, 0:1], None, ALU.add))
            wait(pe, t_col, xt_in.now())
            t_wt = M.mark(pe.transpose(ps[0:NT, 7, 0:NP], w_col[:, :], ident[0:NP, 0:NP]))
            wait(vec, t_wt)
            wait(sp, V.mark(vec.tensor_copy(w_turned[:, :], ps[0:NT, 7, 0:NP])))
            wait(sp, d_in[8].mark(sp.dma_start(w_tab.rearrange("(t p) -> t p", p=NP), w_turned[:, :])))
            t_all = row_bcast(w_all[:, :], w_tab, d_in[8], NP)

            ffn_start = A.base + A.n
            with loop(nc, NODE_STEPS, {M: 16 + U5, A: 16 + U5}) as i:
                a0 = A.now()
                t_g = []
                for c in range(HID // 128):
                    for half, (lo, n) in enumerate(SPLIT):
                        b = (2 * c + half) % 4
                        wait(pe, t_g[-4] if len(t_g) >= 4 else a0)
                        for k in range(2):
                            m = pe.matmul(ps[:, b, 0:n], w1_s[:, k, c * 128:(c + 1) * 128],
                                          xn_t[:, k, bass.ds(i * (U5 * NP) + lo, n)], start=(k == 0), stop=(k == 1))
                        wait(act, M.mark(m))
                        t_g.append(A.mark(act.activation(hid[:, c, lo:lo + n], ps[:, b, 0:n], ACT.Gelu_apprx_tanh,
                                                         bias=b1_s[:, c:c + 1])))
                t_y = []
                for u in range(U5):
                    b = 4 + u % 2
                    wait(pe, t_y[u - 2] if u >= 2 else a0)
                    for c in range(HID // 128):
                        if u == 0:
                            wait(pe, t_g[2 * c])
                        elif c == HID // 128 - 1:
                            wait(pe, t_g[-1])
                        m = pe.matmul(ps[0:NP, b, 0:D], hid[:, c, u * NP:(u + 1) * NP], w2_s[:, c, :],
                                      start=(c == 0), stop=(c == HID // 128 - 1))
                    wait(act, M.mark(m))
                    t_y.append(A.mark(act.copy(acc_cols(i * U5 + u, 0, D), ps[0:NP, b, 0:D])))
            wait(vec, t_all, t_col)
            for t in range(NT):
                lo, hi = t * NP, (t + 1) * NP
                w = w_col[:, t:t + 1]
                if t:
                    V.mark(vec.tensor_scalar(junk[:, 0:lo], w_all[0:NP, 0:lo], w, None, ALU.is_ge, ALU.add, accum_out=above[:, t, 0:1]))
                else:
                    V.mark(vec.memset(above[:, 0, 0:1], 0.0))
                V.mark(vec.tensor_scalar(junk[:, lo:], w_all[0:NP, lo:], w, None, ALU.is_gt, ALU.add, accum_out=above[:, t, 1:2]))
                wait(vec, V.now())
                V.mark(vec.scalar_tensor_tensor(same[:, :], w_all[0:NP, lo:hi], w, lower[0:NP, 0:NP], ALU.is_equal, ALU.mult,
                                                accum_out=above[:, t, 2:3]))
                wait(vec, V.now())
            V.mark(vec.tensor_reduce(gate[:, :], above[:, :, :], AX, ALU.add))
            wait(vec, V.now())
            V.mark(vec.scalar_tensor_tensor(gate[:, :], gate[:, :], TOPK - 0.5, w_col[:, :], ALU.is_lt, ALU.mult))
            wait(vec, V.now(), x_added.now())
            with loop(nc, NODE_STEPS, {V: U5}) as i:
                for u in range(U5):
                    t = i * U5 + u
                    V.mark(vec.scalar_tensor_tensor(flat(xa, t), b2_s[:, :], col(gate, t), flat(xa, t), ALU.mult, ALU.add))
            wait(vec, V.now())
            with loop(nc, NODE_STEPS, {V: 2 * U5}) as i:
                wait(vec, (A.sem, ffn_start + (i + 1) * (16 + U5)))
                t_x = [V.mark(vec.scalar_tensor_tensor(flat(xa, i * U5 + u), acc_cols(i * U5 + u, 0, D), col(gate, i * U5 + u),
                                                       flat(xa, i * U5 + u), ALU.mult, ALU.add)) for u in range(U5)]
                for u in range(U5):
                    wait(vec, t_x[u])
                    V.mark(vec.bn_stats(flat(stats, i * U5 + u), flat(xa, i * U5 + u)))
            everyone(turned_x, xt_in, x_added, dotted)

        with tab_ctx:
            def sbt(name, shape, dt=F32):
                return sb(name, shape, dt, tab_ctx)

            ybuf = sbt("ybuf", [NP, U5, REL, D])
            t_acc = P.mark(pool.memset(acc[:, :], 0.0))
            t_one = P.mark(pool.memset(gath[:, :, D:AW], 1.0))
            t_norm = norm_factors()
            for e in (vec, act, pe):
                wait(e, t_norm, t_rel)
            y_rows = y_tab.rearrange("(r n) d -> n r d", r=REL)
            s_y = [sem(f"y_stored_{u}") for u in range(U5)]
            y_made, y_out = Lane(nc, pe, sem("y_rows_made")), Lane(nc, act, sem("y_rows_copied"))
            with loop(nc, NODE_STEPS, {V: U5, S: 2, **{lane: U5 for lane in (turned_x, xt_in, y_made, y_out)}}) as i:
                s_now, y0 = [S.last(1), S.last(2)], y_out.now()
                norm, turn = norm_steps(i, t_used=lambda u: y_made.last(u + 1))
                t_xt, t_y = [], []
                for step in range(U5 + 2):
                    if step < U5:
                        norm(step)
                    if 0 < step <= U5:
                        t_xt.append(turn(step - 1))
                    u = step - 2
                    if u >= 0:
                        b = 2 + 2 * (u % 2)
                        wait(pe, t_xt[u], t_y[u - 2] if u >= 2 else y0)
                        for half in range(2):
                            for k in range(2):
                                m = pe.matmul(ps[0:NP, b + half, :], xt[:, u, k, :], rel_s[:, k, 2 * half:2 * half + 2, :].rearrange("p r d -> p (r d)"),
                                              start=(k == 0), stop=(k == 1))
                        wait(act, y_made.mark(m), s_now[u >= 2])
                        t_y.append(y_out.mark(act.copy(ybuf[:, u, :, :].rearrange("p (a r) d -> p a (r d)", a=2), ps[0:NP, b:b + 2, :])))
                        wait(sp, t_y[-1])
                        sp.dma_start(y_rows[bass.ds((i * U5 + u) * NP, NP), :, :], ybuf[:, u, :, :]).then_inc(s_y[u], 16)
                        if u == 2:
                            stored(s_y[:2], i)
                stored(s_y[2:], i)
            everyone(turned_x, xt_in, y_made, y_out)

        w1b = sb("w1b", [128, EXP, W1B])
        mw2_s = sb("mw2_s", [128, EXP * 2 * D])
        r_s = sb("r_s", [EXP, D])
        t_r = d_in[13].mark(sp.dma_start(r_s[:, :], router))
        for e in range(EXP):
            d_in[11].mark(sp.dma_start(w1b[:, e, 0:2 * D].rearrange("p (k n) -> p k n", k=2), matrix(mw1[e])))
            t_m1 = row_bcast(w1b[:, e, 2 * D:3 * D], mb2[e], d_in[11], 128)
            t_m2 = d_in[12].mark(sp.dma_start(mw2_s[:, e * 2 * D:(e + 1) * 2 * D].rearrange("p (k n) -> p k n", k=2), matrix(mw2[e])))
        for k in range(2):
            t_m1 = d_in[11].mark(sp.dma_start(w1b[:, :, 3 * D + k:3 * D + k + 1], mb1[:, k * 128:(k + 1) * 128].rearrange("e (p o) -> p e o", o=1),
                                              allow_slow_non_contiguous=True))

        self_made, self_out = Lane(nc, pe, sem("self_rows_made")), Lane(nc, vec, sem("self_rows_copied"))

        def relation_body(i, with_self):
            used = [summed.last(4), summed.last(8)]
            for g in range(GRPS):
                gather(i, g, y_tab, D, slots["b"][1], [used[g], used[g]])
            t_hot = [one_hots(i, g, slots["b"][0], used[g]) for g in range(GRPS)]
            v_off = pair_offsets(ENG.DVE, slots["b"][2], i * (RING // 2) + LEAD, (NT - 1) * AW)
            if with_self:
                wait(vec, turned_x.now())
                t_n = V.mark(vec.tensor_scalar(xs[:, 0, :], flat(xa, i), col(rstd, i), col(nmr, i), ALU.mult, ALU.add))
                wait(pe, t_n, xt_in.now())
                for k in range(2):
                    m = pe.transpose(ps[:, 0, k * NP:(k + 1) * NP], xs[:, 0, k * 128:(k + 1) * 128], ident[0:NP, 0:NP])
                wait(act, turned_x.mark(m), self_made.now())
                t_xt = xt_in.mark(act.copy(xt[:, 0, :, :], ps[:, 0, 0:2 * NP].rearrange("p (k n) -> p k n", k=2)))
            t_add = [added.last(7), added.last(8)]
            for g in range(GRPS):
                wait(pe, t_hot[g])
                for q in range(g * GRP // 2, (g + 1) * GRP // 2):
                    gathered(pe, i + EDGE_STEPS + g, 2 * q, 2 * q + 2)
                    t = sum_pair(q, D + 1, t_add[q % 2])
                    t_add[q % 2] = add_pair(q, v_off[q], D + 1, t)
                if with_self and g == 0:
                    wait(pe, t_xt, self_out.now())
                    for k in range(2):
                        m = pe.matmul(ps[0:NP, 1, 0:D], xt[:, 0, k, :], self_s[:, k, :], start=(k == 0), stop=(k == 1))
                    wait(vec, self_made.mark(m))
                    self_out.mark(vec.tensor_tensor(flat(xb, i), ps[0:NP, 1, 0:D], sb_s[:, :], ALU.add))

        BODY = {V: GRPS, added: 8, P: GRPS, passed: 2 * GRPS, summed: 8}
        for e in (vec, pe, act):
            wait(e, t_norm, t_rel, t_sb)
        with loop(nc, NT, {**BODY, V: GRPS + 1, turned_x: 1, xt_in: 1, self_made: 1, self_out: 1}) as i:
            relation_body(i, True)
        with loop(nc, EDGE_STEPS - NT, BODY) as i:
            relation_body(i + NT, False)
        everyone(added, self_out, self_made, xt_in)

        with ExitStack() as moe_ctx:
            def sbm(name, shape, dt=F32):
                return sb(name, shape, dt, moe_ctx)

            r_t = sbm("r_t", [128, 2, EXP])
            logit, prob, comb, sel, place = (sbm(n, [NP, NT, EXP]) for n in ("logit", "prob", "comb", "sel", "place"))
            top, order = sbm("top", [NP, NT, EXP]), sbm("order", [NP, NT, EXP])
            s1, s2 = (sbm(n, [NP, NT]) for n in ("s1", "s2"))
            tile_id, row_id = sbm("tile_id", [NP, 2, NT]), sbm("row_id", [NP, 1])
            KTH = 32
            node_f, kth, empty, dump, dest_f = (sbm(n, [128, MOE_TILES]) for n in ("node_f", "kth", "empty", "dump", "dest_f"))
            dest_i = sbm("dest_i", [128, MOE_TILES], I32)
            at_out = sbm("at_out", [128, MOE_BODY], I32)
            cnt_e, offs_e = (sbm(n, [NP, EXP]) for n in ("cnt_e", "offs_e"))
            tot_e = sbm("tot_e", [EXP, 3])
            starts_e = sbm("starts_e", [EXP, EXP])
            reach_e = sbm("reach_e", [EXP, MOE_TILES])
            tile_e = sbm("tile_e", [1, MOE_TILES])
            at_w1, at_w2 = (sbm(n, [1, MOE_STEPS, MOE_ROW], I32) for n in ("at_w1", "at_w2"))
            slot, slot_row, slot_col, coef = (sbm(n, [NP, 2, NT]) for n in ("slot", "slot_row", "slot_col", "coef"))
            node_i = sbm("node_i", [128, MOE_TILES + MOE_BODY // 2], I32)
            free = hot[:, :, :].rearrange("p s n -> p (s n)")
            x_t, hid = (free[:, j * 512:(j + 1) * 512].rearrange("p (b k n) -> p b k n", b=2, k=2) for j in range(2))
            w1_now = sbm("w1_now", [128, 2, 2, D])
            y_buf = sbm("y_buf", [128, MOE_BODY, D])
            P.mark(pool.iota(order[:, :, :], [[0, NT], [-1, EXP]], base=EXP, channel_multiplier=0, allow_small_or_imprecise_dtypes=True))
            P.mark(pool.iota(tile_id[:, :, :], [[KTH, 2], [1, NT]], base=0, channel_multiplier=0, allow_small_or_imprecise_dtypes=True))
            P.mark(pool.iota(dump[:, :], [[128, MOE_TILES]], base=2 * N + 2, channel_multiplier=1, allow_small_or_imprecise_dtypes=True))
            P.mark(pool.memset(node_i[:, MOE_TILES:], 0))
            t_iota = P.mark(pool.iota(row_id[:, :], [[1, 1]], base=1, channel_multiplier=1, allow_small_or_imprecise_dtypes=True))
            wait(pe, t_r, V.now(), A.now())
            for k in range(2):
                m = pe.transpose(ps[:, 0, k * EXP:(k + 1) * EXP], r_s[:, k * 128:(k + 1) * 128], ident[0:EXP, 0:EXP])
            wait(act, M.mark(m), V.now())
            t_rt = A.mark(act.copy(r_t[:, :, :], ps[:, 0, 0:2 * EXP].rearrange("p (k e) -> p k e", k=2)))

            V.mark(vec.tensor_scalar(s1[:, :], acc3[:, :, D], 1.0, None, ALU.max))
            wait(vec, V.now())
            V.mark(vec.reciprocal(s2[:, :], s1[:, :]))
            wait(vec, V.now())
            def third_sum(t):
                wait(act, V.mark(vec.scalar_tensor_tensor(flat(xb, t), acc_cols(t, 0, D), col(s2, t), flat(xb, t), ALU.mult, ALU.add)))
                wait(pool, A.mark(act.activation(flat(xb, t), flat(xb, t), ACT.Relu)))
                return P.mark(pool.tensor_tensor(flat(xa, t), flat(xa, t), flat(xb, t), ALU.add))

            def third_stats(t, t_sum):
                wait(vec, t_sum)
                V.mark(vec.bn_stats(flat(stats, t), flat(xa, t)))

            for u in range(U5):
                third_sum(u)
            with loop(nc, NODE_STEPS - 1, {V: 2 * U5, A: U5, P: U5}) as i:
                t_before = [(P.sem, P.base + u + 1 - U5) for u in range(U5)]
                for u in range(U5):
                    third_sum((i + 1) * U5 + u)
                    third_stats(i * U5 + u, t_before[u])
            for u in range(U5):
                third_stats((NODE_STEPS - 1) * U5 + u, (P.sem, P.base + P.n + u + 1 - U5))
            t_norm = norm_factors()
            wait(vec, t_iota)
            for e in (vec, act, pool, pe):
                wait(e, t_norm, t_rt)
            s_xn = [sem(f"xn_stored_{u}") for u in range(U5)]
            routed = Lane(nc, pe, sem("logits_made"))
            wait(sp, V.now())
            for u in range(U5):
                sp.dma_start(y_nodes[u:u + 1, 0:16], xs[0:1, u, 0:16]).then_inc(s_xn[u], 16)
            with loop(nc, NODE_STEPS, {V: U5, A: U5, **{lane: U5 for lane in (turned_x, xt_in, x_added, routed)}}) as i:
                a0 = A.now()
                norm, turn = norm_steps(i, add_back=True, t_stored=lambda u: (s_xn[u], i * 16 + 16), t_used=lambda u: routed.last(u + 1))
                t_xt, t_l = [], []
                for step in range(U5 + 2):
                    if step < U5:
                        wait(sp, norm(step))
                        sp.dma_start(xn_tab[bass.ds((i * U5 + step) * NP, NP), :], xs[:, step, :]).then_inc(s_xn[step], 16)
                    if 0 < step <= U5:
                        t_xt.append(turn(step - 1))
                    u = step - 2
                    if u >= 0:
                        wait(pe, t_xt[u], t_l[u - 2] if u >= 2 else a0)
                        for k in range(2):
                            m = pe.matmul(ps[0:NP, 2 + u % 2, 0:EXP], xt[:, u, k, :], r_t[:, k, :], start=(k == 0), stop=(k == 1))
                        wait(act, routed.mark(m))
                        t_l.append(A.mark(act.copy(flat(logit, i * U5 + u), ps[0:NP, 2 + u % 2, 0:EXP])))
            own = lambda: wait(vec, V.now())
            b8 = lambda tile: tile[:, :].unsqueeze(2).to_broadcast([NP, NT, EXP])
            wait(vec, A.now())
            V.mark(vec.tensor_reduce(s1[:, :], logit[:, :, :], AX, ALU.max))
            own()
            wait(act, V.mark(vec.tensor_tensor(logit[:, :, :], logit[:, :, :], b8(s1), ALU.subtract)))
            wait(vec, A.mark(act.activation(prob[:, :, :], logit[:, :, :], ACT.Exp)))
            V.mark(vec.tensor_reduce(s1[:, :], prob[:, :, :], AX, ALU.add))
            own()
            V.mark(vec.reciprocal(s2[:, :], s1[:, :]))
            own()
            V.mark(vec.tensor_tensor(prob[:, :, :], prob[:, :, :], b8(s2), ALU.mult))
            own()
            left = prob
            for k in range(2):
                V.mark(vec.tensor_reduce(s1[:, :], left[:, :, :], AX, ALU.max))
                own()
                V.mark(vec.tensor_tensor(top[:, :, :], left[:, :, :], b8(s1), ALU.is_equal))
                own()
                V.mark(vec.tensor_tensor(top[:, :, :], top[:, :, :], order[:, :, :], ALU.mult))
                own()
                V.mark(vec.tensor_reduce(s1[:, :], top[:, :, :], AX, ALU.max))
                own()
                V.mark(vec.tensor_tensor(top[:, :, :], top[:, :, :], b8(s1), ALU.is_equal))
                own()
                if k == 0:
                    V.mark(vec.scalar_tensor_tensor(comb[:, :, :], top[:, :, :], -2.0, prob[:, :, :], ALU.mult, ALU.add))
                    V.mark(vec.tensor_copy(sel[:, :, :], top[:, :, :]))
                    left = comb
                else:
                    V.mark(vec.tensor_tensor(sel[:, :, :], sel[:, :, :], top[:, :, :], ALU.add))
                own()
            t_cnt = V.mark(vec.tensor_reduce(cnt_e[:, :], sel[:, :, :].rearrange("p t e -> p e t"), AX, ALU.add))

            wait(pe, t_cnt)
            wait(vec, M.mark(pe.matmul(ps[0:EXP, 4, 0:1], cnt_e[:, :], ones[0:NP, 0:1], start=True, stop=True)))
            V.mark(vec.tensor_scalar(tot_e[:, 0:1], ps[0:EXP, 4, 0:1], 1.0 / 128, 127 / 2 / 128, ALU.mult, ALU.add))
            own()
            V.mark(vec.tensor_scalar(tot_e[:, 1:2], tot_e[:, 0:1], BIG, BIG, ALU.add, ALU.subtract))
            own()
            t_starts = V.mark(vec.tensor_scalar(starts_e[:, :], before[0:EXP, 0:EXP], tot_e[:, 1:2], 128.0, ALU.mult, ALU.mult))
            wait(pe, t_starts)
            t_cum = M.mark(pe.matmul(ps[0:EXP, 4, 8:9], upto[0:EXP, 0:EXP], tot_e[:, 1:2], start=True, stop=True))
            pe.matmul(ps[0:NP, 7, 0:EXP], before[0:NP, 0:NP], cnt_e[:, :], start=True, stop=False)
            t_offs = M.mark(pe.matmul(ps[0:NP, 7, 0:EXP], ones[0:EXP, 0:NP], starts_e[:, :], start=False, stop=True))
            V.mark(vec.tensor_tensor(comb[:, :, :], sel[:, :, :], prob[:, :, :], ALU.mult))
            own()
            V.mark(vec.tensor_reduce(s1[:, :], comb[:, :, :], AX, ALU.add))
            own()
            V.mark(vec.tensor_scalar(s1[:, :], s1[:, :], 1e-12, None, ALU.max))
            own()
            V.mark(vec.reciprocal(s2[:, :], s1[:, :]))
            own()
            V.mark(vec.tensor_tensor(comb[:, :, :], comb[:, :, :], b8(s2), ALU.mult))
            wait(vec, t_cum)
            V.mark(vec.tensor_copy(tot_e[:, 2:3], ps[0:EXP, 4, 8:9]))
            own()
            t_reach = V.mark(vec.tensor_scalar(reach_e[:, :], iota_c[0:EXP, 0:MOE_TILES], tot_e[:, 2:3], None, ALU.is_ge))
            wait(pe, t_reach)
            t_tile = M.mark(pe.matmul(ps[0:1, 4, 0:MOE_TILES], ones[0:EXP, 0:1], reach_e[:, :], start=True, stop=True))
            wait(vec, t_offs)
            V.mark(vec.tensor_scalar(offs_e[:, :], ps[0:NP, 7, 0:EXP], -1.0, None, ALU.add))
            own()
            for e in range(EXP):
                V.mark(vec.tensor_tensor_scan(place[:, :, e], sel[:, :, e], zeros_e[0:NP, 0:NT], offs_e[:, e:e + 1], ALU.add, ALU.add))
            wait(vec, t_tile)
            V.mark(vec.tensor_scalar(tile_e[:, :], ps[0:1, 4, 0:MOE_TILES], float(EXP - 1), None, ALU.min))
            own()
            by_body = tile_e[:, :].rearrange("o (s b) -> o s b", b=MOE_BODY)
            V.mark(vec.tensor_scalar(at_w1[:, :, 0:MOE_BODY], by_body, float(W1B), None, ALU.mult))
            V.mark(vec.tensor_scalar(at_w2[:, :, 0:MOE_BODY], by_body, 2.0 * D, None, ALU.mult))
            V.mark(vec.tensor_tensor(place[:, :, :], place[:, :, :], sel[:, :, :], ALU.mult))
            own()
            V.mark(vec.tensor_reduce(slot[:, 1, :], place[:, :, :], AX, ALU.max))
            V.mark(vec.tensor_reduce(s1[:, :], place[:, :, :], AX, ALU.add))
            own()
            V.mark(vec.tensor_tensor(slot[:, 0, :], s1[:, :], slot[:, 1, :], ALU.subtract))
            own()
            V.mark(vec.tensor_scalar(slot_row[:, :, :], slot[:, :, :], 1.0 / 128, -63.5 / 128, ALU.mult, ALU.add))
            own()
            V.mark(vec.tensor_scalar(slot_col[:, :, :], slot_row[:, :, :], BIG, BIG, ALU.add, ALU.subtract))
            own()
            V.mark(vec.scalar_tensor_tensor(slot_row[:, :, :], slot_col[:, :, :], -128.0, slot[:, :, :], ALU.mult, ALU.add))
            own()
            hot_r = acc[:, 0:NT * 128].bitcast(F16).rearrange("p (j r) -> p j r", r=128)
            hot_c = wide[0:NP, 0:2 * NT * MOE_TILES].bitcast(F16).rearrange("p (k t v c) -> p k t v c", k=2, v=2, c=MOE_TILES)
            spread = lambda v, n: v.unsqueeze(len(v.shape)).to_broadcast([*v.shape, n])
            t_row, t_tile = [], []
            for k in range(2):
                wait(pool, V.mark(vec.tensor_tensor(hot_c[:, k, :, 0, :], iota_r[0:NP, 0:MOE_TILES].unsqueeze(1).to_broadcast([NP, NT, MOE_TILES]),
                                                    spread(slot_col[:, k, :], MOE_TILES), ALU.is_equal)))
                t_tile.append(P.mark(pool.tensor_tensor(hot_c[:, k, :, 1, :], hot_c[:, k, :, 0, :], spread(tile_id[:, k, :], MOE_TILES), ALU.mult)))
                wait(act, t_tile[k])
                t_row.append(A.mark(act.mul(hot_c[:, k, :, 0, :], hot_c[:, k, :, 0, :], row_id[:, 0:1])))
            for k in range(2):
                t_hot = V.mark(vec.tensor_tensor(hot_r[:, k * NT:(k + 1) * NT, :], iota_r[0:NP, :].unsqueeze(1).to_broadcast([NP, NT, 128]),
                                                 spread(slot_row[:, k, :], 128), ALU.is_equal))
                wait(pe, t_hot, t_row[k])
                for t in range(NT):
                    m = pe.matmul(ps[:, 6, 0:2 * MOE_TILES], hot_r[:, k * NT + t, :], hot_c[:, k, t, :, :].rearrange("p v c -> p (v c)"),
                                  start=(k == 0 and t == 0), stop=(k == 1 and t == NT - 1))
            t_nodes = M.mark(m)
            V.mark(vec.tensor_tensor(sel[:, :, :], place[:, :, :], b8(slot[:, 1, :]), ALU.is_equal))
            own()
            V.mark(vec.tensor_tensor(sel[:, :, :], sel[:, :, :], comb[:, :, :], ALU.mult))
            own()
            V.mark(vec.tensor_reduce(coef[:, 1, :], sel[:, :, :], AX, ALU.add))
            V.mark(vec.tensor_tensor(comb[:, :, :], comb[:, :, :], sel[:, :, :], ALU.subtract))
            own()
            V.mark(vec.tensor_reduce(coef[:, 0, :], comb[:, :, :], AX, ALU.add))
            wait(vec, t_nodes)
            V.mark(vec.tensor_scalar(kth[:, :], ps[:, 6, MOE_TILES:2 * MOE_TILES], float(KTH), None, ALU.is_ge))
            own()
            V.mark(vec.scalar_tensor_tensor(node_f[:, :], kth[:, :], -float(KTH), ps[:, 6, MOE_TILES:2 * MOE_TILES], ALU.mult, ALU.add))
            own()
            V.mark(vec.scalar_tensor_tensor(node_f[:, :], node_f[:, :], float(NP), ps[:, 6, 0:MOE_TILES], ALU.mult, ALU.add))
            own()
            V.mark(vec.tensor_scalar(empty[:, :], node_f[:, :], 0.0, None, ALU.is_equal))
            V.mark(vec.tensor_scalar(node_i[:, 0:MOE_TILES], node_f[:, :], -1.0, 0.0, ALU.add, ALU.max))
            V.mark(vec.scalar_tensor_tensor(dest_f[:, :], node_f[:, :], 2.0, kth[:, :], ALU.mult, ALU.add))
            own()
            V.mark(vec.tensor_tensor(empty[:, :], empty[:, :], dump[:, :], ALU.mult))
            own()
            t_plan = V.mark(vec.scalar_tensor_tensor(dest_i[:, :], dest_f[:, :], -2.0, empty[:, :], ALU.add, ALU.add))

            turned, first_done, second_done = (Lane(nc, pe, sem(n)) for n in ("rows_turned", "first_products", "second_products"))
            hidden = Lane(nc, act, sem("gelu_done"))
            rows_in, staged, y_done = (Lane(nc, vec, sem(n)) for n in ("rows_copied", "weights_staged", "y_done"))
            s_y = [sem(f"y_slot_stored_{u}") for u in range(MOE_BODY)]
            w1_flat = w1b[:, :, :].rearrange("p e n -> p (e n)")
            HALF = MOE_BODY // 2
            GATHERS = 2 * EDGE_STEPS
            wait(pool, x_added.now(), *((sem_u, 16 * NODE_STEPS + 16) for sem_u in s_xn))
            for e in (vec, act, pool, pe):
                wait(e, t_plan, t_m1, t_m2, V.now(), A.now(), P.now(), M.now())

            def load_offsets(engine, table, i, top):
                return nc.values_load_multi_w_load_instructions(
                    table[:, :, :].rearrange("o s b -> o (s b)")[0:1, bass.ds(i * MOE_ROW, MOE_BODY)], engines=[engine], min_val=0, max_val=top,
                    skip_runtime_bounds_check_because="the expert is the minimum of a count and EXP - 1")[1]

            def stage_half(h, at, t_used):
                wait(pool, t_used)
                wait_apart(passed, P.mark(pool.tensor_copy(at_rows[:, h, 0:HALF], node_i[:, bass.ds(at, HALF)])))

            def gather_x(u):
                pool.indirect_dma_start(gath[:, u, 0:D], None, xn_tab,
                                        bass.IndirectOffsetOnAxis(ap=at_rows[:, u // HALF, u % HALF:u % HALF + 1], axis=0)
                                        ).then_inc(s_gath[u], 16)

            stage_half(0, 0, turned.now())
            for u in range(HALF):
                gather_x(u)
            with loop(nc, MOE_STEPS, {P: 3, passed: 3 + HALF - 1 + MOE_BODY, S: 2, **{lane: MOE_BODY for lane in (
                    turned, first_done, second_done, rows_in, hidden, staged, y_done)}}) as i:
                s_now = [S.last(1), S.last(2)]
                stage_half(1, i * MOE_BODY + HALF, turned.last(MOE_BODY))
                for u in range(HALF, MOE_BODY):
                    if u % HALF:
                        wait_apart(passed, turned.last(u + 1))
                    gather_x(u)
                wait(pool, S.now())
                wait_apart(passed, P.mark(pool.tensor_copy(at_out[:, :], dest_i[:, bass.ds(i * MOE_BODY, MOE_BODY)])))
                v_at = load_offsets(ENG.DVE, at_w1, i, (EXP - 1) * W1B)
                a_at = load_offsets(ENG.Activation, at_w1, i, (EXP - 1) * W1B)
                p_at = load_offsets(ENG.PE, at_w2, i, (EXP - 1) * 2 * D)
                ticks = {lane: [] for lane in (turned, first_done, second_done, rows_in, hidden, staged, y_done)}

                def mark(lane, ins):
                    ticks[lane].append(lane.mark(ins))

                def two_before(lane, u):
                    return ticks[lane][u - 2] if u >= 2 else lane.last(MOE_BODY + u - 1)

                for step in range(MOE_BODY + 2):
                    u = step
                    if u < MOE_BODY:
                        gathered(pe, i + GATHERS + (u >= GRP), u, u + 1)
                        wait(pe, two_before(rows_in, u))
                        for k in range(2):
                            m = pe.transpose(ps[:, u % 2, k * 128:(k + 1) * 128], gath[:, u, k * 128:(k + 1) * 128], ident[:, :])
                        mark(turned, m)
                        wait(vec, two_before(first_done, u))
                        mark(staged, vec.tensor_copy(w1_now[:, u % 2, :, :].rearrange("p k n -> p (k n)"), w1_flat[:, bass.ds(v_at[u], 2 * D)]))
                        wait(vec, ticks[turned][u])
                        mark(rows_in, vec.tensor_copy(x_t[:, u % 2, :, :].rearrange("p k n -> p (k n)"), ps[:, u % 2, 0:256]))
                    u = step - 1
                    if 0 <= u < MOE_BODY:
                        wait(pe, ticks[rows_in][u], ticks[staged][u], two_before(hidden, u))
                        for c in range(2):
                            for k in range(2):
                                m = pe.matmul(ps[:, 2 + u % 2, c * 128:(c + 1) * 128], w1_now[:, u % 2, k, c * 128:(c + 1) * 128],
                                              x_t[:, u % 2, k, :], start=(k == 0), stop=(k == 1))
                        mark(first_done, m)
                        wait(act, ticks[first_done][u], two_before(second_done, u))
                        for c in range(2):
                            t = act.activation(hid[:, u % 2, c, :], ps[:, 2 + u % 2, c * 128:(c + 1) * 128], ACT.Gelu,
                                               bias=w1_flat[:, bass.ds(a_at[u] + 3 * D + c, 1)])
                        mark(hidden, t)
                    u = step - 2
                    if u >= 0:
                        wait(pe, ticks[hidden][u], two_before(y_done, u))
                        for c in range(2):
                            m = pe.matmul(ps[:, 4 + u % 2, 0:D], hid[:, u % 2, c, :], mw2_s[:, bass.ds(p_at[u] + c * D, D)],
                                          start=(c == 0), stop=(c == 1))
                        mark(second_done, m)
                        wait(vec, ticks[second_done][u], s_now[u // HALF])
                        mark(y_done, vec.tensor_tensor(y_buf[:, u, :], ps[:, 4 + u % 2, 0:D], w1_flat[:, bass.ds(v_at[u] + 2 * D, D)], ALU.add))
                        wait_apart(passed, ticks[y_done][u])
                        pool.indirect_dma_start(y_nodes, bass.IndirectOffsetOnAxis(ap=at_out[:, u:u + 1], axis=0),
                                                y_buf[:, u, :], None).then_inc(s_y[u], 16)
                        if u == HALF - 3:
                            stage_half(0, (i + 1) * MOE_BODY, ticks[turned][HALF - 1])
                        if HALF - 3 <= u < MOE_BODY - 3:
                            gather_x(u - (HALF - 3))
                        if u == HALF:
                            stored(s_y[0:HALF], i)
                stored(s_y[HALF:], i)

            out_rows = out.rearrange("(t p) d -> p t d", p=NP)
            y_rows = y_nodes[0:2 * N, :].rearrange("(t p k) d -> p t k d", p=NP, k=2)
            s_out = sem("out_stored")
            s_in = [sem(f"y_loaded_{u}") for u in range(U5)]
            combined = Lane(nc, vec, sem("combined"))
            gathered(sp, GATHERS + MOE_STEPS, 0, HALF)
            for e in (sp, vec):
                wait(e, S.now(), turned.now(), x_added.now())
            with loop(nc, NODE_STEPS, {combined: 2 * U5}) as i:
                for u in range(U5):
                    wait(sp, combined.last(min(2 * u + 3, 2 * U5)))
                    sp.dma_start(gath[0:NP, 2 * u:2 * u + 2, 0:D], y_rows[:, bass.ds(i * U5 + u, 1), :, :].rearrange("p a k d -> p (a k) d")
                                 ).then_inc(s_in[u], 16)
                t_first = {}
                for step in range(U5 + 1):
                    for u, k in ((step, 0), (step - 1, 1)):
                        if not 0 <= u < U5:
                            continue
                        if k == 0:
                            vec.wait_ge(s_in[u], i * 16 + 16)
                        else:
                            wait(vec, t_first[u])
                        t = combined.mark(vec.scalar_tensor_tensor(flat(xa, i * U5 + u), gath[0:NP, 2 * u + k, 0:D], coef[:, k, bass.ds(i * U5 + u, 1)],
                                                                   flat(xa, i * U5 + u), ALU.mult, ALU.add))
                        t_first[u] = t
                wait(act, t)
                act.dma_start(out_rows[:, bass.ds(i * U5, U5), :], xa[:, bass.ds(i * U5, U5), :]).then_inc(s_out, 16)
            sp.wait_ge(s_out, 16 * NODE_STEPS)
            everyone(combined)


_INS = ["x", "src", "dst", "edge_type_4", "L0_gnn_W", "L0_gnn_a_l", "L0_gnn_a_r", "L0_ffn_wr", "L0_ffn_br",
        "L0_ffn_w1", "L0_ffn_b1", "L0_ffn_w2", "L0_ffn_b2", "L1_gnn_self_W", "L1_gnn_self_b", "L1_gnn_rel_W",
        "L1_ffn_router_w", "L1_ffn_w1", "L1_ffn_b1", "L1_ffn_w2", "L1_ffn_b2"]


def kernel(**inputs):
    import numpy as _np
    import concourse.bacc as _bacc
    from concourse import mybir as _mybir
    from concourse.bass_utils import run_bass_kernel_spmd as _run

    nc = _bacc.Bacc("TRN2", target_bir_lowering=False, num_devices=1)
    arrays, args = {}, []
    for name in _INS:
        a = _np.ascontiguousarray(inputs[name])
        arrays[f"in_{name}"] = a
        args.append(nc.dram_tensor(f"in_{name}", a.shape, _mybir.dt.from_np(a.dtype), kind="ExternalInput").ap())
    args.append(nc.dram_tensor("out_0", (N, D), F32, kind="ExternalOutput").ap())
    build(nc, *args)
    r = _run(nc, [arrays], core_ids=[0])
    return r.results[0]["out_0"]
```
